# Optimizing a Trainium2 kernel written in Bass

```python
import numpy as np
import jax
import jax.numpy as jnp

def _softmax(x, axis=-1):
    return jax.nn.softmax(x, axis=axis)

def _gelu(x):
    return jax.nn.gelu(x, approximate=True)

def _silu(x):
    return jax.nn.silu(x)

def _sigmoid(x):
    return jax.nn.sigmoid(x)

def _layernorm(x, axis=-1, eps=1e-05):
    m = jnp.mean(x, axis=axis, keepdims=True)
    v = jnp.var(x, axis=axis, keepdims=True)
    return (x - m) / jnp.sqrt(v + eps)

def _scatter_add(tgt, idx, src, axis=0):
    return tgt.at[idx].add(src)

def _segment_sum(src, seg, n):
    return jax.ops.segment_sum(src, seg, n)
kernel_name = 'mk_seq_preln_d2_jaxref_r8_98706d'

def setup_inputs(seed: int=0):
    np.random.seed(seed)
    _w = jnp.asarray

    def _L0_attn_setup():
        import jax, jax.numpy as jnp
        import numpy as np
        EMBED_DIM = 128
        NUM_HEADS = 16
        EFF_HEADS = NUM_HEADS // 2
        HEAD_DIM = EMBED_DIM // NUM_HEADS
        LAMBDA_INIT = 0.8
        B, N = (2, 256)
        key = jax.random.key(seed)
        ks = jax.random.split(key, 14)
        s = 0.02
        return {'x': jax.random.normal(ks[0], (B, N, EMBED_DIM), dtype=jnp.float32), 'Wq': jax.random.normal(ks[1], (EMBED_DIM, EMBED_DIM), dtype=jnp.float32) * s, 'bq': jnp.zeros((EMBED_DIM,), dtype=jnp.float32), 'Wk': jax.random.normal(ks[2], (EMBED_DIM, EMBED_DIM), dtype=jnp.float32) * s, 'bk': jnp.zeros((EMBED_DIM,), dtype=jnp.float32), 'Wv': jax.random.normal(ks[3], (EMBED_DIM, EMBED_DIM), dtype=jnp.float32) * s, 'bv': jnp.zeros((EMBED_DIM,), dtype=jnp.float32), 'Wp': jax.random.normal(ks[4], (EMBED_DIM, EMBED_DIM), dtype=jnp.float32) * s, 'bp': jnp.zeros((EMBED_DIM,), dtype=jnp.float32), 'lambda_q1': jax.random.normal(ks[5], (EFF_HEADS, 1, HEAD_DIM), dtype=jnp.float32) * s, 'lambda_k1': jax.random.normal(ks[6], (EFF_HEADS, 1, HEAD_DIM), dtype=jnp.float32) * s, 'lambda_q2': jax.random.normal(ks[7], (EFF_HEADS, 1, HEAD_DIM), dtype=jnp.float32) * s, 'lambda_k2': jax.random.normal(ks[8], (EFF_HEADS, 1, HEAD_DIM), dtype=jnp.float32) * s}
    _L0_attn_in = _L0_attn_setup()

    def _L0_ffn_setup():
        import jax, jax.numpy as jnp
        import numpy as np
        import math
        DMODEL = 128
        DFF = 512
        NUM_EXPERTS = 8
        TOPK = 2
        CAP_FACTOR = 1.25
        EPS = 1.1920929e-07

        def _trunc_normal(key, shape, fan_in, scale=1.0):
            std = scale * (1.0 / fan_in) ** 0.5
            return jax.random.truncated_normal(key, -2.0, 2.0, shape, jnp.float32) * std
        key = jax.random.key(seed)
        ks = jax.random.split(key, 5)
        return {'x': jax.random.normal(ks[0], (2, 256, DMODEL), jnp.float32), 'router_weight': _trunc_normal(ks[1], (NUM_EXPERTS, DMODEL), DMODEL), 'ff_pre_act_weight': _trunc_normal(ks[2], (NUM_EXPERTS, DFF, DMODEL), DMODEL), 'gate_weight': _trunc_normal(ks[3], (NUM_EXPERTS, DFF, DMODEL), DMODEL), 'ff_post_act_weight': _trunc_normal(ks[4], (NUM_EXPERTS, DMODEL, DFF), DFF)}
    _L0_ffn_in = _L0_ffn_setup()

    def _L1_attn_setup():
        import jax, jax.numpy as jnp
        import numpy as np
        D_MODEL = 128
        NUM_HEADS = 16
        D_HEAD = 64
        N_CTX = 256
        BATCH = 4
        NEG_INF = -10000000000.0
        key = jax.random.key(seed)
        k1, k2, k3, k4, k5 = jax.random.split(key, 5)
        s = 1.0 / np.sqrt(D_MODEL).astype(np.float32)
        x = jax.random.normal(k1, (BATCH, N_CTX, D_MODEL), dtype=jnp.float32)
        W_K = jax.random.normal(k2, (NUM_HEADS, D_HEAD, D_MODEL), dtype=jnp.float32) * s
        W_Q = jax.random.normal(k3, (NUM_HEADS, D_HEAD, D_MODEL), dtype=jnp.float32) * s
        W_V = jax.random.normal(k4, (NUM_HEADS, D_HEAD, D_MODEL), dtype=jnp.float32) * s
        W_O = jax.random.normal(k5, (D_MODEL, NUM_HEADS * D_HEAD), dtype=jnp.float32) * s
        return {'x': x, 'W_K': W_K, 'W_Q': W_Q, 'W_V': W_V, 'W_O': W_O}
    _L1_attn_in = _L1_attn_setup()

    def _L1_ffn_setup():
        import jax, jax.numpy as jnp
        import numpy as np
        K = 4
        ROUTED_SCALING = 1.0
        NORM_TOPK = True

        def _gate(hidden_states, router_w, router_bias):
            logits = jnp.einsum('bsh,he->bse', hidden_states, router_w).astype(jnp.float32)
            scores = jax.nn.softmax(logits, axis=-1)
            corrected = scores + router_bias
            _, top_k_indices = jax.lax.top_k(corrected, K)
            top_k_weights = jnp.take_along_axis(scores, top_k_indices, axis=-1)
            if NORM_TOPK:
                top_k_weights = top_k_weights / (top_k_weights.sum(-1, keepdims=True) + 1e-20)
            top_k_weights = top_k_weights * ROUTED_SCALING
            return (top_k_weights.astype(hidden_states.dtype), top_k_indices)
        key = jax.random.key(seed)
        ks = jax.random.split(key, 9)
        B, S, H, E, I, IS = (2, 128, 128, 8, 64, 256)
        sc = 0.02
        return {'hidden_states': jax.random.normal(ks[0], (B, S, H), jnp.float32), 'router_w': jax.random.normal(ks[1], (H, E), jnp.float32) * sc, 'router_bias': jnp.zeros((), jnp.float32), 'gate_w': jax.random.normal(ks[2], (E, H, I), jnp.float32) * sc, 'up_w': jax.random.normal(ks[3], (E, H, I), jnp.float32) * sc, 'down_w': jax.random.normal(ks[4], (E, I, H), jnp.float32) * sc, 's_gate_w': jax.random.normal(ks[5], (H, IS), jnp.float32) * sc, 's_up_w': jax.random.normal(ks[6], (H, IS), jnp.float32) * sc, 's_down_w': jax.random.normal(ks[7], (IS, H), jnp.float32) * sc}
    _L1_ffn_in = _L1_ffn_setup()
    _d = {'L0_attn_x': _L0_attn_in['x'], 'L0_attn_Wq': _L0_attn_in['Wq'], 'L0_attn_bq': _L0_attn_in['bq'], 'L0_attn_Wk': _L0_attn_in['Wk'], 'L0_attn_bk': _L0_attn_in['bk'], 'L0_attn_Wv': _L0_attn_in['Wv'], 'L0_attn_bv': _L0_attn_in['bv'], 'L0_attn_Wp': _L0_attn_in['Wp'], 'L0_attn_bp': _L0_attn_in['bp'], 'L0_attn_lambda_q1': _L0_attn_in['lambda_q1'], 'L0_attn_lambda_k1': _L0_attn_in['lambda_k1'], 'L0_attn_lambda_q2': _L0_attn_in['lambda_q2'], 'L0_attn_lambda_k2': _L0_attn_in['lambda_k2'], 'L0_ffn_router_weight': _L0_ffn_in['router_weight'], 'L0_ffn_ff_pre_act_weight': _L0_ffn_in['ff_pre_act_weight'], 'L0_ffn_gate_weight': _L0_ffn_in['gate_weight'], 'L0_ffn_ff_post_act_weight': _L0_ffn_in['ff_post_act_weight'], 'L1_attn_W_K': _L1_attn_in['W_K'], 'L1_attn_W_Q': _L1_attn_in['W_Q'], 'L1_attn_W_V': _L1_attn_in['W_V'], 'L1_attn_W_O': _L1_attn_in['W_O'], 'L1_ffn_router_w': _L1_ffn_in['router_w'], 'L1_ffn_router_bias': _L1_ffn_in['router_bias'], 'L1_ffn_gate_w': _L1_ffn_in['gate_w'], 'L1_ffn_up_w': _L1_ffn_in['up_w'], 'L1_ffn_down_w': _L1_ffn_in['down_w'], 'L1_ffn_s_gate_w': _L1_ffn_in['s_gate_w'], 'L1_ffn_s_up_w': _L1_ffn_in['s_up_w'], 'L1_ffn_s_down_w': _L1_ffn_in['s_down_w']}
    _x0 = _d['L0_attn_x']
    _d['L0_attn_x'] = jax.random.normal(jax.random.fold_in(jax.random.key(seed), 1), (8, 512, 128), dtype=_x0.dtype)
    del _x0
    return _d

def reference(L0_attn_x, L0_attn_Wq, L0_attn_bq, L0_attn_Wk, L0_attn_bk, L0_attn_Wv, L0_attn_bv, L0_attn_Wp, L0_attn_bp, L0_attn_lambda_q1, L0_attn_lambda_k1, L0_attn_lambda_q2, L0_attn_lambda_k2, L0_ffn_router_weight, L0_ffn_ff_pre_act_weight, L0_ffn_gate_weight, L0_ffn_ff_post_act_weight, L1_attn_W_K, L1_attn_W_Q, L1_attn_W_V, L1_attn_W_O, L1_ffn_router_w, L1_ffn_router_bias, L1_ffn_gate_w, L1_ffn_up_w, L1_ffn_down_w, L1_ffn_s_gate_w, L1_ffn_s_up_w, L1_ffn_s_down_w):

    def _L0_attn_ref(x, Wq, bq, Wk, bk, Wv, bv, Wp, bp, lambda_q1, lambda_k1, lambda_q2, lambda_k2):
        import jax, jax.numpy as jnp
        import numpy as np
        EMBED_DIM = 128
        NUM_HEADS = 16
        EFF_HEADS = NUM_HEADS // 2
        HEAD_DIM = EMBED_DIM // NUM_HEADS
        LAMBDA_INIT = 0.8
        B, N = (2, 256)
        Bb, Nn, C = x.shape
        H, H2, hd = (NUM_HEADS, EFF_HEADS, HEAD_DIM)
        scale = hd ** (-0.5)
        q = (x @ Wq.T + bq).reshape(Bb, Nn, H, hd).transpose(0, 2, 1, 3)
        k = (x @ Wk.T + bk).reshape(Bb, Nn, H, hd).transpose(0, 2, 1, 3)
        v = (x @ Wv.T + bv).reshape(Bb, Nn, H, hd).transpose(0, 2, 1, 3)
        q1, q2 = (q[:, :H2], q[:, H2:])
        k1, k2 = (k[:, :H2], k[:, H2:])
        v1, v2 = (v[:, :H2], v[:, H2:])
        l1 = jnp.exp(jnp.minimum((lambda_q1 * lambda_k1).sum((-1, -2)), 5.0))
        l2 = jnp.exp(jnp.minimum((lambda_q2 * lambda_k2).sum((-1, -2)), 5.0))
        lv = (l1 - l2 + LAMBDA_INIT).mean()
        a1 = jax.nn.softmax(jnp.einsum('bhnd,bhmd->bhnm', q1, k1) * scale, axis=-1)
        x1 = jnp.einsum('bhnm,bhmd->bhnd', a1, v1).transpose(0, 2, 1, 3).reshape(Bb, Nn, C // 2)
        a2 = jax.nn.softmax(jnp.einsum('bhnd,bhmd->bhnm', q2, k2) * scale, axis=-1)
        x2 = jnp.einsum('bhnm,bhmd->bhnd', a2, v2).transpose(0, 2, 1, 3).reshape(Bb, Nn, C // 2)
        out = jnp.concatenate([x1 - lv * x2, x2], axis=-1) @ Wp.T + bp
        return out

    def _L0_ffn_ref(x, router_weight, ff_pre_act_weight, gate_weight, ff_post_act_weight):
        import jax, jax.numpy as jnp
        import numpy as np
        import math
        DMODEL = 128
        DFF = 512
        NUM_EXPERTS = 8
        TOPK = 2
        CAP_FACTOR = 1.25
        EPS = 1.1920929e-07

        def _trunc_normal(key, shape, fan_in, scale=1.0):
            std = scale * (1.0 / fan_in) ** 0.5
            return jax.random.truncated_normal(key, -2.0, 2.0, shape, jnp.float32) * std
        orig_shape = x.shape
        h = x.reshape(-1, DMODEL)
        T = h.shape[0]
        logits = jnp.einsum('th,eh->te', h, router_weight)
        probs = jax.nn.softmax(logits.astype(jnp.float32), axis=-1)
        topk_probs, selected = jax.lax.top_k(probs, TOPK)
        topk_probs = topk_probs / jnp.maximum(topk_probs.sum(-1, keepdims=True), EPS)
        flat_tokens = jnp.repeat(jnp.arange(T), TOPK)
        flat_experts = selected.reshape(-1)
        flat_weights = topk_probs.reshape(-1)
        A = T * TOPK
        capacity = max(1, math.ceil(CAP_FACTOR * A / NUM_EXPERTS))
        weight_order = jnp.argsort(-flat_weights, stable=True)
        grouped_order = jnp.argsort(flat_experts[weight_order], stable=True)
        sort_order = weight_order[grouped_order]
        se = flat_experts[sort_order]
        st = flat_tokens[sort_order]
        sw = flat_weights[sort_order]
        counts = jnp.bincount(se, length=NUM_EXPERTS)
        offsets = jnp.cumsum(counts) - counts
        slot = jnp.arange(A) - offsets[se]
        keep = slot < capacity
        sw = jnp.where(keep, sw, 0.0)
        token_wsum = jnp.zeros(T, jnp.float32).at[st].add(sw)
        kept_w = sw / jnp.maximum(token_wsum[st], EPS)
        FC = NUM_EXPERTS * capacity
        dispatch = jnp.where(keep, se * capacity + slot, FC)
        expert_inputs = jnp.zeros((FC + 1, DMODEL), x.dtype).at[dispatch].set(h[st])
        expert_inputs = expert_inputs[:FC].reshape(NUM_EXPERTS, capacity, DMODEL)
        pre = jnp.einsum('ech,edh->ecd', expert_inputs, ff_pre_act_weight)
        gate = jnp.einsum('ech,edh->ecd', expert_inputs, gate_weight)
        expert_out = jnp.einsum('ecd,ehd->ech', pre * jax.nn.silu(gate), ff_post_act_weight)
        eo_flat = jnp.concatenate([expert_out.reshape(FC, DMODEL), jnp.zeros((1, DMODEL), x.dtype)], axis=0)
        updates = eo_flat[dispatch] * kept_w.astype(x.dtype)[:, None]
        out = jnp.zeros((T, DMODEL), x.dtype).at[st].add(updates)
        return out.reshape(orig_shape)

    def _L1_attn_ref(x, W_K, W_Q, W_V, W_O):
        import jax, jax.numpy as jnp
        import numpy as np
        D_MODEL = 128
        NUM_HEADS = 16
        D_HEAD = 64
        N_CTX = 256
        BATCH = 4
        NEG_INF = -10000000000.0
        b, q_len, d_model = x.shape
        d_head = W_K.shape[1]
        K = jnp.einsum('bpd,ihd->biph', x, W_K)
        Q = jnp.einsum('bpd,ihd->biph', x, W_Q)
        V = jnp.einsum('bpd,ihd->biph', x, W_V)
        scores = jnp.einsum('biph,biqh->biqp', K, Q)
        mask = jnp.tril(jnp.ones((q_len, q_len), dtype=bool))
        scores = jnp.where(mask[None, None, :, :], scores, NEG_INF)
        attn = jax.nn.softmax(scores / np.sqrt(d_head).astype(np.float32), axis=-1)
        z = jnp.einsum('biph,biqp->biqh', V, attn)
        z_flat = jnp.transpose(z, (0, 2, 1, 3)).reshape(b, q_len, -1)
        out = jnp.einsum('bqf,df->bqd', z_flat, W_O)
        return out

    def _L1_ffn_ref(hidden_states, router_w, router_bias, gate_w, up_w, down_w, s_gate_w, s_up_w, s_down_w):
        import jax, jax.numpy as jnp
        import numpy as np
        K = 4
        ROUTED_SCALING = 1.0
        NORM_TOPK = True

        def _gate(hidden_states, router_w, router_bias):
            logits = jnp.einsum('bsh,he->bse', hidden_states, router_w).astype(jnp.float32)
            scores = jax.nn.softmax(logits, axis=-1)
            corrected = scores + router_bias
            _, top_k_indices = jax.lax.top_k(corrected, K)
            top_k_weights = jnp.take_along_axis(scores, top_k_indices, axis=-1)
            if NORM_TOPK:
                top_k_weights = top_k_weights / (top_k_weights.sum(-1, keepdims=True) + 1e-20)
            top_k_weights = top_k_weights * ROUTED_SCALING
            return (top_k_weights.astype(hidden_states.dtype), top_k_indices)
        B, S, H = hidden_states.shape
        tk_w, tk_i = _gate(hidden_states, router_w, router_bias)
        hf = hidden_states.reshape(-1, H)
        tk_w = tk_w.reshape(-1, K)
        tk_i = tk_i.reshape(-1, K)
        gate_all = jnp.einsum('nh,ehi->nei', hf, gate_w)
        up_all = jnp.einsum('nh,ehi->nei', hf, up_w)
        act = jax.nn.silu(gate_all) * up_all
        down_all = jnp.einsum('nei,eih->neh', act, down_w)
        sel = jnp.take_along_axis(down_all, tk_i[:, :, None], axis=1)
        routed = (sel * tk_w[:, :, None]).sum(axis=1).reshape(B, S, H)
        g = jnp.einsum('bsh,hm->bsm', hidden_states, s_gate_w)
        u = jnp.einsum('bsh,hm->bsm', hidden_states, s_up_w)
        shared = jnp.einsum('bsm,mh->bsh', jax.nn.silu(g) * u, s_down_w)
        return routed + shared
    x = L0_attn_x
    x = x + _L0_attn_ref(_layernorm(x, axis=-1), L0_attn_Wq, L0_attn_bq, L0_attn_Wk, L0_attn_bk, L0_attn_Wv, L0_attn_bv, L0_attn_Wp, L0_attn_bp, L0_attn_lambda_q1, L0_attn_lambda_k1, L0_attn_lambda_q2, L0_attn_lambda_k2)
    x = x + _L0_ffn_ref(_layernorm(x, axis=-1), L0_ffn_router_weight, L0_ffn_ff_pre_act_weight, L0_ffn_gate_weight, L0_ffn_ff_post_act_weight)
    x = x + _L1_attn_ref(_layernorm(x, axis=-1), L1_attn_W_K, L1_attn_W_Q, L1_attn_W_V, L1_attn_W_O)
    x = x + _L1_ffn_ref(_layernorm(x, axis=-1), L1_ffn_router_w, L1_ffn_router_bias, L1_ffn_gate_w, L1_ffn_up_w, L1_ffn_down_w, L1_ffn_s_gate_w, L1_ffn_s_up_w, L1_ffn_s_down_w)
    return x

_drawn_inputs = setup_inputs


def setup_inputs(seed=0):
    import zlib

    import numpy as np

    out = dict(_drawn_inputs(seed))
    spreads = {'L0_attn_bq': (0.0, 0.8),
     'L0_attn_bk': (0.0, 2.0),
     'L0_attn_bv': (0.0, 0.1),
     'L0_attn_bp': (0.0, 0.1)}
    factors = {'L0_attn_Wq': 8.0,
     'L0_attn_Wk': 8.0,
     'L0_attn_Wv': 4.94,
     'L0_attn_lambda_q1': 64.0,
     'L0_attn_lambda_k1': 37.723,
     'L0_attn_lambda_q2': 27.385,
     'L0_attn_lambda_k2': 29.596,
     'L1_ffn_router_w': 8.0,
     'L1_ffn_gate_w': 8.0,
     'L1_ffn_up_w': 8.0,
     'L1_ffn_down_w': 8.0,
     'L1_ffn_s_gate_w': 8.0,
     'L1_ffn_s_up_w': 8.0,
     'L1_ffn_s_down_w': 8.0}
    for name, (base, spread) in spreads.items():
        noise = np.random.default_rng([zlib.crc32(name.encode()), seed]).standard_normal(out[name].shape)
        drawn = base * np.exp(spread * noise) if base else spread * noise
        out[name] = jnp.asarray(drawn.astype(out[name].dtype))
    for name, factor in factors.items():
        out[name] = (out[name] * factor).astype(out[name].dtype)
    return out
```

```python
import numpy as np
import concourse.bass as bass
from concourse import mybir
from concourse.alu_op_type import AluOpType as ALU

F32 = mybir.dt.float32
BF16 = mybir.dt.bfloat16
I32 = mybir.dt.int32
U32 = mybir.dt.uint32
ACT = mybir.ActivationFunctionType
AX = mybir.AxisListType

NB = 8
NT = 32
E = 8
CAP = 1280
ROWS = E * CAP
EPS = 1.1920929e-07
LN_EPS = 1e-5
NEG = -1e10


class Eng:

    def __init__(self, nc, eng, name):
        self.e = eng
        self.sem = nc.alloc_semaphore("done_" + name)
        self.n = 0
        self.seen = {}

    def did(self, ins):
        self.n += 1
        ins.then_inc(self.sem, 1)
        return (self.sem, self.n)

    def need(self, *marks):
        for m in marks:
            if m is None:
                continue
            sem, val = m
            key = sem.name if hasattr(sem, "name") else id(sem)
            if self.seen.get(key, 0) < val:
                self.e.wait_ge(sem, val)
                self.seen[key] = val


class Arrivals:

    def __init__(self, nc, name):
        self.sem = nc.alloc_semaphore(name)
        self.n = 0

    def add(self, ins):
        self.n += 16
        ins.then_inc(self.sem, 16)
        return (self.sem, self.n)


def program(nc, T, out, upto=9):
    pe, dve, act, pool, sp = (Eng(nc, e, n) for e, n in (
        (nc.tensor, "pe"), (nc.vector, "dve"), (nc.scalar, "act"), (nc.gpsimd, "pool"), (nc.sync, "sp")))
    V, S, G, M = nc.vector, nc.scalar, nc.gpsimd, nc.tensor

    def sb(name, shape, dt=F32):
        return nc.alloc_sbuf_tensor(name, shape, dt)

    def dram(name, shape, dt=F32):
        return nc.dram_tensor(name, shape, dt, kind="Internal").ap()

    x = sb("x", [128, NT, 128])
    identf = sb("identf", [128, 128])
    identb = sb("identb", [128, 128], BF16)
    onesf = sb("onesf", [128, 128])
    ustrict = sb("ustrict", [128, 128])
    maskb = sb("maskb", [128, 128], BF16)
    mhalf = sb("mhalf", [128, 32])
    w0 = sb("w0", [128, 4, 128])
    bqk = sb("bqk", [128, 2])
    bvp = sb("bvp", [128, 2, 128])
    lam = sb("lam", [8, 4, 8])
    lamw = sb("lamw", [8, 32])
    nlv = sb("nlv", [128, 1])
    ar1 = sb("ar1", [128, 16384])
    ar2 = sb("ar2", [128, 8192])
    xn = sb("xn", [128, 4, 128])
    xnT = [sb(f"xnT{i}", [128, 512]) for i in range(2)]
    stt = sb("stt", [128, 4, 6])
    mv = sb("mv", [128, 4, 2])
    ve = sb("ve", [128, 4])
    rstd = sb("rstd", [128, 4])

    bank = [nc.alloc_psum_tensor(f"bank{i}", [128, 512], F32) for i in range(4)]
    pS = [nc.alloc_psum_tensor(f"pS{i}", [128, 1024], F32) for i in range(2)]
    misc = bank[3]
    misc_free = [None]

    xin = T["x"].rearrange("(t p) d -> p t d", p=128)
    ax = [Arrivals(nc, f"ax{b}") for b in range(NB)]
    aw = Arrivals(nc, "aw")
    for b in range(1):
        t_x0 = ax[b].add(nc.sync.dma_start(x[:, 4 * b:4 * b + 4, :], xin[:, 4 * b:4 * b + 4, :]))
    got_x = [t_x0]
    for dst, src in ((w0, "W0"), (bqk, "bqk"), (bvp, "bvp"), (lam, "lam")):
        got_w = aw.add(nc.sync.dma_start(dst[tuple(slice(None) for _ in dst.shape)], T[src]))
    for b in range(1, NB):
        got_x.append(ax[b].add(nc.sync.dma_start(x[:, 4 * b:4 * b + 4, :], xin[:, 4 * b:4 * b + 4, :])))

    c0 = pool.did(G.memset(identf[:, :], 0.0))
    c1 = pool.did(G.memset(identb[:, :], 0.0))
    c2 = pool.did(G.memset(onesf[:, :], 1.0))
    c3 = pool.did(G.memset(mhalf[:, :], -0.5))
    pool.need(c0)
    G_id = pool.did(G.affine_select(out=identf[:, :], in_=identf[:, :], compare_op=ALU.not_equal, fill=1.0,
                                    base=0, pattern=[[-1, 128]], channel_multiplier=1))
    pool.need(c1)
    G_idb = pool.did(G.affine_select(out=identb[:, :], in_=identb[:, :], compare_op=ALU.not_equal, fill=1.0,
                                     base=0, pattern=[[-1, 128]], channel_multiplier=1))

    rt0 = sb("rt0", [128, E])
    got_rt = Arrivals(nc, "a_rt").add(nc.sync.dma_start(rt0[:, :], T["rt0"]))
    rr = sb("rr", [128, 6, NT, E])
    rd, rp, rsrt, rg, rq, rpx = (rr[:, n] for n in range(6))
    re_ = sb("re", [128, 9, E, NT])
    ew, ewm, esel, eg, eq, epos, ekeep, epx, ewk = (re_[:, n] for n in range(9))
    rsel_ = sb("rsel", [128, NT, E])
    rsel = rsel_[:, :, :]
    escan_ = sb("escan", [128, 256])
    escan = escan_[:, :]
    rs8 = sb("rs8", [128, 32])
    r32 = [sb(f"r32_{n}", [128, NT]) for n in range(4)]
    kw_ = [sb(f"kw{n}", [128, NT]) for n in range(2)]
    idx = [sb(f"idx{n}", [128, NT], U32) for n in range(2)]
    segm = sb("segm", [128, 256])
    eoff = sb("eoff", [128, E])
    zero = sb("zero", [128, 1024])
    wv1, wo1 = sb("wv1", [128, 1024]), sb("wo1", [128, 8, 128])
    gw1, uw1, dw1 = sb("gw1", [128, 768]), sb("uw1", [128, 768]), sb("dw1", [128, 6, 128])
    rt1, rb1 = sb("rt1", [128, E]), sb("rb1", [128, 1])
    nm1, den1, rd1 = (sb(n, [128, 8]) for n in ("nm1", "den1", "rd1"))
    xT4 = sb("xT4", [128, 4096])
    a_wl1 = Arrivals(nc, "a_wl1")
    for t_, n in ((wv1, "wv1"), (wo1, "wo1"), (gw1, "gw1"), (uw1, "uw1"), (dw1, "dw1"), (rt1, "rt1"), (rb1, "rb1")):
        got_w1 = a_wl1.add(nc.sync.dma_start(t_[tuple(slice(None) for _ in t_.shape)], T[n]))
    k = pool.did(G.memset(maskb[:, :], 0.0))
    pool.need(k)
    c_mask = pool.did(G.affine_select(out=maskb[:, :], in_=maskb[:, :], compare_op=ALU.is_ge, fill=NEG,
                                      base=0, pattern=[[-1, 128]], channel_multiplier=1))
    rows_in = dram("rows_in", [ROWS, 128])
    rows_out = dram("rows_out", [ROWS + 1, 128])
    pool.need(c2)
    c_us = pool.did(G.affine_select(out=ustrict[:, :], in_=onesf[:, :], compare_op=ALU.is_gt, fill=0.0,
                                    base=0, pattern=[[1, 128]], channel_multiplier=-1))
    k = pool.did(G.memset(zero[:, :], 0.0))
    a_z = Arrivals(nc, "a_z")
    act.need(k)
    for n in range(10):
        k_zero = a_z.add(nc.scalar.dma_start(
            rows_in.rearrange("(p r) d -> p (r d)", p=128)[:, 1024 * n:1024 * n + 1024], zero[:, :]))
    a_zr = Arrivals(nc, "a_zr")
    k_zrow = a_zr.add(nc.scalar.dma_start(rows_out[ROWS:ROWS + 1, :], zero[0:1, 0:128]))
    k = dve.did(V.memset(segm[:, :], 1.0))
    dve.need(k)
    c_seg = dve.did(V.memset(segm[:, 0:256:NT], 0.0))
    for e in range(E):
        c_seg = dve.did(V.memset(eoff[:, e:e + 1], float(CAP * e - ROWS)))
    dve.need(c_seg)

    xn_free = [None]

    def ln_stats(b, ready):
        dve.need(ready)
        for t in range(4):
            k = dve.did(V.bn_stats(stt[:, t, :], x[:, 4 * b + t, :]))
        dve.need(k)
        for t in range(4):
            k = dve.did(V.bn_aggr(mv[:, t, :], stt[:, t, :]))
        dve.need(k)
        k = dve.did(V.tensor_scalar(ve[:, :], mv[:, :, 1], LN_EPS, None, ALU.add))
        pool.need(k, c3)
        return pool.did(G.tensor_tensor(rstd[:, :], ve[:, :], mhalf[:, 0:4], ALU.pow))

    def ln_apply(b, k_rstd, dst=None, free=None):
        dve.need(k_rstd, free if dst is not None else xn_free[0])
        for t in range(4):
            k = dve.did(V.tensor_scalar(dst[:, 4 * b + t, :] if dst is not None else xn[:, t, :],
                                        x[:, 4 * b + t, :], mv[:, t, 0:1], rstd[:, t:t + 1],
                                        ALU.subtract, ALU.mult))
        return k

    def transpose_tiles(srcs, ready):
        pe.need(ready, misc_free[0], G_id)
        for t, s in enumerate(srcs):
            ins = M.transpose(misc[:, 128 * t:128 * t + 128], s, identf[:, :])
        return pe.did(ins)

    ab = ar1[:, :].bitcast(BF16).rearrange("p (r s h n) -> p r s h n", r=2, s=2, h=16)
    qst = [ab[:, i, 0] for i in range(2)]
    kst = [ab[:, i, 1] for i in range(2)]
    vst = [ar2[:, 2048 * i:2048 * i + 2048].rearrange("p (k h c) -> p k h c", k=4, h=16) for i in range(2)]
    NPT = 8
    pt = [ar2[:, 4096 + 512 * i:4096 + 512 * i + 512] for i in range(NPT)]
    qkp = [sb(f"qkp{i}", [128, 3, 512], BF16) for i in range(2)]
    res = sb("res", [128, 512])
    mx = [sb(f"mx{i}", [128, 16]) for i in range(2)]
    mr = sb("mr", [128, 4, 4])
    mp = [sb(f"mp{i}", [128, 4, 12], BF16) for i in range(2)]
    mT = [sb(f"mT{i}", [12, 512], BF16) for i in range(2)]
    oT = sb("oT", [128, 512])
    rden = sb("rden", [128, 4, 4])
    att = [sb(f"att{i}", [128, 4, 128]) for i in range(2)]
    aT = sb("aT", [128, 512])
    dq = [dram(f"dq{i}", [16, 24, 512], BF16) for i in range(2)]
    dk = [dram(f"dk{i}", [16, 40, 512], BF16) for i in range(2)]
    dm = [dram(f"dm{i}", [12, 512], BF16) for i in range(2)]
    a_dq, a_dk, a_dm = ([Arrivals(nc, f"a_{n}{i}") for i in range(2)] for n in ("dq", "dk", "dm"))
    a_qs, a_ks, a_ms = ([Arrivals(nc, f"a_{n}{i}") for i in range(2)] for n in ("qs", "ks", "ms"))

    one_pair = float(np.frombuffer(np.uint32(0x3F803F80).tobytes(), np.float32)[0])
    flat = ar1[:, :].rearrange("p (r s f) -> p r s f", r=2, s=2)
    z_stack, z_v = [], []
    for i in range(2):
        a = dve.did(V.memset(flat[64:96, i, 0], 0.0))
        pool.need((pool.sem, pool.n))
        b_ = pool.did(G.memset(flat[64:96, i, 1], 0.0))
        pool.need(b_)
        c = pool.did(G.memset(flat[96:99, i, 1], one_pair))
        z_stack.append((a, b_, c))
        v0 = dve.did(V.memset(ar2[:, 2048 * i:2048 * i + 2048], 0.0))
        dve.need(v0)
        z_v.append(dve.did(V.memset(vst[i][:, :, :, 8:9], 1.0)))

    pool.need((pool.sem, pool.n))

    dve.need(got_w)
    k = dve.did(V.tensor_tensor(lamw[:, 0:16].rearrange("p (a d) -> p a d", a=2), lam[:, 0:4:2, :], lam[:, 1:4:2, :],
                                ALU.mult))
    dve.need(k)
    k = dve.did(V.tensor_reduce(lamw[:, 16:18], lamw[:, 0:16].rearrange("p (a d) -> p a d", a=2), AX.X, ALU.add))
    dve.need(k)
    k = dve.did(V.tensor_scalar(lamw[:, 18:20], lamw[:, 16:18], 5.0, None, ALU.min))
    act.need(k)
    k = act.did(S.activation(lamw[:, 20:22], lamw[:, 18:20], ACT.Exp))
    dve.need(k)
    k = dve.did(V.tensor_tensor(lamw[:, 22:23], lamw[:, 20:21], lamw[:, 21:22], ALU.subtract))
    dve.need(k)
    k = dve.did(V.tensor_scalar(lamw[:, 23:24], lamw[:, 22:23], 0.8, -1.0 / 8, ALU.add, ALU.mult))
    pe.need(k, c2)
    k = pe.did(M.matmul(misc[:, 0:1], onesf[0:8, :], lamw[:, 23:24], start=True, stop=True))
    dve.need(k)
    k_nlv = dve.did(V.tensor_copy(nlv[:, :], misc[:, 0:1]))
    misc_free[0] = k_nlv

    st = {"xnT_free": [None, None], "qkp_free": [None, None], "res_free": None, "v_ready": [None] * NB,
          "stack_ready": [None] * NB, "st_done": [None] * NB, "s_done": [None] * NB, "pv_done": [None] * NB,
          "x_done": [None] * NB}

    def prep(b):
        i = b % 2
        k = ln_stats(b, got_x[b])
        k = ln_apply(b, k)
        k_xn = k
        yield
        k = transpose_tiles([xn[:, t, :] for t in range(4)], k_xn)
        xn_free[0] = k
        pool.need(k_xn, got_w)
        st["xb%d" % b] = pool.did(G.tensor_tensor(
            x[:, 4 * b:4 * b + 4, :], x[:, 4 * b:4 * b + 4, :],
            bvp[:, 1, :][:, None, :].broadcast_to([128, 4, 128]), ALU.add))
        act.need(k, st["xnT_free"][i])
        k_T = act.did(S.copy(xnT[i][:, :], misc[:, :]))
        misc_free[0] = k_T
        yield
        for n in range(2):
            pe.need(k_T, misc_free[0], got_w)
            k = pe.did(M.matmul(misc[:, :], w0[:, n, :], xnT[i][:, :], start=True, stop=True))
            act.need(k, st["qkp_free"][n])
            k1 = act.did(S.activation(qkp[n][:, 0, :], misc[:, :], ACT.Identity, bias=bqk[:, n:n + 1]))
            dve.need(k1, st["res_free"])
            k2 = dve.did(V.scalar_tensor_tensor(res[:, :], misc[:, :], bqk[:, n:n + 1], qkp[n][:, 0, :],
                                                ALU.add, ALU.subtract))
            misc_free[0] = k2
            dve.need(k2)
            k3 = dve.did(V.tensor_copy(qkp[n][:, 1, :], res[:, :]))
            dve.need(k3)
            k4 = dve.did(V.tensor_tensor(qkp[n][:, 2, :], res[:, :], qkp[n][:, 1, :], ALU.subtract))
            st["res_free"] = k4
            if n == 0:
                sp.need(k1, k4, st["dq_free"][i] if "dq_free" in st else None)
                for a in range(3):
                    w = a_dq[i].add(nc.sync.dma_start(dq[i][:, 8 * a:8 * a + 8, :], qkp[0][:, a, :]))
                st["qkp_free"][0] = w
                yield
                sp.need(w, *z_stack[i], st["st_done"][b - 2] if b >= 2 else None)
                for g in range(3):
                    w = a_qs[i].add(nc.sync.dma_start(qst[i][24 * g:24 * g + 24, :, :],
                                                      dq[i].rearrange("h c n -> c h n")))
                k_qs = w
            else:
                sp.need(k1, k4)
                for a in range(5):
                    w = a_dk[i].add(nc.sync.dma_start(dk[i][:, 8 * a:8 * a + 8, :], qkp[1][:, a % 3, :]))
                st["qkp_free"][1] = w
                yield
                sp.need(w)
                for g in range(3):
                    w = a_ks[i].add(nc.sync.dma_start(kst[i][24 * g:24 * g + 24, :, :],
                                                      dk[i][:, 8 * g:8 * g + 24, :].rearrange("h c n -> c h n")))
                k_ks = w
        st["stack_ready"][b] = (k_qs, k_ks)
        pe.need(misc_free[0])
        for t in range(4):
            ins = M.matmul(misc[:, 128 * t:128 * t + 128], xnT[i][:, 128 * t:128 * t + 128], w0[:, 2, :],
                           start=True, stop=True)
        k = pe.did(ins)
        st["xnT_free"][i] = k
        dve.need(k, z_v[i], st["pv_done"][b - 2] if b >= 2 else None)
        k = dve.did(V.tensor_tensor(vst[i][:, :, :, 0:8],
                                    misc[:, :].rearrange("p (t h d) -> p t h d", t=4, h=16),
                                    bvp[:, 0, :].rearrange("p (h d) -> p h d", d=8)[:, None, :, :]
                                    .broadcast_to([128, 4, 16, 8]), ALU.add))
        misc_free[0] = k
        st["v_ready"][b] = k
        yield

    pS_free = [None, None]
    ns = [0]
    mx_free = [None, None]
    mx_ready = {}

    def scores(Gr, j):
        b, g = Gr // 4, Gr % 4
        h = 4 * g + j
        for half in range(2):
            s = ns[0] % 2
            ns[0] += 1
            pe.need(*st["stack_ready"][b], *z_stack[b % 2], pS_free[s])
            for q in range(2):
                qb = 2 * half + q
                ins = M.matmul(pS[s][:, 512 * q:512 * q + 512], qst[b % 2][0:96, h, 128 * qb:128 * qb + 128],
                               kst[b % 2][0:96, h, :], start=True, stop=True)
            k = pe.did(ins)
            dve.need(k, mx_free[Gr % 2])
            c = 4 * j + 2 * half
            pS_free[s] = dve.did(V.tensor_reduce(mx[Gr % 2][:, c:c + 2],
                                                 pS[s][:, :].rearrange("p (a n) -> p a n", a=2),
                                                 AX.X, ALU.max, negate=True))
        mx_ready[Gr] = pS_free[s]
        if g == 3 and j == 3:
            st["s_done"][b] = k

    mp_free, mT_free, m_ready = [None, None], [None, None], {}

    def shift_rows(Gr):
        b, g, i = Gr // 4, Gr % 4, Gr % 2
        mv_ = mx[i][:, :].rearrange("p (j q) -> p q j", j=4)
        dve.need(mx_ready[Gr], mp_free[i])
        k = dve.did(V.tensor_copy(mp[i][:, :, 0:4], mv_))
        dve.need(k)
        k = dve.did(V.tensor_tensor(mr[:, :, :], mv_, mp[i][:, :, 0:4], ALU.subtract))
        mx_free[i] = k
        dve.need(k)
        k = dve.did(V.tensor_copy(mp[i][:, :, 4:8], mr[:, :, :]))
        dve.need(k)
        k = dve.did(V.tensor_tensor(mp[i][:, :, 8:12], mr[:, :, :], mp[i][:, :, 4:8], ALU.subtract))
        pe.need(k, misc_free[0], G_idb)
        mb = misc[:, :].bitcast(BF16)
        for q in range(4):
            ins = M.transpose(mb[0:12, 128 * q:128 * q + 128], mp[i][:, q, :], identb[:, :])
        k = pe.did(ins)
        mp_free[i] = k
        act.need(k, mT_free[i])
        k = act.did(S.copy(mT[i][:, :], mb[0:12, 0:512]))
        misc_free[0] = k
        sp.need(k, m_ready.get(Gr - 2))
        w = a_dm[i].add(nc.sync.dma_start(dm[i], mT[i][:, :]))
        mT_free[i] = w
        sp.need(w, st["st_done"][b - 2] if b >= 2 else None)
        m_ready[Gr] = a_ms[i].add(nc.sync.dma_start(qst[b % 2][96:99, 4 * g:4 * g + 4, :],
                                                    dm[i].rearrange("(a j) n -> a j n", a=3)))

    bST = [bank[0], bank[1]]
    bST_free = [None, None]
    bO, bO_free = bank[2], [None]
    pt_free = [None] * NPT
    pt_ready = {}
    nst = [0]

    def st_exp(Gr, kb, j):
        b, g = Gr // 4, Gr % 4
        h = 4 * g + j
        s = nst[0] % 2
        p = nst[0] % NPT
        nst[0] += 1
        pe.need(m_ready[Gr], bST_free[s])
        k = pe.did(M.matmul(bST[s][:, :], kst[b % 2][0:99, h, 128 * kb:128 * kb + 128], qst[b % 2][0:99, h, :],
                            start=True, stop=True))
        if (g, kb, j) == (3, 3, 3):
            st["st_done"][b] = k
        act.need(k, pt_free[p])
        bST_free[s] = act.did(S.activation(pt[p], bST[s][:, :], ACT.Exp, scale=8 ** -0.5))
        pt_ready[(Gr, kb, j)] = (p, bST_free[s])

    def pv(Gr, kb):
        b, g = Gr // 4, Gr % 4
        pe.need(st["v_ready"][b])
        if kb == 0:
            pe.need(bO_free[0])
        for j in range(4):
            p, ready = pt_ready.pop((Gr, kb, j))
            pe.need(ready)
            ins = M.matmul(bO[32 * j:32 * j + 32, :], vst[b % 2][:, kb, 4 * g + j, :], pt[p],
                           start=(kb == 0), stop=(kb == 3))
            pt_free[p] = k = pe.did(ins)
        if kb == 3:
            if g == 3:
                st["pv_done"][b] = k
            st["o_done"] = k

    oT_free = [None]
    att_free = [None, None]

    def take_values():
        act.need(st["o_done"], oT_free[0])
        bO_free[0] = act.did(S.copy(oT[:, :], bO[:, :]))

    def finish_group(Gr):
        b, g = Gr // 4, Gr % 4
        k = bO_free[0]
        k = transpose_tiles([oT[:, 128 * t:128 * t + 128] for t in range(4)], k)
        oT_free[0] = k
        mvw = misc[:, :].rearrange("p (t j c) -> p t j c", t=4, j=4)
        dve.need(k)
        k = dve.did(V.reciprocal(rden[:, :, :], mvw[:, :, :, 8]))
        dve.need(k, att_free[b % 2])
        k = dve.did(V.tensor_tensor(att[b % 2][:, :, 32 * g:32 * g + 32].rearrange("p t (j d) -> p t j d", j=4),
                                    mvw[:, :, :, 0:8],
                                    rden[:, :, :, None].broadcast_to([128, 4, 4, 8]), ALU.mult))
        misc_free[0] = k
        return k

    aT_free = [None]

    def project(b, ready):
        i = b % 2
        dve.need(ready, k_nlv)
        k = dve.did(V.scalar_tensor_tensor(att[i][:, :, 0:64], att[i][:, :, 64:128], nlv[:, 0:1],
                                           att[i][:, :, 0:64], ALU.mult, ALU.add))
        k = transpose_tiles([att[i][:, t, :] for t in range(4)], k)
        att_free[i] = k
        act.need(k, aT_free[0])
        k = act.did(S.copy(aT[:, :], misc[:, :]))
        misc_free[0] = k
        pe.need(k)
        for t in range(4):
            ins = M.matmul(misc[:, 128 * t:128 * t + 128], aT[:, 128 * t:128 * t + 128], w0[:, 3, :],
                           start=True, stop=True)
        k = pe.did(ins)
        aT_free[0] = k
        dve.need(k, st["xb%d" % b])
        k = dve.did(V.tensor_tensor(x[:, 4 * b:4 * b + 4, :], misc[:, :].rearrange("p (t d) -> p t d", t=4),
                                    x[:, 4 * b:4 * b + 4, :], ALU.add))
        misc_free[0] = k
        st["x_done"][b] = k

    for _ in prep(0):
        pass
    NG = 4 * NB
    for Gr in range(2):
        for j in range(4):
            scores(Gr, j)
        shift_rows(Gr)
    work = iter(())
    todo = None
    for Gr in range(NG):
        b, g = Gr // 4, Gr % 4
        if g == 0 and b + 1 < NB:
            work = prep(b + 1)
        for kb in range(4):
            st_exp(Gr, kb, 0)
            st_exp(Gr, kb, 1)
            if g < 2:
                next(work, None)
            if Gr + 2 < NG:
                scores(Gr + 2, kb)
            st_exp(Gr, kb, 2)
            if kb > 0:
                pv(Gr, kb - 1)
            elif Gr > 0:
                pv(Gr - 1, 3)
                take_values()
                todo = Gr - 1
            st_exp(Gr, kb, 3)
            if kb == 1 and todo is not None:
                k = finish_group(todo)
                st["fin"] = k
            if kb == 2 and todo is not None:
                if todo % 4 == 3:
                    project(todo // 4, st["fin"])
                todo = None
            if kb == 3 and Gr + 2 < NG:
                shift_rows(Gr + 2)
        if g == 1:
            for _ in work:
                pass
    pv(NG - 1, 3)
    take_values()
    project(NB - 1, finish_group(NG - 1))

    if upto == 1:
        return finish(nc, sp, out, x, st["x_done"])

    xs = ar1[:, 0:4096].rearrange("p (t d) -> p t d", d=128)
    xe = [ar1[:, 4096 + 1280 * i:5376 + 1280 * i].rearrange("p (t d) -> p t d", d=128) for i in range(2)]
    xeT = [ar1[:, 6656 + 1280 * i:7936 + 1280 * i] for i in range(2)]
    hT = [[ar1[:, 9216 + 2048 * i + 512 * f:9728 + 2048 * i + 512 * f] for f in range(4)] for i in range(2)]
    sg = [ar1[:, 13312 + 512 * i:13824 + 512 * i] for i in range(2)]
    eo = [ar1[:, 14336 + 512 * i:14848 + 512 * i] for i in range(2)]
    NWS = 5
    wx = [ar2[:, 1536 * i:1536 * i + 1536].rearrange("p (m f) -> p m f", m=3) for i in range(NWS)]
    a_wx = [Arrivals(nc, f"a_wx{i}") for i in range(NWS)]
    wx_ready = {}

    def load_expert(e, free):
        i = e % NWS
        sp.need(free)
        wx_ready[e] = a_wx[i].add(nc.sync.dma_start(wx[i], T["wx"][e]))

    for e in range(NWS):
        load_expert(e, st["pv_done"][NB - 1])

    lgp = pS[0][:, 0:256].rearrange("p (t e) -> p t e", e=E)
    xs_done, xT_free = [None] * NB, [None, None]
    for b in range(NB):
        i = b % 2
        k = ln_stats(b, st["x_done"][b])
        k = ln_apply(b, k, xs, st["st_done"][NB - 1])
        xs_done[b] = k
        k = transpose_tiles([xs[:, 4 * b + t, :] for t in range(4)], k)
        act.need(k, xT_free[i], st["xnT_free"][i])
        k = act.did(S.copy(xnT[i][:, :], misc[:, :]))
        misc_free[0] = k
        pe.need(k, got_rt, pS_free[0])
        for t in range(4):
            ins = M.matmul(lgp[:, 4 * b + t, :], xnT[i][:, 128 * t:128 * t + 128], rt0[:, :], start=True, stop=True)
        k = xT_free[i] = pe.did(ins)
    lg_done = k

    def soft(lg, ready):
        dve.need(ready)
        k = dve.did(V.tensor_reduce(r32[0][:, :], lg, AX.X, ALU.max))
        dve.need(k)
        k = dve.did(V.tensor_tensor(rd, lg, r32[0][:, :, None].broadcast_to([128, NT, E]), ALU.subtract))
        act.need(k)
        k = act.did(S.activation(rd, rd, ACT.Exp))
        dve.need(k)
        k = dve.did(V.tensor_reduce(r32[1][:, :], rd, AX.X, ALU.add))
        dve.need(k)
        k = dve.did(V.reciprocal(r32[2][:, :], r32[1][:, :]))
        dve.need(k)
        return dve.did(V.tensor_tensor(rp, rd, r32[2][:, :, None].broadcast_to([128, NT, E]), ALU.mult))

    def top(pr, K, ready):
        dve.need(ready)
        for t in range(NT):
            k = dve.did(V.max(rsrt[:, t, :], pr[:, t, :]))
        dve.need(k)
        kth = rsrt[:, :, K - 1:K].broadcast_to([128, NT, E])
        k = dve.did(V.tensor_tensor(rg, pr, kth, ALU.is_gt))
        k2 = dve.did(V.tensor_tensor(rq, pr, kth, ALU.is_equal))
        k3 = dve.did(V.memset(rpx[:, :, 0:1], 0.0))
        dve.need(k)
        k = dve.did(V.tensor_reduce(r32[3][:, :], rg, AX.X, ALU.add))
        for e in range(1, E):
            dve.need(k3)
            k3 = dve.did(V.tensor_tensor(rpx[:, :, e], rpx[:, :, e - 1], rq[:, :, e - 1], ALU.add))
        dve.need(k3)
        k = dve.did(V.tensor_tensor(rpx, rpx, r32[3][:, :, None].broadcast_to([128, NT, E]), ALU.add))
        dve.need(k)
        k = dve.did(V.scalar_tensor_tensor(rq, rpx, float(K) - 0.5, rq, ALU.is_lt, ALU.mult))
        dve.need(k)
        return dve.did(V.tensor_tensor(rsel, rg, rq, ALU.add))

    k = soft(lgp, lg_done)
    pS_free[0] = k
    k = top(rp, 2, k)
    dve.need(k)
    k = dve.did(V.tensor_tensor(rd, rp, rsel, ALU.mult))
    dve.need(k)
    k = dve.did(V.tensor_reduce(r32[0][:, :], rd, AX.X, ALU.add))
    dve.need(k)
    k = dve.did(V.tensor_scalar(r32[1][:, :], r32[0][:, :], EPS, None, ALU.max))
    dve.need(k)
    k = dve.did(V.reciprocal(r32[2][:, :], r32[1][:, :]))
    dve.need(k)

    def by_expert(a):
        return a.rearrange("p e t -> p t e")

    k = dve.did(V.tensor_tensor(by_expert(ew), rd, r32[2][:, :, None].broadcast_to([128, NT, E]), ALU.mult))
    k = dve.did(V.tensor_copy(by_expert(esel), rsel))
    dve.need(k)
    k = dve.did(V.scalar_tensor_tensor(ewm, ew, -1.0, esel, ALU.add, ALU.add))

    tau, cand, cnt, hit = (rs8[:, 8 * n:8 * n + 8] for n in range(4))
    k_tau = dve.did(V.memset(tau, 0.0))

    def every(a):
        return a[:, :, None].broadcast_to([128, E, NT])

    def count(ready, bankk):
        dve.need(ready)
        k = dve.did(V.tensor_reduce(cnt, eg, AX.X, ALU.add))
        pe.need(k)
        return pe.did(M.matmul(bankk[:, 0:8], onesf[:, :], cnt, start=True, stop=True))

    pe.need(misc_free[0])
    for bit in range(29, -1, -1):
        dve.need(k, k_tau)
        k = dve.did(V.tensor_scalar(cand.bitcast(I32), tau.bitcast(I32), 1 << bit, None, ALU.bitwise_or))
        dve.need(k)
        k = dve.did(V.tensor_tensor(eg, ewm, every(cand), ALU.is_ge))
        k = count(k, misc)
        dve.need(k)
        k = dve.did(V.scalar_tensor_tensor(hit, misc[:, 0:8], CAP - 0.5, cand, ALU.is_ge, ALU.mult))
        dve.need(k)
        k_tau = dve.did(V.tensor_tensor(tau, tau, hit, ALU.max))
        pe.need(k)
    dve.need(k_tau)
    k = dve.did(V.tensor_tensor(eg, ewm, every(tau), ALU.is_gt))
    kq = dve.did(V.tensor_tensor(eq, ewm, every(tau), ALU.is_equal))
    k = count(k, misc)
    dve.need(k)
    k_more = dve.did(V.tensor_copy(hit, misc[:, 0:8]))

    def places(a, ready, dst):
        af = a.rearrange("p e t -> p (e t)")
        pe.need(ready, k_more)
        M.matmul(misc[:, 0:256], ustrict[:, :], af, start=True, stop=True)
        k = pe.did(M.matmul(misc[:, 256:512], onesf[:, :], af, start=True, stop=True))
        dve.need(k, c_seg)
        k = dve.did(V.tensor_tensor_scan(escan, segm[:, :], misc[:, 256:512], 0.0, ALU.mult, ALU.add))
        dve.need(k)
        k = dve.did(V.tensor_tensor(escan, escan, misc[:, 256:512], ALU.subtract))
        dve.need(k)
        k = dve.did(V.tensor_tensor(dst.rearrange("p e t -> p (e t)"), misc[:, 0:256], escan, ALU.add))
        pe.need(k)
        return k

    pe.need(c_us)
    k = places(eq, kq, epos)
    dve.need(k)
    k = dve.did(V.tensor_tensor(epos, epos, every(hit), ALU.add))
    dve.need(k)
    k = dve.did(V.scalar_tensor_tensor(eq, epos, CAP - 0.5, eq, ALU.is_lt, ALU.mult))
    dve.need(k)
    k = dve.did(V.tensor_tensor(ekeep, eg, eq, ALU.add))
    k = places(ekeep, k, epos)
    misc_free[0] = k
    kk = dve.did(V.memset(epx[:, 0, :], 0.0))
    for e in range(1, E):
        dve.need(kk)
        kk = dve.did(V.tensor_tensor(epx[:, e, :], epx[:, e - 1, :], esel[:, e - 1, :], ALU.add))
    dve.need(k, kk)
    k = dve.did(V.tensor_tensor(epos, epos, every(eoff[:, :]), ALU.add))
    kw = dve.did(V.tensor_tensor(ewk, ew, ekeep, ALU.mult))
    dve.need(k)
    k = dve.did(V.tensor_tensor(epos, epos, ekeep, ALU.mult))
    for n in range(2):
        f = eg if n == 0 else eq
        k1 = dve.did(V.scalar_tensor_tensor(f, epx, float(n), esel, ALU.is_equal, ALU.mult))
        dve.need(k1, k)
        k1 = dve.did(V.tensor_tensor(ewm, f, epos, ALU.mult))
        dve.need(k1)
        k1 = dve.did(V.tensor_reduce(r32[0][:, :], by_expert(ewm), AX.X, ALU.add))
        dve.need(k1)
        k = dve.did(V.tensor_scalar(idx[n][:, :], r32[0][:, :], float(ROWS), None, ALU.add))
        dve.need(kw)
        k1 = dve.did(V.tensor_tensor(ewm, f, ewk, ALU.mult))
        dve.need(k1)
        k1 = dve.did(V.tensor_reduce(kw_[n][:, :], by_expert(ewm), AX.X, ALU.add))
        dve.need(k1)
    k_idx = k
    k1 = dve.did(V.tensor_tensor(r32[0][:, :], kw_[0][:, :], kw_[1][:, :], ALU.add))
    dve.need(k1)
    k1 = dve.did(V.tensor_scalar(r32[1][:, :], r32[0][:, :], EPS, None, ALU.max))
    dve.need(k1)
    k1 = dve.did(V.reciprocal(r32[2][:, :], r32[1][:, :]))
    dve.need(k1)
    for n in range(2):
        k_w = dve.did(V.tensor_tensor(kw_[n][:, :], kw_[n][:, :], r32[2][:, :], ALU.mult))

    a_sc = Arrivals(nc, "a_sc")
    pool.need(k_idx, k_zero, *xs_done)
    for t in range(NT):
        for n in range(2):
            k_sc = a_sc.add(G.indirect_dma_start(
                rows_in, bass.IndirectOffsetOnAxis(ap=idx[n][:, t:t + 1], axis=0), xs[:, t, :], None,
                bounds_check=ROWS - 1, oob_is_err=False))

    a_xe = [Arrivals(nc, f"a_xe{i}") for i in range(2)]
    a_eo = [Arrivals(nc, f"a_eo{i}") for i in range(2)]
    xe_ready, xe_free, xeT_ready, xeT_free = {}, {}, {}, {}
    tb, tb_free, nt = [misc, bank[2]], [misc_free[0], bO_free[0]], [0]

    def load_rows(e):
        i = e % 2
        sp.need(k_sc, xe_free.get(e - 2), st["st_done"][NB - 1])
        xe_ready[e] = a_xe[i].add(nc.sync.dma_start(
            xe[i], rows_in[CAP * e:CAP * e + CAP, :].rearrange("(t p) d -> p t d", p=128)))

    def turn_rows(e):
        i = e % 2
        pe.need(xe_ready[e])
        for a, n in ((0, 4), (4, 4), (8, 2)):
            s = nt[0] % 2
            nt[0] += 1
            pe.need(tb_free[s])
            for t in range(n):
                ins = M.transpose(tb[s][:, 128 * t:128 * t + 128], xe[i][:, a + t, :], identf[:, :])
            k = pe.did(ins)
            act.need(k, xeT_free.get(e - 2))
            tb_free[s] = act.did(S.copy(xeT[i][:, 128 * a:128 * (a + n)], tb[s][:, 0:128 * n]))
        xe_free[e] = k
        xeT_ready[e] = tb_free[s]

    pg = [[pS[0][:, 0:512], pS[0][:, 512:1024]], [pS[1][:, 0:512], pS[1][:, 512:1024]]]
    pg_free = [pS_free[0], pS_free[1]]
    sg_free, hT_free, hT_ready = [None, None], [None, None], {}
    po, po_free = [bank[0], bank[1]], [bST_free[0], bST_free[1]]
    eo_free = [None, None]
    nf = [0]

    def hidden(n, e, c):
        i, w = e % 2, 512 if c < 2 else 256
        W = wx[e % NWS]
        pe.need(wx_ready[e], xeT_ready[e])
        for f in range(4):
            s = nf[0] % 2
            nf[0] += 1
            pe.need(pg_free[s])
            r = xeT[i][:, 512 * c:512 * c + w]
            M.matmul(pg[s][0][:, 0:w], W[:, 0, 128 * f:128 * f + 128], r, start=True, stop=True)
            k = pe.did(M.matmul(pg[s][1][:, 0:w], W[:, 1, 128 * f:128 * f + 128], r, start=True, stop=True))
            act.need(k, sg_free[s])
            k2 = act.did(S.activation(sg[s][:, 0:w], pg[s][1][:, 0:w], ACT.Silu))
            dve.need(k2, hT_free[n % 2])
            sg_free[s] = pg_free[s] = dve.did(V.tensor_tensor(hT[n % 2][f][:, 0:w], pg[s][0][:, 0:w],
                                                              sg[s][:, 0:w], ALU.mult))
        if c == 2:
            xeT_free[e] = k
        hT_ready[n] = pg_free[s]

    def outward(n, e, c):
        i, m = n % 2, 4 if c < 2 else 2
        W = wx[e % NWS][:, 2, :].rearrange("p (f d) -> p f d", f=4)
        pe.need(hT_ready[n], po_free[i])
        for t in range(m):
            for f in range(4):
                ins = M.matmul(po[i][:, 128 * t:128 * t + 128], hT[i][f][:, 128 * t:128 * t + 128], W[:, f, :],
                               start=(f == 0), stop=(f == 3))
        k = hT_free[i] = pe.did(ins)
        dve.need(k, eo_free[i])
        k2 = po_free[i] = dve.did(V.tensor_copy(eo[i][:, 0:128 * m], po[i][:, 0:128 * m]))
        sp.need(k2)
        r = CAP * e + 512 * c
        eo_free[i] = a_eo[i].add(nc.sync.dma_start(
            rows_out[r:r + 128 * m, :].rearrange("(t p) d -> p t d", p=128),
            eo[i][:, 0:128 * m].rearrange("p (t d) -> p t d", d=128)))
        if c == 2 and e + NWS < E:
            load_expert(e + NWS, k)
        st["hid_done"] = k

    load_rows(0)
    load_rows(1)
    turn_rows(0)
    parts = [(e, c) for e in range(E) for c in range(3)]
    for n, (e, c) in enumerate(parts):
        hidden(n, e, c)
        if c == 0 and e + 1 < E:
            turn_rows(e + 1)
            if e + 2 < E:
                load_rows(e + 2)
        if n:
            outward(n - 1, *parts[n - 1])
    outward(len(parts) - 1, *parts[-1])

    NGR = 8
    gat = [[ar1[:, 4096 + 256 * i + 128 * n:4224 + 256 * i + 128 * n] for n in range(2)] for i in range(NGR)]
    a_ga = [Arrivals(nc, f"a_ga{i}") for i in range(NGR)]
    gat_free = [xeT_free[E - 1]] * NGR
    pool.need(*eo_free, k_zrow)
    for t in range(NT):
        i = t % NGR
        pool.need(gat_free[i])
        for n in range(2):
            w = a_ga[i].add(G.indirect_dma_start(gat[i][n], None, rows_out,
                                                 bass.IndirectOffsetOnAxis(ap=idx[n][:, t:t + 1], axis=0)))
        dve.need(w, k_w)
        k = dve.did(V.scalar_tensor_tensor(x[:, t, :], gat[i][0], kw_[0][:, t:t + 1], x[:, t, :], ALU.mult, ALU.add))
        dve.need(k)
        gat_free[i] = k = dve.did(V.scalar_tensor_tensor(x[:, t, :], gat[i][1], kw_[1][:, t:t + 1], x[:, t, :],
                                                         ALU.mult, ALU.add))
        st["x_done"][t // 4] = k

    if upto == 2:
        return finish(nc, sp, out, x, st["x_done"])

    wq1 = ar2[0:64, 0:2048].rearrange("p (h d) -> p h d", h=16)
    wk1 = ar2[0:64, 2048:4096].rearrange("p (h d) -> p h d", h=16)
    mh = ar2[:, 4096:6144].rearrange("p (h d) -> p h d", h=16)
    zT = ar2[:, 0:4096].rearrange("p (r n) -> p r n", r=8)
    v1 = [ar1[:, 4096 * i:4096 * i + 4096].rearrange("p (k f) -> p k f", k=4) for i in range(2)]
    yT = [[ar1[:, 8192 + 1024 * i + 512 * a:8704 + 1024 * i + 512 * a] for a in range(2)] for i in range(2)]
    NP, NQ = 8, 4
    pr_ = [ar1[:, 10240 + 512 * i:10752 + 512 * i] for i in range(NP)]
    pT = [ar1[:, 14336 + 512 * i:14848 + 512 * i] for i in range(NQ)]

    old1 = [gat_free[t % NGR] for t in range(NT)]
    a_w1 = Arrivals(nc, "a_w1")
    sp.need(hT_free[(len(parts) - 1) % 2])
    nc_k = a_w1.add(nc.sync.dma_start(wq1, T["wq1"]))
    nc_k = a_w1.add(nc.sync.dma_start(wk1, T["wk1"]))
    mfree = misc_free[0] = tb_free[0]
    bank2_free = [tb_free[1]]
    k_mh = None
    for a in range(4):
        pe.need(nc_k, misc_free[0])
        for q in range(4):
            h = 4 * a + q
            ins = M.matmul(misc[:, 128 * q:128 * q + 128], wq1[:, h, :], wk1[:, h, :], start=True, stop=True)
        k = pe.did(ins)
        k_wqk = k
        act.need(k)
        k_mh = misc_free[0] = act.did(S.mul(ar2[:, 4096 + 512 * a:4608 + 512 * a], misc[:, :], 0.125))

    xT1 = xnT
    xT1_free, v1_free = [xT_free[0], xT_free[1]], [None, None]
    xT1_ready, v1_ready = {}, {}
    st["x_done1"] = [None] * NB

    def turn_batch(b, dst, free):
        k = ln_stats(b, st["x_done"][b])
        k = ln_apply(b, k)
        yield k
        k = transpose_tiles([xn[:, t, :] for t in range(4)], k)
        xn_free[0] = k
        act.need(k, free)
        misc_free[0] = k = act.did(S.copy(dst, misc[:, :]))
        yield k

    def prep1(b):
        i = b % 2
        part = turn_batch(b, xT1[i][:, :], xT1_free[i])
        next(part)
        yield
        xT1_ready[b] = k = next(part)
        yield
        for t in range(4):
            for n in range(2):
                pe.need(k, misc_free[0], got_w1)
                k1 = pe.did(M.matmul(misc[:, :], xT1[i][:, 128 * t:128 * t + 128], wv1[:, 512 * n:512 * n + 512],
                                     start=True, stop=True))
                e_ = act if n else dve
                e_.need(k1, v1_free[i], *old1)
                o = v1[i][:, t, 512 * n:512 * n + 512]
                misc_free[0] = e_.did(S.copy(o, misc[:, :]) if n else V.tensor_copy(o, misc[:, :]))
                v1_ready.setdefault(b, []).append(misc_free[0])
            yield

    y_ready, y_free, ny = {}, [None, None], [0]

    def heads(b, r):
        i = (8 * b + r) % 2
        for a in range(2):
            pe.need(xT1_ready[b], misc_free[0], k_mh)
            k = pe.did(M.matmul(misc[:, :], mh[:, 2 * r + a, :], xT1[b % 2][:, :], start=True, stop=True))
            dve.need(k, y_free[i], *old1)
            misc_free[0] = dve.did(V.tensor_copy(yT[i][a], misc[:, :]))
        y_ready[(b, r)] = misc_free[0]

    p_ready, p_free, q_ready, q_free = {}, [None] * NP, {}, [None] * NQ
    s1_free = [pg_free[0], pg_free[1]]
    tt_free = [po_free[0], po_free[1]]
    o1_free = [bank2_free[0]]
    s1_pe = [None, None]

    def weights(u, b, r, qb):
        s, w = u % 2, 128 * (qb + 1)
        i = (8 * b + r) % 2
        pe.need(y_ready[(b, r)], s1_free[s], *([st["hid_done"]] if u < 2 else []), c_mask)
        ks = []
        for a in range(2):
            o = pS[s][:, 512 * a:512 * a + w]
            M.matmul(o, yT[i][a][:, 128 * qb:128 * qb + 128], xT1[b % 2][:, 0:w], start=True, stop=False)
            ks.append(pe.did(M.matmul(o[:, w - 128:w], identb[:, :], maskb[:, :], start=False, stop=True)))
        if qb == 3:
            y_free[i] = k_ = ks[1]
            if r == 7:
                xT1_free[b % 2] = k_
        for a in range(2):
            o = pS[s][:, 512 * a:512 * a + w]
            c = 2 * (u % 4) + a
            pi = (2 * u + a) % NP
            dve.need(ks[a])
            k = dve.did(V.tensor_reduce(nm1[:, c:c + 1], o, AX.X, ALU.max, negate=True))
            act.need(k, p_free[pi])
            k = act.did(S.activation(pr_[pi][:, 0:w], o, ACT.Exp, bias=nm1[:, c:c + 1], accum_out=den1[:, c:c + 1]))
            s1_free[s] = k
            dve.need(k)
            k = dve.did(V.reciprocal(rd1[:, c:c + 1], den1[:, c:c + 1]))
            pool.need(k)
            p_ready[(u, a)] = pool.did(G.tensor_scalar(pr_[pi][:, 0:w], pr_[pi][:, 0:w], rd1[:, c:c + 1], 1.0,
                                                       ALU.mult, ALU.mult))

    tbank = [bank[0], bank[1]]

    def turn(u, qb):
        w = 128 * (qb + 1)
        for a in range(2):
            pi, qi = (2 * u + a) % NP, (2 * u + a) % NQ
            pe.need(p_ready.pop((u, a)), tt_free[a])
            for t in range(qb + 1):
                ins = M.transpose(tbank[a][:, 128 * t:128 * t + 128], pr_[pi][:, 128 * t:128 * t + 128], identf[:, :])
            k = p_free[pi] = pe.did(ins)
            e_ = dve if a else act
            e_.need(k, q_free[qi])
            o = pT[qi][:, 0:w]
            tt_free[a] = q_ready[(u, a)] = e_.did(V.tensor_copy(o, tbank[a][:, 0:w]) if a
                                                  else S.copy(o, tbank[a][:, 0:w]))

    z_free = [None]

    def values(u, b, r, qb):
        pe.need(q_ready.pop((u, 0)), q_ready.pop((u, 1)), *v1_ready[b])
        if qb == 0:
            pe.need(o1_free[0])
        for t in range(qb + 1):
            for a in range(2):
                h = 2 * r + a
                ins = M.matmul(bank[2][64 * a:64 * a + 64, 128 * qb:128 * qb + 128], v1[b % 2][:, t, 64 * h:64 * h + 64],
                               pT[(2 * u + a) % NQ][:, 128 * t:128 * t + 128], start=(t == 0), stop=(t == qb))
        k = pe.did(ins)
        for a in range(2):
            q_free[(2 * u + a) % NQ] = k
        if qb == 3:
            act.need(k, z_free[0], k_wqk)
            o1_free[0] = act.did(S.copy(zT[:, r, :], bank[2][:, :]))
            if r == 7:
                v1_free[b % 2] = k

    def project1(b):
        pe.need(o1_free[0], misc_free[0], got_w1)
        for t in range(4):
            for r in range(8):
                ins = M.matmul(misc[:, 128 * t:128 * t + 128], zT[:, r, 128 * t:128 * t + 128], wo1[:, r, :],
                               start=(r == 0), stop=(r == 7))
        k = z_free[0] = pe.did(ins)
        dve.need(k)
        xb = x[:, 4 * b:4 * b + 4, :]
        misc_free[0] = st["x_done1"][b] = dve.did(V.tensor_tensor(xb, misc[:, :].rearrange("p (t d) -> p t d", t=4),
                                                                  xb, ALU.add))

    for _ in prep1(0):
        pass
    heads(0, 0)
    units = [(b, r, qb) for b in range(NB) for r in range(8) for qb in range(4)]
    work = iter(())
    LT, LV = 2, 3
    for u in range(len(units) + LV):
        if u < len(units):
            b, r, qb = units[u]
            if r == 5 and qb == 0 and b + 1 < NB:
                work = prep1(b + 1)
            if qb % 2 == 0:
                next(work, None)
            weights(u, b, r, qb)
            if qb == 1:
                if r < 7:
                    heads(b, r + 1)
                elif b + 1 < NB:
                    for _ in work:
                        pass
                    heads(b + 1, 0)
        if 0 <= u - LT < len(units):
            turn(u - LT, units[u - LT][2])
        if 0 <= u - LV < len(units):
            values(u - LV, *units[u - LV])
            if units[u - LV][1:] == (7, 3):
                project1(units[u - LV][0])
    if upto == 3:
        return finish(nc, sp, out, x, st["x_done1"])

    st["x_done"] = st["x_done1"]
    lgp = pS[0][:, 0:256].rearrange("p (t e) -> p t e", e=E)
    xT4_done = [None] * NB
    for b in range(NB):
        part = turn_batch(b, xT4[:, 512 * b:512 * b + 512], None)
        next(part)
        k = xT4_done[b] = next(part)
        pe.need(k, s1_free[0], got_w1)
        for t in range(4):
            c = 512 * b + 128 * t
            ins = M.matmul(lgp[:, 4 * b + t, :], xT4[:, c:c + 128], rt1[:, :], start=True, stop=True)
        k = pe.did(ins)
    k_p = soft(lgp, k)
    s1_free[0] = k_p
    dve.need(k_p, got_w1)
    k = dve.did(V.tensor_scalar(rd, rp, rb1[:, 0:1], None, ALU.add))
    k = top(rd, 4, k)
    dve.need(k)
    k = dve.did(V.tensor_tensor(rq, rp, rsel, ALU.mult))
    dve.need(k)
    k = dve.did(V.tensor_reduce(r32[0][:, :], rq, AX.X, ALU.add))
    dve.need(k)
    k = dve.did(V.tensor_scalar(r32[1][:, :], r32[0][:, :], 1e-20, None, ALU.add))
    dve.need(k)
    k = dve.did(V.reciprocal(r32[2][:, :], r32[1][:, :]))
    dve.need(k)
    k_w1 = dve.did(V.tensor_tensor(rg, rq, r32[2][:, :, None].broadcast_to([128, NT, E]), ALU.mult))

    sr = [ar1[:, 768 * i:768 * i + 768] for i in range(2)]
    aa = [ar1[:, 2048 + 768 * i:2816 + 768 * i] for i in range(2)]
    aaT = [ar1[:, 4096 + 768 * i:4864 + 768 * i].rearrange("p (c n) -> p c n", c=6) for i in range(2)]
    g_free = [s1_free[0], s1_free[1]]
    h_free = [tt_free[0], tt_free[1]]
    sr_free, aa_free, aT4_free = [None, None], [None, None], [None, None]
    aa_ready, aT4_ready = {}, {}
    tr_free = [o1_free[0]]
    ar1_free = v1_free + [q_free[n] for n in range(NQ)]

    def gate(t):
        i = t % 2
        xt = xT4[:, 128 * t:128 * t + 128]
        pe.need(xT4_done[t // 4], g_free[i], h_free[i], s1_free[i])
        M.matmul(pS[i][:, 0:512], xt, gw1[:, 0:512], start=True, stop=True)
        k1 = pe.did(M.matmul(pS[i][:, 512:1024], xt, uw1[:, 0:512], start=True, stop=True))
        M.matmul(bank[i][:, 0:256], xt, gw1[:, 512:768], start=True, stop=True)
        k2 = pe.did(M.matmul(bank[i][:, 256:512], xt, uw1[:, 512:768], start=True, stop=True))
        act.need(k1, sr_free[i], *ar1_free)
        k1 = act.did(S.activation(sr[i][:, 0:512], pS[i][:, 0:512], ACT.Silu))
        act.need(k2)
        k2 = act.did(S.activation(sr[i][:, 512:768], bank[i][:, 0:256], ACT.Silu))
        dve.need(k1, aa_free[i])
        g_free[i] = k1 = dve.did(V.tensor_tensor(aa[i][:, 0:512], pS[i][:, 512:1024], sr[i][:, 0:512], ALU.mult))
        dve.need(k2)
        h_free[i] = sr_free[i] = k2 = dve.did(V.tensor_tensor(aa[i][:, 512:768], bank[i][:, 256:512],
                                                              sr[i][:, 512:768], ALU.mult))
        pool.need(k1, k_w1)
        av = aa[i][:, 0:512].rearrange("p (e n) -> p e n", e=E)
        k1 = pool.did(G.tensor_tensor(av, av, rg[:, t, :][:, :, None].broadcast_to([128, E, 64]), ALU.mult))
        aa_ready[t] = (k1, k2)

    def turn4(t):
        i = t % 2
        pe.need(*aa_ready.pop(t), tr_free[0], misc_free[0])
        for c in range(4):
            ins = M.transpose(bank[2][:, 128 * c:128 * c + 128], aa[i][:, 128 * c:128 * c + 128], identf[:, :])
        k1 = pe.did(ins)
        for c in range(2):
            ins = M.transpose(misc[:, 128 * c:128 * c + 128], aa[i][:, 512 + 128 * c:640 + 128 * c], identf[:, :])
        k2 = aa_free[i] = pe.did(ins)
        act.need(k1, aT4_free[i])
        tr_free[0] = k1 = act.did(S.copy(aaT[i][:, 0:4, :], bank[2][:, :].rearrange("p (c n) -> p c n", c=4)))
        act.need(k2)
        k2 = act.did(S.copy(aaT[i][:, 4:6, :], misc[:, 0:256].rearrange("p (c n) -> p c n", c=2)))
        misc_free[0] = k2
        aT4_ready[t] = (k1, k2)

    def down(t):
        i = t % 2
        pe.need(*aT4_ready.pop(t), misc_free[0])
        for c in range(6):
            ins = M.matmul(misc[:, 256:384], aaT[i][:, c, :], dw1[:, c, :], start=(c == 0), stop=(c == 5))
        k = aT4_free[i] = pe.did(ins)
        dve.need(k)
        misc_free[0] = k = dve.did(V.tensor_tensor(x[:, t, :], misc[:, 256:384], x[:, t, :], ALU.add))
        if t % 4 == 3:
            b = t // 4
            sp.need(k)
            done.append(a_out[b].add(nc.sync.dma_start(oview[:, 4 * b:4 * b + 4, :], x[:, 4 * b:4 * b + 4, :])))

    oview = out.rearrange("(t p) d -> p t d", p=128)
    a_out = [Arrivals(nc, f"a_out{b}") for b in range(NB)]
    done = []
    for t in range(NT + 2):
        if t < NT:
            gate(t)
        if 0 <= t - 1 < NT:
            turn4(t - 1)
        if 0 <= t - 2 < NT:
            down(t - 2)
    sp.need(*done)


def finish(nc, sp, out, x, done):
    o = out.rearrange("(t p) d -> p t d", p=128)
    a = Arrivals(nc, "a_out")
    for b in range(NB):
        sp.need(done[b])
        w = a.add(nc.sync.dma_start(o[:, 4 * b:4 * b + 4, :], x[:, 4 * b:4 * b + 4, :]))
    sp.need(w)


def layout(inputs):
    f = {k: np.asarray(v) for k, v in inputs.items()}
    c = np.ascontiguousarray
    r = {}
    r["x"] = c(f["L0_attn_x"].reshape(4096, 128))
    r["W0"] = c(np.stack([f["L0_attn_W" + n].T for n in "qkvp"], axis=1))
    r["bqk"] = c(np.stack([f["L0_attn_bq"], f["L0_attn_bk"]], axis=1))
    r["bvp"] = c(np.broadcast_to(np.stack([f["L0_attn_bv"], f["L0_attn_bp"]])[None], (128, 2, 128)))
    r["lam"] = c(np.stack([f["L0_attn_lambda_" + n][:, 0, :] for n in ("q1", "k1", "q2", "k2")], axis=1))
    r["rt0"] = c(f["L0_ffn_router_weight"].T)
    r["wx"] = c(np.stack([f["L0_ffn_ff_pre_act_weight"].transpose(0, 2, 1), f["L0_ffn_gate_weight"].transpose(0, 2, 1),
                          f["L0_ffn_ff_post_act_weight"].reshape(8, 128, 4, 128).transpose(0, 3, 2, 1)
                          .reshape(8, 128, 512)], axis=2))
    r["wq1"] = c(f["L1_attn_W_Q"].transpose(1, 0, 2))
    r["wk1"] = c(f["L1_attn_W_K"].transpose(1, 0, 2))
    r["wv1"] = c(f["L1_attn_W_V"].reshape(1024, 128).T)
    r["wo1"] = c(f["L1_attn_W_O"].T.reshape(8, 128, 128).transpose(1, 0, 2))
    for n, m in (("gw1", "gate_w"), ("uw1", "up_w")):
        r[n] = c(np.concatenate([f["L1_ffn_" + m].transpose(1, 0, 2).reshape(128, 512), f["L1_ffn_s_" + m]], axis=1))
    r["dw1"] = c(np.concatenate([f["L1_ffn_down_w"].reshape(512, 128), f["L1_ffn_s_down_w"]])
                 .reshape(6, 128, 128).transpose(1, 0, 2))
    r["rt1"] = c(f["L1_ffn_router_w"])
    r["rb1"] = c(np.broadcast_to(f["L1_ffn_router_bias"], (128, 1)))
    return r


def kernel(**inputs):
    from concourse import bacc
    from concourse.bass_utils import run_bass_kernel_spmd

    arrays = layout(inputs)
    nc = bacc.Bacc("TRN2", target_bir_lowering=False, num_devices=1)
    T = {n: nc.dram_tensor("in_" + n, a.shape, mybir.dt.from_np(a.dtype), kind="ExternalInput").ap()
         for n, a in arrays.items()}
    out = nc.dram_tensor("out", (4096, 128), F32, kind="ExternalOutput").ap()
    program(nc, T, out)
    r = run_bass_kernel_spmd(nc, [{"in_" + n: a for n, a in arrays.items()}], core_ids=[0])
    return r.results[0]["out"].reshape(8, 512, 128)
```

```python
from itertools import chain

import numpy as np
import concourse.bass as bass
from concourse import mybir
from concourse.alu_op_type import AluOpType as ALU

F32 = mybir.dt.float32
BF16 = mybir.dt.bfloat16
I32 = mybir.dt.int32
U32 = mybir.dt.uint32
ACT = mybir.ActivationFunctionType
AX = mybir.AxisListType

NB = 8
NT = 32
E = 8
CAP = 1280
LIST = 4096
CH = 256
NCH = 39
ROWS = NCH * CH
EPS = 1.1920929e-07
LN_EPS = 1e-5
NEG = -1e10


class Eng:

    def __init__(self, nc, eng, name):
        self.e = eng
        self.sem = nc.alloc_semaphore("done_" + name)
        self.n = 0
        self.seen = {}

    def did(self, ins):
        self.n += 1
        ins.then_inc(self.sem, 1)
        return (self.sem, self.n)

    def need(self, *marks):
        for m in marks:
            if m is None:
                continue
            sem, val = m
            key = sem.name if hasattr(sem, "name") else id(sem)
            if self.seen.get(key, 0) < val:
                self.e.wait_ge(sem, val)
                self.seen[key] = val


class Arrivals:

    def __init__(self, nc, name):
        self.sem = nc.alloc_semaphore(name)
        self.n = 0

    def add(self, ins):
        self.n += 16
        ins.then_inc(self.sem, 16)
        return (self.sem, self.n)


def program(nc, T, out):
    pe, dve, act, pool, sp = (Eng(nc, e, n) for e, n in (
        (nc.tensor, "pe"), (nc.vector, "dve"), (nc.scalar, "act"), (nc.gpsimd, "pool"), (nc.sync, "sp")))
    V, S, G, M = nc.vector, nc.scalar, nc.gpsimd, nc.tensor

    def sb(name, shape, dt=F32):
        return nc.alloc_sbuf_tensor(name, shape, dt)

    def dram(name, shape, dt=F32):
        return nc.dram_tensor(name, shape, dt, kind="Internal").ap()

    x = sb("x", [128, NT, 128])
    identf = sb("identf", [128, 128])
    identb = sb("identb", [128, 128], BF16)
    onesf = sb("onesf", [128, 128])
    ustrict = sb("ustrict", [128, 128])
    maskf = sb("maskf", [128, 512])
    mhalf = sb("mhalf", [128, 32])
    w0 = sb("w0", [128, 4, 128])
    bqk = sb("bqk", [128, 2])
    bvp = sb("bvp", [128, 2, 128])
    lam = sb("lam", [8, 4, 8])
    lamw = sb("lamw", [8, 32])
    nlv = sb("nlv", [128, 1])
    warm = sb("warm", [128, 4])
    ar1 = sb("ar1", [128, 16384])
    ar2 = sb("ar2", [128, 8192])
    xn = sb("xn", [128, 4, 128])
    xnT = [sb(f"xnT{i}", [128, 512]) for i in range(2)]
    ln_sets = [[sb(f"ln_{n}{i}", [128, *d]) for n, d in (("st", (4, 6)), ("mv", (4, 2)), ("ve", (4,)), ("rs", (4,)))]
               for i in range(2)]

    bank = [nc.alloc_psum_tensor(f"bank{i}", [128, 512], F32) for i in range(4)]
    pS = [nc.alloc_psum_tensor(f"pS{i}", [128, 1024], F32) for i in range(2)]
    misc = bank[3]
    misc_free = [None]

    xin = T["x"].rearrange("(t p) d -> p t d", p=128)
    ax = [Arrivals(nc, f"ax{b}") for b in range(NB)]
    aw = Arrivals(nc, "aw")
    def whole(t):
        return t[tuple(slice(None) for _ in t.shape)]

    got, late = {}, []

    def load(key, queue, sem, dst, src):
        got[key] = sem.add(queue.dma_start(dst, src))

    load("x0", nc.sync, ax[0], x[:, 0:4, :], xin[:, 0:4, :])
    for dst, src in ((w0, "W0"), (bqk, "bqk"), (bvp, "bvp"), (lam, "lam")):
        load("w0", nc.sync, aw, whole(dst), T[src])
    load("x1", nc.sync, ax[1], x[:, 4:8, :], xin[:, 4:8, :])
    late += [(f"x{b}", nc.sync, ax[b], x[:, 4 * b:4 * b + 4, :], xin[:, 4 * b:4 * b + 4, :]) for b in range(2, NB)]

    c0 = pool.did(G.memset(identf[:, :], 0.0))
    c1 = pool.did(G.memset(identb[:, :], 0.0))
    c2 = pool.did(G.memset(onesf[:, :], 1.0))
    c3 = pool.did(G.memset(mhalf[:, :], -0.5))
    pool.need(c0)
    G_id = pool.did(G.affine_select(out=identf[:, :], in_=identf[:, :], compare_op=ALU.not_equal, fill=1.0,
                                    base=0, pattern=[[-1, 128]], channel_multiplier=1))
    pool.need(c1)
    G_idb = pool.did(G.affine_select(out=identb[:, :], in_=identb[:, :], compare_op=ALU.not_equal, fill=1.0,
                                     base=0, pattern=[[-1, 128]], channel_multiplier=1))

    rt0 = sb("rt0", [128, E])
    cst = sb("cst", [128, 174])
    late += [("rt", nc.sync, Arrivals(nc, "a_rt"), rt0[:, :], T["rt0"]),
             ("cst", nc.sync, Arrivals(nc, "a_cst"), cst[:, :], T["cst"])]
    c_pass, c_row, c_steps, c_p, c_list, c_seg8 = (cst[:, a:b] for a, b in (
        (0, 39), (39, 117), (117, 133), (133, 134), (134, 142), (142, 174)))
    rr = sb("rr", [128, 11, NT, E])
    rd, rp, rsrt, rg, rq, rpx, rsel, rw, rpos, rf0, rf1 = (rr[:, n] for n in range(11))
    re_ = sb("re", [128, 5, E, NT])
    ewm, eg, eq, epos, etmp = (re_[:, n] for n in range(5))
    rsum = sb("rsum", [128, NT + 1, E])
    escan_ = sb("escan", [128, 256])
    escan = escan_[:, :]
    rs8 = sb("rs8", [128, 48])
    r32 = [sb(f"r32_{n}", [128, NT]) for n in range(4)]
    kw_ = [sb(f"kw{n}", [128, NT]) for n in range(2)]
    sidx = [sb(f"sidx{n}", [128, NT], U32) for n in range(2)]
    idx = [sb(f"idx{n}", [128, NT], U32) for n in range(2)]
    widx, ridx = sb("widx", [128, NCH], U32), sb("ridx", [128, 2 * NCH], U32)
    segm = sb("segm", [128, 256])
    xs = [sb(f"xs{i}", [128, 4, 128]) for i in range(2)]
    xsT = sb("xsT", [128, 512])
    zrow = sb("zrow", [128, 512])
    wv1, wo1 = sb("wv1", [128, 1024]), sb("wo1", [128, 8, 128])
    gw1, uw1, dw1 = sb("gw1", [128, 768]), sb("uw1", [128, 768]), sb("dw1", [128, 6, 128])
    rt1, rb1 = sb("rt1", [128, E]), sb("rb1", [128, 1])
    nm1, den1, rd1 = (sb(n, [128, 8]) for n in ("nm1", "den1", "rd1"))
    xT4 = sb("xT4", [128, 4096])
    wq1 = xT4[0:64, 0:2048].rearrange("p (h d) -> p h d", h=16)
    wk1 = xT4[0:64, 2048:4096].rearrange("p (h d) -> p h d", h=16)
    a_wl1 = Arrivals(nc, "a_wl1")
    for t_, n in ((wv1, "wv1"), (wo1, "wo1"), (gw1, "gw1"), (uw1, "uw1"), (dw1, "dw1"), (rt1, "rt1"), (rb1, "rb1")):
        late.append(("w1", nc.sync, a_wl1, whole(t_), T[n]))
    a_wqk = Arrivals(nc, "a_wqk")
    for t_, n in ((wq1, "wq1"), (wk1, "wk1")):
        late.append(("wqk", nc.sync, a_wqk, t_, T[n]))
    rows_in = dram("rows_in", [E * LIST, 128])
    rows_out = dram("rows_out", [ROWS + 1, 128])
    xn_free = [None]

    def ln_stats(b, ready, i=0):
        stt, mv, ve, rstd = ln_sets[i]
        dve.need(ready)
        for t in range(4):
            k = dve.did(V.bn_stats(stt[:, t, :], x[:, 4 * b + t, :]))
        dve.need(k)
        for t in range(4):
            k = dve.did(V.bn_aggr(mv[:, t, :], stt[:, t, :]))
        dve.need(k)
        k = dve.did(V.tensor_scalar(ve[:, :], mv[:, :, 1], LN_EPS, None, ALU.add))
        pool.need(k, c3)
        return pool.did(G.tensor_tensor(rstd[:, :], ve[:, :], mhalf[:, 0:4], ALU.pow))

    def ln_apply(b, k_rstd, dst, free, i=0):
        mv, rstd = ln_sets[i][1], ln_sets[i][3]
        dve.need(k_rstd, free)
        for t in range(4):
            k = dve.did(V.tensor_scalar(dst[:, t, :], x[:, 4 * b + t, :], mv[:, t, 0:1], rstd[:, t:t + 1],
                                        ALU.subtract, ALU.mult))
        return k

    def transpose_tiles(srcs, ready):
        pe.need(ready, misc_free[0], G_id)
        for t, s in enumerate(srcs):
            ins = M.transpose(misc[:, 128 * t:128 * t + 128], s, identf[:, :])
        return pe.did(ins)

    ab = ar1[:, :].bitcast(BF16).rearrange("p (r s h n) -> p r s h n", r=2, s=2, h=16)
    qst = [ab[:, i, 0] for i in range(2)]
    kst = [ab[:, i, 1] for i in range(2)]
    vst = [ar2[:, 2048 * i:2048 * i + 2048].rearrange("p (k h c) -> p k h c", k=4, h=16) for i in range(2)]
    NPT = 8
    pt = [ar2[:, 4096 + 512 * i:4096 + 512 * i + 512] for i in range(NPT)]
    qkp = [sb(f"qkp{i}", [128, 3, 512], BF16) for i in range(2)]
    res = sb("res", [128, 512])
    mx = [sb(f"mx{i}", [128, 16]) for i in range(2)]
    mr = sb("mr", [128, 4, 4])
    mp = [sb(f"mp{i}", [128, 4, 12], BF16) for i in range(2)]
    mT = [sb(f"mT{i}", [12, 512], BF16) for i in range(2)]
    oT = sb("oT", [128, 512])
    rden = sb("rden", [128, 4, 4])
    att = [sb(f"att{i}", [128, 4, 128]) for i in range(2)]
    aT = sb("aT", [128, 512])
    dq = [dram(f"dq{i}", [16, 24, 512], BF16) for i in range(2)]
    dk = [dram(f"dk{i}", [16, 40, 512], BF16) for i in range(2)]
    dm = [dram(f"dm{i}", [12, 512], BF16) for i in range(2)]
    a_dq, a_dk, a_dm = ([Arrivals(nc, f"a_{n}{i}") for i in range(2)] for n in ("dq", "dk", "dm"))
    a_qs, a_ks, a_ms = ([Arrivals(nc, f"a_{n}{i}") for i in range(2)] for n in ("qs", "ks", "ms"))

    flat_st = ar1[:, :].rearrange("p (r s f) -> p r s f", r=2, s=2)
    z_stack, z_v = [], []
    for i in range(2):
        a_zs = Arrivals(nc, f"a_zs{i}")
        a_zs.add(nc.scalar.dma_start(flat_st[72:96, i, 0], T["stack"][0:24]))
        z_stack.append((a_zs.add(nc.scalar.dma_start(flat_st[72:99, i, 1], T["stack"])),))
    st = {"xnT_free": [None, None], "qkp_free": [None, None], "res_free": None, "v_ready": [None] * NB,
          "stack_ready": [None] * NB, "st_done": [None] * NB, "s_done": [None] * NB, "pv_done": [None] * NB,
          "x_done": [None] * NB}

    def prep(b):
        i = b % 2
        k = ln_stats(b, got[f"x{b}"])
        yield
        k_xn = k = ln_apply(b, k, xn, xn_free[0])
        yield
        k = transpose_tiles([xn[:, t, :] for t in range(4)], k_xn)
        xn_free[0] = k
        pool.need(k_xn, got["w0"])
        st["xb%d" % b] = pool.did(G.tensor_tensor(
            x[:, 4 * b:4 * b + 4, :], x[:, 4 * b:4 * b + 4, :],
            bvp[:, 1, :][:, None, :].broadcast_to([128, 4, 128]), ALU.add))
        act.need(k, st["xnT_free"][i])
        k_T = act.did(S.copy(xnT[i][:, :], misc[:, :]))
        misc_free[0] = k_T
        yield
        own = b == 0
        kq, kqueue = (act, nc.scalar) if own else (sp, nc.sync)
        for n in range(2):
            o, rest = (bank[0], oT) if own and n else (misc, res)
            pe.need(k_T, bST_free[0] if own and n else misc_free[0], got["w0"])
            k = pe.did(M.matmul(o[:, :], w0[:, n, :], xnT[i][:, :], start=True, stop=True))
            act.need(k, st["qkp_free"][n])
            k1 = act.did(S.activation(qkp[n][:, 0, :], o[:, :], ACT.Identity, bias=bqk[:, n:n + 1]))
            dve.need(k1, None if own else st["res_free"])
            k2 = dve.did(V.scalar_tensor_tensor(rest[:, :], o[:, :], bqk[:, n:n + 1], qkp[n][:, 0, :],
                                                ALU.add, ALU.subtract))
            if own and n:
                bST_free[0] = k2
            else:
                misc_free[0] = k2
            dve.need(k2)
            k3 = dve.did(V.tensor_copy(qkp[n][:, 1, :], rest[:, :]))
            dve.need(k3)
            k4 = dve.did(V.tensor_tensor(qkp[n][:, 2, :], rest[:, :], qkp[n][:, 1, :], ALU.subtract))
            if own and n:
                oT_free[0] = k4
            else:
                st["res_free"] = k4
            if n == 0:
                for a in range(3):
                    sp.need(k4 if a else k1)
                    w = a_dq[i].add(nc.sync.dma_start(dq[i][:, 8 * a:8 * a + 8, :], qkp[0][:, a, :]))
                st["qkp_free"][0] = w
                yield
                sp.need(w, *z_stack[i], st["st_done"][b - 2] if b >= 2 else None)
                for g in range(3):
                    w = a_qs[i].add(nc.sync.dma_start(qst[i][24 * g:24 * g + 24, :, :],
                                                      dq[i].rearrange("h c n -> c h n")))
                k_qs = w
            else:
                for a in (0, 3, 1, 4, 2):
                    kq.need(k4 if a % 3 else k1)
                    w = a_dk[i].add(kqueue.dma_start(dk[i][:, 8 * a:8 * a + 8, :], qkp[1][:, a % 3, :]))
                st["qkp_free"][1] = w
                yield
                kq.need(w)
                for g in range(3):
                    w = a_ks[i].add(kqueue.dma_start(kst[i][24 * g:24 * g + 24, :, :],
                                                      dk[i][:, 8 * g:8 * g + 24, :].rearrange("h c n -> c h n")))
                k_ks = w
        st["stack_ready"][b] = (k_qs, k_ks)
        pe.need(misc_free[0])
        for t in range(4):
            ins = M.matmul(misc[:, 128 * t:128 * t + 128], xnT[i][:, 128 * t:128 * t + 128], w0[:, 2, :],
                           start=True, stop=True)
        k = pe.did(ins)
        st["xnT_free"][i] = k
        dve.need(k, z_v[i], st["pv_done"][b - 2] if b >= 2 else None)
        k = dve.did(V.tensor_tensor(vst[i][:, :, :, 0:8],
                                    misc[:, :].rearrange("p (t h d) -> p t h d", t=4, h=16),
                                    bvp[:, 0, :].rearrange("p (h d) -> p h d", d=8)[:, None, :, :]
                                    .broadcast_to([128, 4, 16, 8]), ALU.add))
        misc_free[0] = k
        st["v_ready"][b] = k
        yield

    pS_free = [None, None]
    ns = [0]
    mx_free = [None, None]
    mx_ready = {}

    def scores(Gr, j, halves=(0, 1)):
        b, g = Gr // 4, Gr % 4
        h = 4 * g + j
        for half in halves:
            s = ns[0] % 2
            ns[0] += 1
            pe.need(*st["stack_ready"][b], *z_stack[b % 2], pS_free[s])
            for q in range(2):
                qb = 2 * half + q
                ins = M.matmul(pS[s][:, 512 * q:512 * q + 512], qst[b % 2][0:96, h, 128 * qb:128 * qb + 128],
                               kst[b % 2][0:96, h, :], start=True, stop=True)
            k = pe.did(ins)
            dve.need(k, mx_free[Gr % 2])
            c = 4 * j + 2 * half
            pS_free[s] = dve.did(V.tensor_reduce(mx[Gr % 2][:, c:c + 2],
                                                 pS[s][:, :].rearrange("p (a n) -> p a n", a=2),
                                                 AX.X, ALU.max, negate=True))
        mx_ready[Gr] = pS_free[s]
        if g == 3 and j == 3:
            st["s_done"][b] = k

    mp_free, mT_free, m_ready = [None, None], [None, None], {}

    def shift_parts(Gr):
        i = Gr % 2
        mv_ = mx[i][:, :].rearrange("p (j q) -> p q j", j=4)
        pool.need(mx_ready[Gr], mp_free[i])
        k = pool.did(G.tensor_copy(mp[i][:, :, 0:4], mv_))
        pool.need(k)
        k = pool.did(G.tensor_tensor(mr[:, :, :], mv_, mp[i][:, :, 0:4], ALU.subtract))
        mx_free[i] = k
        pool.need(k)
        k = pool.did(G.tensor_copy(mp[i][:, :, 4:8], mr[:, :, :]))
        pool.need(k)
        return pool.did(G.tensor_tensor(mp[i][:, :, 8:12], mr[:, :, :], mp[i][:, :, 4:8], ALU.subtract))

    def shift_rows(Gr, ready):
        b, g, i = Gr // 4, Gr % 4, Gr % 2
        pe.need(ready, misc_free[0], G_idb)
        mb = misc[:, :].bitcast(BF16)
        for q in range(4):
            ins = M.transpose(mb[0:12, 128 * q:128 * q + 128], mp[i][:, q, :], identb[:, :])
        k = pe.did(ins)
        mp_free[i] = k
        act.need(k, mT_free[i])
        k = act.did(S.copy(mT[i][:, :], mb[0:12, 0:512]))
        misc_free[0] = k
        sp.need(k, m_ready.get(Gr - 2))
        w = a_dm[i].add(nc.sync.dma_start(dm[i], mT[i][:, :]))
        mT_free[i] = w
        sp.need(w, st["st_done"][b - 2] if b >= 2 else None)
        m_ready[Gr] = a_ms[i].add(nc.sync.dma_start(qst[b % 2][96:99, 4 * g:4 * g + 4, :],
                                                    dm[i].rearrange("(a j) n -> a j n", a=3)))

    bST = [bank[0], bank[1]]
    bST_free = [None, None]
    bO, bO_free = bank[2], [None]
    pt_free = [None] * NPT
    pt_ready = {}
    nst = [0]

    def st_exp(Gr, kb, j):
        b, g = Gr // 4, Gr % 4
        h = 4 * g + j
        s = nst[0] % 2
        p = nst[0] % NPT
        nst[0] += 1
        pe.need(m_ready[Gr], bST_free[s])
        k = pe.did(M.matmul(bST[s][:, :], kst[b % 2][0:99, h, 128 * kb:128 * kb + 128], qst[b % 2][0:99, h, :],
                            start=True, stop=True))
        if (g, kb, j) == (3, 3, 3):
            st["st_done"][b] = k
        act.need(k, pt_free[p])
        bST_free[s] = act.did(S.activation(pt[p], bST[s][:, :], ACT.Exp, scale=8 ** -0.5))
        pt_ready[(Gr, kb, j)] = (p, bST_free[s])

    def pv(Gr, kb, j):
        b, g = Gr // 4, Gr % 4
        p, ready = pt_ready.pop((Gr, kb, j))
        pe.need(st["v_ready"][b], bO_free[0], ready)
        k = pt_free[p] = pe.did(M.matmul(bO[32 * j:32 * j + 32, :], vst[b % 2][:, kb, 4 * g + j, :], pt[p],
                                         start=(kb == 0), stop=(kb == 3)))
        if (kb, j) == (3, 3):
            if g == 3:
                st["pv_done"][b] = k
            st["o_done"] = k

    oT_free = [None]
    att_free = [None, None]

    def take_values():
        act.need(st["o_done"], oT_free[0])
        bO_free[0] = act.did(S.copy(oT[:, :], bO[:, :]))

    def finish_group(Gr):
        b, g = Gr // 4, Gr % 4
        k = bO_free[0]
        k = transpose_tiles([oT[:, 128 * t:128 * t + 128] for t in range(4)], k)
        oT_free[0] = k
        mvw = misc[:, :].rearrange("p (t j c) -> p t j c", t=4, j=4)
        dve.need(k)
        k = dve.did(V.reciprocal(rden[:, :, :], mvw[:, :, :, 8]))
        dve.need(k, att_free[b % 2])
        k = dve.did(V.tensor_tensor(att[b % 2][:, :, 32 * g:32 * g + 32].rearrange("p t (j d) -> p t j d", j=4),
                                    mvw[:, :, :, 0:8],
                                    rden[:, :, :, None].broadcast_to([128, 4, 4, 8]), ALU.mult))
        misc_free[0] = k
        return k

    aT_free = [None]

    def project(b, ready):
        i = b % 2
        dve.need(ready, k_nlv)
        k = dve.did(V.scalar_tensor_tensor(att[i][:, :, 0:64], att[i][:, :, 64:128], nlv[:, 0:1],
                                           att[i][:, :, 0:64], ALU.mult, ALU.add))
        yield
        k = transpose_tiles([att[i][:, t, :] for t in range(4)], k)
        att_free[i] = k
        act.need(k, aT_free[0])
        k = act.did(S.copy(aT[:, :], misc[:, :]))
        misc_free[0] = k
        yield
        pe.need(k, misc_free[0])
        for t in range(4):
            ins = M.matmul(misc[:, 128 * t:128 * t + 128], aT[:, 128 * t:128 * t + 128], w0[:, 3, :],
                           start=True, stop=True)
        k = pe.did(ins)
        aT_free[0] = k
        dve.need(k, st["xb%d" % b])
        k = dve.did(V.tensor_tensor(x[:, 4 * b:4 * b + 4, :], misc[:, :].rearrange("p (t d) -> p t d", t=4),
                                    x[:, 4 * b:4 * b + 4, :], ALU.add))
        misc_free[0] = k
        st["x_done"][b] = k
        yield

    a_sc = [Arrivals(nc, f"a_sc{i}") for i in range(2)]
    a_zero = [Arrivals(nc, f"a_zero{b}") for b in range(NB)]
    k_clear = [None] * NB

    def clear(b, half):
        sp.need(k_zero)
        rows = rows_in.rearrange("(e n) d -> e n d", e=E)[4 * half:4 * half + 4, 512 * b:512 * b + 512, :]
        k_clear[b] = a_zero[b].add(nc.sync.dma_start(rows.rearrange("e (p r) d -> p e (r d)", p=128),
                                                     zrow[:, None, :].broadcast_to([128, 4, 512])))

    sc_done, xsT_free = [None] * NB, [None]
    k_sel = [None] * NB

    def over(a, b):
        return a[:, 4 * b:4 * b + 4, None].broadcast_to([128, 4, E])

    def logits(b, ready, xT, w):
        B = slice(4 * b, 4 * b + 4)
        pe.need(ready, got["rt"], got["w1"], misc_free[0])
        for t in range(4):
            ins = M.matmul(misc[:, 8 * t:8 * t + 8], xT[:, 128 * t:128 * t + 128], w[:, :], start=True, stop=True)
        k_pe = pe.did(ins)
        lg = misc[:, 0:32].rearrange("p (t e) -> p t e", e=E)
        dve.need(k_pe)
        k = dve.did(V.tensor_reduce(r32[0][:, B], lg, AX.X, ALU.max))
        dve.need(k)
        k = misc_free[0] = dve.did(V.tensor_tensor(rd[:, B, :], lg, over(r32[0], b), ALU.subtract))
        act.need(k)
        return k_pe, act.did(S.activation(rd[:, B, :], rd[:, B, :], ACT.Exp))

    def likely(b, ready):
        B = slice(4 * b, 4 * b + 4)
        yield
        dve.need(ready)
        k = dve.did(V.tensor_reduce(r32[1][:, B], rd[:, B, :], AX.X, ALU.add))
        dve.need(k)
        k = dve.did(V.reciprocal(r32[2][:, B], r32[1][:, B]))
        dve.need(k)
        k = dve.did(V.tensor_tensor(rp[:, B, :], rd[:, B, :], over(r32[2], b), ALU.mult))
        dve.need(k)

    def flat(a, b):
        return a[:, 4 * b:4 * b + 4, :].rearrange("p t e -> p (t e)")

    def chosen(b, pr, K):
        B = slice(4 * b, 4 * b + 4)
        for t in range(4 * b, 4 * b + 4):
            k = dve.did(V.max(rsrt[:, t, :], pr[:, t, :]))
        yield
        dve.need(k, got["cst"])
        last = rsrt[:, B, K - 1:K].broadcast_to([128, 4, E])
        k = dve.did(V.tensor_tensor(rg[:, B, :], pr[:, B, :], last, ALU.is_gt))
        k1 = dve.did(V.tensor_tensor(rq[:, B, :], pr[:, B, :], last, ALU.is_equal))
        dve.need(k)
        k2 = dve.did(V.tensor_reduce(r32[3][:, B], rg[:, B, :], AX.X, ALU.add))
        dve.need(k1)
        k = dve.did(V.tensor_tensor_scan(flat(rpx, b), c_seg8, flat(rq, b), 0.0, ALU.mult, ALU.add))
        dve.need(k, k2)
        k = dve.did(V.tensor_tensor(rpx[:, B, :], rpx[:, B, :], over(r32[3], b), ALU.add))
        dve.need(k)
        k = dve.did(V.scalar_tensor_tensor(rq[:, B, :], rpx[:, B, :], K + 0.5, rq[:, B, :], ALU.is_lt, ALU.mult))
        dve.need(k)
        return dve.did(V.tensor_tensor(rsel[:, B, :], rg[:, B, :], rq[:, B, :], ALU.add))

    def route(b):
        i, B = b % 2, slice(4 * b, 4 * b + 4)
        wide = [128, 4, E]

        k = ln_stats(b, st["x_done"][b], 1)
        yield
        k_xs = k = ln_apply(b, k, xs[i], sc_done[b - 2] if b >= 2 else None, 1)
        yield
        k = transpose_tiles([xs[i][:, t, :] for t in range(4)], k)
        act.need(k, xsT_free[0])
        k = misc_free[0] = act.did(S.copy(xsT[:, :], misc[:, :]))
        yield
        k_lg = logits(b, k, xsT, rt0)
        xsT_free[0] = k_lg[0]
        yield from likely(b, k_lg[1])
        k = yield from chosen(b, rp, 2)
        k_sel[b] = k
        for t in range(4 * b, 4 * b + 4):
            dve.need(k)
            k = dve.did(V.tensor_tensor(rsum[:, t + 1, :], rsum[:, t, :], rsel[:, t, :], ALU.add))
        k_sum = k
        yield
        yield
        pe.need(k_sum, k_sel[b], misc_free[0], c_us, c2)
        M.matmul(misc[:, 0:32], ustrict[:, :], flat(rsel, b), start=True, stop=False)
        k_pl = pe.did(M.matmul(misc[:, 0:32], onesf[:, :], flat(rsum, b), start=False, stop=True))
        k = dve.did(V.tensor_tensor_scan(flat(rpx, b), c_seg8, flat(rsel, b), 0.0, ALU.mult, ALU.add))
        dve.need(k)
        k = dve.did(V.scalar_tensor_tensor(rf0[:, B, :], rpx[:, B, :], 1.0, rsel[:, B, :], ALU.is_equal, ALU.mult))
        k_f = dve.did(V.scalar_tensor_tensor(rf1[:, B, :], rpx[:, B, :], 2.0, rsel[:, B, :], ALU.is_equal, ALU.mult))
        dve.need(k_pl)
        k = misc_free[0] = dve.did(V.tensor_copy(flat(rpos, b), misc[:, 0:32]))
        yield
        dve.need(k, k_f)
        k = dve.did(V.tensor_tensor(rd[:, B, :], rpos[:, B, :], c_list[:, None, :].broadcast_to(wide), ALU.add))
        dve.need(k)
        k1 = dve.did(V.tensor_tensor(rg[:, B, :], rf0[:, B, :], rd[:, B, :], ALU.mult))
        k2 = dve.did(V.tensor_tensor(rq[:, B, :], rf1[:, B, :], rd[:, B, :], ALU.mult))
        dve.need(k1)
        k1 = dve.did(V.tensor_reduce(r32[0][:, B], rg[:, B, :], AX.X, ALU.add))
        dve.need(k2)
        k2 = dve.did(V.tensor_reduce(r32[1][:, B], rq[:, B, :], AX.X, ALU.add))
        dve.need(k1)
        k1 = dve.did(V.tensor_scalar(sidx[0][:, B], r32[0][:, B], 0.0, None, ALU.add))
        dve.need(k2)
        k2 = dve.did(V.tensor_scalar(sidx[1][:, B], r32[1][:, B], 0.0, None, ALU.add))
        yield
        pool.need(k1, k2, k_xs, k_clear[b])
        for t in range(4):
            for n in range(2):
                sc_done[b] = a_sc[i].add(G.indirect_dma_start(
                    rows_in, bass.IndirectOffsetOnAxis(ap=sidx[n][:, 4 * b + t:4 * b + t + 1], axis=0),
                    xs[i][:, t, :], None))
            yield

    first = prep(0)
    next(first)
    for i in range(2):
        v0 = pool.did(G.memset(ar2[:, 2048 * i:2048 * i + 2048], 0.0))
        pool.need(v0)
        z_v.append(pool.did(G.memset(vst[i][:, :, :, 8:9], 1.0)))
    for _ in first:
        pass

    dve.need(got["w0"])
    k = dve.did(V.tensor_tensor(lamw[:, 0:16].rearrange("p (a d) -> p a d", a=2), lam[:, 0:4:2, :], lam[:, 1:4:2, :],
                                ALU.mult))
    dve.need(k)
    k = dve.did(V.tensor_reduce(lamw[:, 16:18], lamw[:, 0:16].rearrange("p (a d) -> p a d", a=2), AX.X, ALU.add))
    dve.need(k)
    k = dve.did(V.tensor_scalar(lamw[:, 18:20], lamw[:, 16:18], 5.0, None, ALU.min))
    act.need(k)
    k = act.did(S.activation(lamw[:, 20:22], lamw[:, 18:20], ACT.Exp))
    dve.need(k)
    k = dve.did(V.tensor_tensor(lamw[:, 22:23], lamw[:, 20:21], lamw[:, 21:22], ALU.subtract))
    dve.need(k)
    k = dve.did(V.tensor_scalar(lamw[:, 23:24], lamw[:, 22:23], 0.8, -1.0 / 8, ALU.add, ALU.mult))
    pe.need(k, c2)
    k = pe.did(M.matmul(misc[:, 0:1], onesf[0:8, :], lamw[:, 23:24], start=True, stop=True))
    dve.need(k)
    k_nlv = dve.did(V.tensor_copy(nlv[:, :], misc[:, 0:1]))
    misc_free[0] = k_nlv

    k = pool.did(G.memset(maskf[:, :], 0.0))
    pool.need(k)
    c_mask = pool.did(G.affine_select(out=maskf[:, 384:512], in_=maskf[:, 384:512], compare_op=ALU.is_ge, fill=NEG,
                                      base=0, pattern=[[-1, 128]], channel_multiplier=1))
    pool.need(c2)
    c_us = pool.did(G.affine_select(out=ustrict[:, :], in_=onesf[:, :], compare_op=ALU.is_gt, fill=0.0,
                                    base=0, pattern=[[1, 128]], channel_multiplier=-1))
    k_warm = pool.did(G.memset(warm[:, :], 0.0))
    act.need(k_warm)
    k_zero = pool.did(G.memset(zrow[:, :], 0.0))
    act.need(k_zero)
    k_zrow = Arrivals(nc, "a_zr").add(nc.scalar.dma_start(rows_out[ROWS:ROWS + 1, :], zrow[0:1, 0:128]))
    k = dve.did(V.memset(segm[:, :], 1.0))
    dve.need(k)
    c_seg = dve.did(V.memset(segm[:, 0:256:NT], 0.0))
    c_seg = dve.did(V.memset(rsum[:, 0, :], 0.0))

    sp.need(*st["stack_ready"][0])
    for ld in late:
        load(*ld)
    NG = 4 * NB
    for j in range(4):
        scores(0, j)
    shift_rows(0, shift_parts(0))
    scores(1, 0)
    scores(1, 1)
    PREP_AT = (13, 14, 15, 0, 3, 5)
    work, proj, rout = iter(()), iter(()), iter(())
    parts_ready = None
    for Gr in range(NG):
        b, g = Gr // 4, Gr % 4
        for kb in range(4):
            if Gr == 0 and kb == 0:
                work = prep(1)
            if 4 * g + kb == PREP_AT[0] and b + 2 < NB:
                work = prep(b + 2)
            before = (Gr, kb - 1) if kb else (Gr - 1, 3)
            for step in "0A1WP2B3":
                if step in "0123":
                    st_exp(Gr, kb, int(step))
                elif step == "P" and before[0] >= 0:
                    for j in range(4):
                        pv(*before, j)
                elif step in "AB" and Gr + 2 < NG:
                    scores(Gr + 2, kb, (0 if step == "A" else 1,))
                elif step == "W" and (Gr < 2 or 4 * g + kb in PREP_AT):
                    next(work, None)
            if kb == 0 and Gr > 0:
                take_values()
                if parts_ready is not None:
                    shift_rows(Gr + 1, parts_ready)
                    parts_ready = None
            if kb == 1 and Gr > 0:
                k = finish_group(Gr - 1)
                if g == 0:
                    proj = project(b - 1, k)
                    next(proj)
            if kb == 1 and g < 2:
                clear(b, g)
            if Gr == 0:
                if kb < 2:
                    scores(1, kb + 2)
                elif kb == 2:
                    shift_rows(1, shift_parts(1))
            if kb >= 2:
                next(proj, None)
            if g == 1 and kb == 0 and b > 0:
                rout = chain(rout, route(b - 1))
            next(rout, None)
            if kb == 3 and Gr + 2 < NG:
                parts_ready = shift_parts(Gr + 2)
        if g == 1:
            for _ in work:
                pass
    for j in range(4):
        pv(NG - 1, 3, j)
    take_values()
    for _ in project(NB - 1, finish_group(NG - 1)):
        pass

    for _ in chain(rout, route(NB - 1)):
        pass
    act.did(S.activation(warm[:, 1:2], warm[:, 0:1], ACT.Silu))

    nall, cend, cbase, tot = rs8[:, 0:8], rs8[:, 8:16], rs8[:, 16:24], rs8[:, 24:25]
    pe.need(misc_free[0], k_sel[NB - 1])
    dve.need((dve.sem, dve.n))
    pe.need((dve.sem, dve.n))
    k = pe.did(M.matmul(misc[:, 0:8], onesf[:, :], rsum[:, NT, :], start=True, stop=True))
    dve.need(k)
    k_nall = misc_free[0] = dve.did(V.tensor_copy(nall, misc[:, 0:8]))

    mh = [res, oT, att[0][:, :, :].rearrange("p t d -> p (t d)"), att[1][:, :, :].rearrange("p t d -> p (t d)")]
    mh_free = [st["res_free"], oT_free[0], att_free[0], att_free[1]]
    for a in range(4):
        pe.need(got["wqk"], misc_free[0])
        for q in range(4):
            h = 4 * a + q
            ins = M.matmul(misc[:, 128 * q:128 * q + 128], wq1[:, h, :], wk1[:, h, :], start=True, stop=True)
        k_wqk = k = pe.did(ins)
        act.need(k, mh_free[a])
        k_mh = misc_free[0] = act.did(S.mul(mh[a][:, :], misc[:, :], 0.125))

    dve.need(k_nall)
    steps = etmp.rearrange("p e t -> p (e t)")[:, 0:128].rearrange("p (e s) -> p e s", s=16)
    k = dve.did(V.tensor_tensor(steps, nall[:, :, None].broadcast_to([128, E, 16]),
                                c_steps[:, None, :].broadcast_to([128, E, 16]), ALU.is_gt))
    dve.need(k)
    k = dve.did(V.tensor_reduce(cbase, steps, AX.X, ALU.add))
    dve.need(k)
    k = dve.did(V.tensor_tensor_scan(cend, segm[:, 1:9], cbase, 0.0, ALU.mult, ALU.add))
    dve.need(k)
    k = dve.did(V.tensor_tensor(cbase, cend, cbase, ALU.subtract))
    k2 = dve.did(V.tensor_scalar(tot, cend[:, 7:8], -1.0, None, ALU.add))
    dve.need(k, k2)
    tab = sb("tab", [128, 5, NCH])
    tb_ = [tab[:, n] for n in range(5)]
    t_c, t_e, t_n, t_b, t_h = tb_
    grid = [re_[:, 0:2].rearrange("p a e t -> p (a e t)")[:, 0:8 * NCH].rearrange("p (c e) -> p c e", e=E),
            re_[:, 2:4].rearrange("p a e t -> p (a e t)")[:, 0:8 * NCH].rearrange("p (c e) -> p c e", e=E)]
    loc = rd.rearrange("p t e -> p (t e)")[:, 0:2 * NCH]
    wide = [128, NCH, E]
    k = dve.did(V.tensor_scalar(t_c, c_pass, tot, None, ALU.min))
    dve.need(k)
    k = dve.did(V.tensor_tensor(grid[0], t_c[:, :, None].broadcast_to(wide), cend[:, None, :].broadcast_to(wide),
                                ALU.is_ge))
    k2 = dve.did(V.tensor_tensor(grid[1], t_c[:, :, None].broadcast_to(wide), cbase[:, None, :].broadcast_to(wide),
                                 ALU.is_ge))
    dve.need(k)
    k_e = dve.did(V.tensor_reduce(t_e, grid[0], AX.X, ALU.add))
    dve.need(k2)
    k = dve.did(V.tensor_tensor(grid[1], grid[1], grid[0], ALU.subtract))
    dve.need(k)
    k = dve.did(V.tensor_tensor(grid[0], grid[1], nall[:, None, :].broadcast_to(wide), ALU.mult))
    k2 = dve.did(V.tensor_tensor(grid[1], grid[1], cbase[:, None, :].broadcast_to(wide), ALU.mult))
    dve.need(k)
    k = dve.did(V.tensor_reduce(t_n, grid[0], AX.X, ALU.add))
    dve.need(k2)
    k2 = dve.did(V.tensor_reduce(t_b, grid[1], AX.X, ALU.add))
    dve.need(k_e)
    k_wi = dve.did(V.tensor_scalar(widx[:, :], t_e, 128.0, c_p, ALU.mult, ALU.add))
    dve.need(k, k2)
    k = dve.did(V.tensor_scalar(t_n, t_n, -1.0, None, ALU.add))
    pair = [128, NCH, 2]

    def twice(a):
        return a[:, :, None].broadcast_to(pair)

    loc2 = loc.rearrange("p (c j) -> p c j", j=2)
    k2 = dve.did(V.scalar_tensor_tensor(loc2, twice(t_b), -float(CH), c_row.rearrange("p (c j) -> p c j", j=2),
                                        ALU.mult, ALU.add))
    dve.need(k, k2)
    k2 = dve.did(V.tensor_tensor(loc2, loc2, twice(t_n), ALU.min))
    dve.need(k2)
    k_ri = dve.did(V.scalar_tensor_tensor(ridx[:, :].rearrange("p (c j) -> p c j", j=2), twice(t_e), float(LIST), loc2,
                                          ALU.mult, ALU.add))

    NWS = 4
    wx = [ar2[:, 1536 * i:1536 * i + 1536].rearrange("p (m f) -> p m f", m=3) for i in range(NWS)]
    xe = [ar1[:, 256 * i:256 * i + 256].rearrange("p (t d) -> p t d", d=128) for i in range(NWS)]
    xeT = [ar1[:, 1024 + 256 * i:1280 + 256 * i] for i in range(2)]
    hT = [[ar1[:, 2048 + 1024 * i + 256 * f:2304 + 1024 * i + 256 * f] for f in range(4)] for i in range(2)]
    sg = [ar1[:, 4096 + 256 * i:4352 + 256 * i] for i in range(4)]
    eo = [ar1[:, 5120 + 256 * i:5376 + 256 * i] for i in range(2)]
    a_wx, a_xe = ([Arrivals(nc, f"a_{n}{i}") for i in range(NWS)] for n in ("wx", "xe"))
    a_eo = [Arrivals(nc, f"a_eo{i}") for i in range(2)]
    wx_ready, wx_free, xe_ready, xe_free, xeT_ready, xeT_free = {}, {}, {}, {}, {}, {}
    wx_rows = T["wx"].rearrange("e p m f -> (e p) (m f)")
    row_bank, row_free = bank[2], [bO_free[0]]

    def fetch_rows(n):
        i = n % NWS
        pool.need(k_ri, sc_done[NB - 1], sc_done[NB - 2], xe_free.get(n - NWS), st["st_done"][NB - 1])
        for j in range(2):
            xe_ready[n] = a_xe[i].add(G.indirect_dma_start(
                xe[i][:, j, :], None, rows_in,
                bass.IndirectOffsetOnAxis(ap=ridx[:, 2 * n + j:2 * n + j + 1], axis=0)))

    def fetch_weights(n):
        i = n % NWS
        pool.need(k_wi, wx_free.get(n - NWS), st["pv_done"][NB - 1])
        wx_ready[n] = a_wx[i].add(G.indirect_dma_start(
            ar2[:, 1536 * i:1536 * i + 1536], None, wx_rows,
            bass.IndirectOffsetOnAxis(ap=widx[:, n:n + 1], axis=0)))

    def turn_rows(n):
        pe.need(xe_ready[n], row_free[0])
        for t in range(2):
            ins = M.transpose(row_bank[:, 128 * t:128 * t + 128], xe[n % NWS][:, t, :], identf[:, :])
        k = xe_free[n] = pe.did(ins)
        act.need(k, xeT_free.get(n - 2))
        row_free[0] = xeT_ready[n] = act.did(S.copy(xeT[n % 2], row_bank[:, 0:CH]))

    pg = [pS[i // 2][:, 512 * (i % 2):512 * (i % 2) + 512] for i in range(4)]
    pg_free = [pS_free[0], pS_free[0], pS_free[1], pS_free[1]]
    sg_free, hT_free, hT_ready = [None] * 4, [None, None], {}
    po, po_free = [bank[0], bank[1]], [bST_free[0], bST_free[1]]
    eo_free = [None, None]

    def hidden(n, f):
        W = wx[n % NWS]
        pe.need(wx_ready[n], xeT_ready[n], pg_free[f])
        r = xeT[n % 2]
        M.matmul(pg[f][:, 0:CH], W[:, 0, 128 * f:128 * f + 128], r, start=True, stop=True)
        k = pe.did(M.matmul(pg[f][:, CH:2 * CH], W[:, 1, 128 * f:128 * f + 128], r, start=True, stop=True))
        act.need(k, sg_free[f])
        k2 = act.did(S.activation(sg[f], pg[f][:, CH:2 * CH], ACT.Silu))
        dve.need(k2, hT_free[n % 2])
        sg_free[f] = pg_free[f] = dve.did(V.tensor_tensor(hT[n % 2][f], pg[f][:, 0:CH], sg[f], ALU.mult))
        if f == 3:
            xeT_free[n] = k
            hT_ready[n] = pg_free[f]

    def outward(n):
        i = n % 2
        W = wx[n % NWS][:, 2, :].rearrange("p (f d) -> p f d", f=4)
        pe.need(hT_ready[n], po_free[i])
        for t in range(2):
            for f in range(4):
                ins = M.matmul(po[i][:, 128 * t:128 * t + 128], hT[i][f][:, 128 * t:128 * t + 128], W[:, f, :],
                               start=(f == 0), stop=(f == 3))
        k = hT_free[i] = wx_free[n] = st["hid_done"] = pe.did(ins)
        dve.need(k, eo_free[i])
        k2 = po_free[i] = dve.did(V.tensor_copy(eo[i], po[i][:, 0:CH]))
        sp.need(k2)
        eo_free[i] = a_eo[i].add(nc.sync.dma_start(
            rows_out[CH * n:CH * n + CH, :].rearrange("(t p) d -> p t d", p=128),
            eo[i].rearrange("p (t d) -> p t d", d=128)))

    def every(a):
        return a[:, :, None].broadcast_to([128, E, NT])

    def by_expert(a):
        return a.rearrange("p t e -> p e t")

    def by_tile(a):
        return a.rearrange("p e t -> p t e")

    def capacity():
        every_t = [128, NT, E]
        k = dve.did(V.tensor_tensor(rd, rp, rsel, ALU.mult))
        dve.need(k)
        k = dve.did(V.tensor_reduce(r32[0][:, :], rd, AX.X, ALU.add))
        dve.need(k)
        k = dve.did(V.tensor_scalar(r32[1][:, :], r32[0][:, :], EPS, None, ALU.max))
        dve.need(k)
        k = dve.did(V.reciprocal(r32[2][:, :], r32[1][:, :]))
        dve.need(k)
        k_rw = dve.did(V.tensor_tensor(rw, rd, r32[2][:, :, None].broadcast_to(every_t), ALU.mult))
        dve.need(k_rw)
        k = dve.did(V.scalar_tensor_tensor(ewm, by_expert(rw), -1.0, by_expert(rsel), ALU.add, ALU.add))
        yield
        tau, cand, cnt, hit, skip = (rs8[:, 8 * n:8 * n + 8] for n in (3, 4, 5, 1, 2))
        k_tau = dve.did(V.memset(tau, 0.0))

        def count(ready):
            dve.need(ready)
            return dve.did(V.tensor_reduce(cnt, eg, AX.X, ALU.add))

        def spread(ready):
            pe.need(ready, misc_free[0])
            return pe.did(M.matmul(misc[:, 0:8], onesf[:, :], cnt, start=True, stop=True))

        for bit in range(29, -1, -1):
            dve.need(k, k_tau)
            k = dve.did(V.tensor_scalar(cand.bitcast(I32), tau.bitcast(I32), 1 << bit, None, ALU.bitwise_or))
            dve.need(k)
            k = count(dve.did(V.tensor_tensor(eg, ewm, every(cand), ALU.is_ge)))
            yield
            k = spread(k)
            yield
            dve.need(k)
            k = misc_free[0] = dve.did(V.scalar_tensor_tensor(hit, misc[:, 0:8], CAP - 0.5, cand, ALU.is_ge, ALU.mult))
            dve.need(k)
            k_tau = dve.did(V.tensor_tensor(tau, tau, hit, ALU.max))
        dve.need(k_tau)
        k = dve.did(V.tensor_tensor(eg, ewm, every(tau), ALU.is_gt))
        kq = dve.did(V.tensor_tensor(eq, ewm, every(tau), ALU.is_equal))
        k = count(k)
        yield
        k = spread(k)
        dve.need(k)
        k_more = misc_free[0] = dve.did(V.tensor_copy(hit, misc[:, 0:8]))
        yield
        af = eq.rearrange("p e t -> p (e t)")
        pe.need(kq, misc_free[0])
        M.matmul(misc[:, 0:256], ustrict[:, :], af, start=True, stop=True)
        k = pe.did(M.matmul(misc[:, 256:512], onesf[:, :], af, start=True, stop=True))
        dve.need(k, c_seg)
        k = dve.did(V.tensor_tensor_scan(escan, segm[:, :], misc[:, 256:512], 0.0, ALU.mult, ALU.add))
        dve.need(k)
        k = dve.did(V.tensor_tensor(escan, escan, misc[:, 256:512], ALU.subtract))
        dve.need(k)
        k = misc_free[0] = dve.did(V.tensor_tensor(epos.rearrange("p e t -> p (e t)"), misc[:, 0:256], escan, ALU.add))
        yield
        dve.need(k, k_more)
        k = dve.did(V.tensor_tensor(epos, epos, every(hit), ALU.add))
        dve.need(k)
        k = dve.did(V.scalar_tensor_tensor(eq, epos, CAP - 0.5, eq, ALU.is_lt, ALU.mult))
        dve.need(k)
        k_keep = dve.did(V.tensor_tensor(by_expert(rg), eg, eq, ALU.add))
        k = dve.did(V.tensor_scalar(skip, cbase_keep, float(CH), -float(ROWS), ALU.mult, ALU.add))
        dve.need(k)
        k = dve.did(V.tensor_tensor(rpos, rpos, skip[:, None, :].broadcast_to(every_t), ALU.add))
        dve.need(k_keep)
        kw = dve.did(V.tensor_tensor(rw, rw, rg, ALU.mult))
        dve.need(k)
        k = dve.did(V.tensor_tensor(rpos, rpos, rg, ALU.mult))
        yield
        for n in range(2):
            f = (rf0, rf1)[n]
            dve.need(k)
            k1 = dve.did(V.tensor_tensor(rd, f, rpos, ALU.mult))
            dve.need(kw)
            k2 = dve.did(V.tensor_tensor(rq, f, rw, ALU.mult))
            dve.need(k1)
            k1 = dve.did(V.tensor_reduce(r32[0][:, :], rd, AX.X, ALU.add))
            dve.need(k2)
            k2 = dve.did(V.tensor_reduce(kw_[n][:, :], rq, AX.X, ALU.add))
            dve.need(k1, k2)
            k = dve.did(V.tensor_scalar(idx[n][:, :], r32[0][:, :], float(ROWS), None, ALU.add))
            yield
        kept["idx"] = k
        dve.need(k)
        k1 = dve.did(V.tensor_tensor(r32[0][:, :], kw_[0][:, :], kw_[1][:, :], ALU.add))
        dve.need(k, k1)
        k1 = dve.did(V.tensor_scalar(r32[1][:, :], r32[0][:, :], EPS, None, ALU.max))
        dve.need(k1)
        k1 = dve.did(V.reciprocal(r32[2][:, :], r32[1][:, :]))
        dve.need(k1)
        for n in range(2):
            kept["w"] = dve.did(V.tensor_tensor(kw_[n][:, :], kw_[n][:, :], r32[2][:, :], ALU.mult))
        yield

    cbase_keep = sb("cbase_keep", [128, E])
    dve.did(V.tensor_copy(cbase_keep[:, :], cbase))
    cbase_keep = cbase_keep[:, :]
    dve.need((dve.sem, dve.n))
    kept = {}
    fetch_weights(0)
    fetch_rows(0)
    for n in range(1, 3):
        fetch_rows(n)
        fetch_weights(n)
    turn_rows(0)
    cap = capacity()
    for n in range(NCH):
        hidden(n, 0)
        hidden(n, 1)
        next(cap, None)
        if n + 1 < NCH:
            turn_rows(n + 1)
        hidden(n, 2)
        hidden(n, 3)
        next(cap, None)
        if n:
            outward(n - 1)
        if n + 3 < NCH:
            fetch_rows(n + 3)
            fetch_weights(n + 3)
    outward(NCH - 1)
    for _ in cap:
        pass
    k_idx, k_w = kept["idx"], kept["w"]
    act.did(S.activation(warm[:, 2:3], warm[:, 0:1], ACT.Exp))

    NGR = 4
    gat = [[ar2[:, 6656 + 256 * i + 128 * n:6784 + 256 * i + 128 * n] for n in range(2)] for i in range(NGR)]
    a_ga = [Arrivals(nc, f"a_ga{i}") for i in range(NGR)]
    gat_free = [st["pv_done"][NB - 1]] * NGR
    pool.need(*eo_free, k_zrow, k_idx)

    def fetch(b, t):
        i = (4 * b + t) % NGR
        pool.need(gat_free[i])
        for n in range(2):
            w = a_ga[i].add(G.indirect_dma_start(
                gat[i][n], None, rows_out, bass.IndirectOffsetOnAxis(ap=idx[n][:, 4 * b + t:4 * b + t + 1], axis=0)))
            yield w

    def combine(b, t, w):
        i, c = (4 * b + t) % NGR, 4 * b + t
        dve.need(w, k_w)
        k = dve.did(V.scalar_tensor_tensor(x[:, c, :], gat[i][0], kw_[0][:, c:c + 1], x[:, c, :], ALU.mult, ALU.add))
        dve.need(k)
        gat_free[i] = st["x_done"][b] = dve.did(V.scalar_tensor_tensor(
            x[:, c, :], gat[i][1], kw_[1][:, c:c + 1], x[:, c, :], ALU.mult, ALU.add))

    def returned(b):
        ws = []
        for t in range(4):
            for w in fetch(b, t):
                yield
            ws.append(w)
        for t in range(4):
            combine(b, t, ws[t])
            yield

    for _ in returned(0):
        pass

    zT = ar2[:, 0:4096].rearrange("p (r n) -> p r n", r=8)
    v1 = [ar1[:, 4096 * i:4096 * i + 4096].rearrange("p (k f) -> p k f", k=4) for i in range(2)]
    yT = [[ar1[:, 8192 + 1024 * i + 512 * a:8704 + 1024 * i + 512 * a] for a in range(2)] for i in range(2)]
    NP = 8
    pr_ = [ar1[:, 10240 + 512 * i:10752 + 512 * i] for i in range(7)] + [ar2[:, 7680:8192]]
    pT = [ar1[:, 13824:16384], ar2[:, 4096:6656]]
    pT4 = [t.rearrange("p (k n) -> p k n", k=4) for t in pT]

    old1 = [hT_free[0], hT_free[1], *eo_free]
    bank2_free = [row_free[0]]

    xT1 = xnT
    xT1_free, v1_free = [st["xnT_free"][0], st["xnT_free"][1]], [None, None]
    xT1_ready, v1_ready = {}, {}
    st["x_done1"] = [None] * NB

    def turn_batch(b, dst, free):
        k = ln_stats(b, st["x_done"][b])
        yield
        k = ln_apply(b, k, xn, xn_free[0])
        yield
        k = transpose_tiles([xn[:, t, :] for t in range(4)], k)
        xn_free[0] = k
        act.need(k, free)
        misc_free[0] = k = act.did(S.copy(dst, misc[:, :]))
        return k

    def prep1(b):
        i = b % 2
        xT1_ready[b] = k = yield from turn_batch(b, xT1[i][:, :], xT1_free[i])
        yield
        for t in range(4):
            for n in range(2):
                o_, f_ = (bank[2], o1_free) if b == 0 and n else (misc, misc_free)
                pe.need(k, f_[0], got["w1"])
                k1 = pe.did(M.matmul(o_[:, :], xT1[i][:, 128 * t:128 * t + 128], wv1[:, 512 * n:512 * n + 512],
                                     start=True, stop=True))
                e_ = act if n else dve
                e_.need(k1, v1_free[i], *old1)
                o = v1[i][:, t, 512 * n:512 * n + 512]
                f_[0] = e_.did(S.copy(o, o_[:, :]) if n else V.tensor_copy(o, o_[:, :]))
                v1_ready.setdefault(b, []).append(f_[0])
                yield

    y_ready, y_free = {}, [None, None]

    def heads(b, r, a):
        i = (8 * b + r) % 2
        o_, f_, n_ = (bank[a], tt_free, a) if b == r == 0 else (misc, misc_free, 0)
        pe.need(xT1_ready[b], f_[n_], k_mh)
        k = pe.did(M.matmul(o_[:, :], mh[r // 2][:, 128 * (2 * (r % 2) + a):128 * (2 * (r % 2) + a) + 128], xT1[b % 2][:, :], start=True, stop=True))
        dve.need(k, y_free[i], *old1)
        f_[n_] = y_ready[(b, r, a)] = dve.did(V.tensor_copy(yT[i][a], o_[:, :]))

    e_ready, p_ready, p_free, q_ready, q_free = {}, {}, [None] * NP, {}, [None, None]
    s1_free = [[pg_free[0], pg_free[1]], [pg_free[2], pg_free[3]]]
    tt_free = [po_free[0], po_free[1]]
    o1_free = [bank2_free[0]]
    nm_free, rd_free = [None] * 8, [None] * 8

    def scores1(u, b, r, qb, a):
        s, w = u % 2, 128 * (qb + 1)
        i = (8 * b + r) % 2
        pe.need(y_ready[(b, r, a)], s1_free[s][a], *([st["hid_done"]] if u < 2 else []))
        o = pS[s][:, 512 * a:512 * a + w]
        k = pe.did(M.matmul(o, yT[i][a][:, 128 * qb:128 * qb + 128], xT1[b % 2][:, 0:w], start=True, stop=True))
        if qb == 3 and a == 1:
            y_free[i] = k
            if r == 7:
                xT1_free[b % 2] = k
        c = 2 * (u % 4) + a
        pi = (2 * u + a) % NP
        p = pr_[pi][:, 0:w]
        dve.need(k, nm_free[c], p_free[pi], c_mask)
        k = s1_free[s][a] = dve.did(V.tensor_tensor_reduce(p, o, maskf[:, 512 - w:512], -1.0, 3e38, ALU.add, ALU.min,
                                                           accum_out=nm1[:, c:c + 1]))
        act.need(k, rd_free[c])
        nm_free[c] = e_ready[(u, a)] = act.did(S.activation(p, p, ACT.Exp, bias=nm1[:, c:c + 1], scale=-1.0,
                                                            accum_out=den1[:, c:c + 1]))

    def normalise(u, qb):
        w, c = 128 * (qb + 1), 2 * (u % 4)
        dve.need(e_ready.pop((u, 0)), e_ready.pop((u, 1)), *[p_ready.get((u - 4, a)) for a in range(2)])
        k = dve.did(V.reciprocal(rd1[:, c:c + 2], den1[:, c:c + 2]))
        rd_free[c] = rd_free[c + 1] = k
        pool.need(k)
        for a in range(2):
            p = pr_[(2 * u + a) % NP][:, 0:w]
            p_ready[(u, a)] = pool.did(G.tensor_scalar(p, p, rd1[:, c + a:c + a + 1], 1.0, ALU.mult, ALU.mult))

    tbank = [bank[0], bank[1]]

    def turn(u, qb, a):
        pi, i = (2 * u + a) % NP, (u // 4) % 2
        w = 128 * (qb + 1)
        pe.need(p_ready[(u, a)], tt_free[a])
        for t in range(qb + 1):
            at = 128 * (qb - t if a else t)
            ins = M.transpose(tbank[a][:, at:at + 128], pr_[pi][:, 128 * t:128 * t + 128], identf[:, :])
        k = p_free[pi] = pe.did(ins)
        e_ = dve if a else act
        e_.need(k, q_free[i])
        src = tbank[a][:, 0:w].rearrange("p (t n) -> p t n", n=128)
        if a:
            k = dve.did(V.tensor_copy(pT4[i][:, 3 - qb:4, w:w + 128], src))
        else:
            o = pT[i][:, 128 * qb:128 * qb + 512 * (qb + 1)].rearrange("p (t n) -> p t n", n=512)
            k = act.did(S.copy(o[:, :, 0:128], src))
        tt_free[a] = q_ready[(u // 4, a)] = k

    z_free = [None]

    def values(pair, kb):
        b, r, i = pair // 8, pair % 8, pair % 2
        pe.need(q_ready[(pair, 0)], q_ready[(pair, 1)], *v1_ready[b])
        if kb == 0:
            pe.need(o1_free[0])
        for a in range(2):
            h = 2 * r + a
            w = pT4[i][:, 3 - kb, 128 * (kb + 1):640] if a else pT4[i][:, kb, 0:128 * (4 - kb)]
            ins = M.matmul(bank[2][64 * a:64 * a + 64, 128 * kb:512], v1[b % 2][:, kb, 64 * h:64 * h + 64], w,
                           start=(kb == 0), stop=(kb == 3))
        k = pe.did(ins)
        if kb == 3:
            q_free[i] = k
            act.need(k, z_free[0], k_wqk)
            o1_free[0] = act.did(S.copy(zT[:, r, :], bank[2][:, :]))
            if r == 7:
                v1_free[b % 2] = k

    def project1(b):
        ready = o1_free[0]
        for t in range(4):
            pe.need(ready, misc_free[0], got["w1"])
            for r in range(8):
                ins = M.matmul(misc[:, 0:128], zT[:, r, 128 * t:128 * t + 128], wo1[:, r, :],
                               start=(r == 0), stop=(r == 7))
            k = z_free[0] = pe.did(ins)
            dve.need(k)
            xt = x[:, 4 * b + t, :]
            misc_free[0] = st["x_done1"][b] = dve.did(V.tensor_tensor(xt, misc[:, 0:128], xt, ALU.add))
            yield

    xT4_done, k_w1 = [None] * NB, [None] * NB

    def route1(b):
        B = slice(4 * b, 4 * b + 4)
        dst = xT4[:, 512 * b:512 * b + 512]
        k = ln_stats(b, st["x_done1"][b], 1)
        yield
        k = ln_apply(b, k, xs[0], xs_free[0], 1)
        yield
        k = xs_free[0] = transpose_tiles([xs[0][:, t, :] for t in range(4)], k)
        act.need(k)
        k = xT4_done[b] = misc_free[0] = act.did(S.copy(dst, misc[:, :]))
        yield
        yield from likely(b, logits(b, k, dst, rt1)[1])
        dve.need(got["w1"])
        k = dve.did(V.tensor_scalar(rd[:, B, :], rp[:, B, :], rb1[:, 0:1], None, ALU.add))
        dve.need(k)
        k = yield from chosen(b, rd, 4)
        yield
        dve.need(k)
        k = dve.did(V.tensor_tensor(rq[:, B, :], rp[:, B, :], rsel[:, B, :], ALU.mult))
        dve.need(k)
        k = dve.did(V.tensor_reduce(r32[0][:, B], rq[:, B, :], AX.X, ALU.add))
        dve.need(k)
        k = dve.did(V.tensor_scalar(r32[1][:, B], r32[0][:, B], 1e-20, None, ALU.add))
        dve.need(k)
        k = dve.did(V.reciprocal(r32[2][:, B], r32[1][:, B]))
        dve.need(k)
        k_w1[b] = dve.did(V.tensor_tensor(rw[:, B, :], rq[:, B, :], over(r32[2], b), ALU.mult))
        yield

    xs_free = [sc_done[NB - 2]]
    work = prep1(0)
    for _ in range(3):
        next(work)
    for a in range(2):
        heads(0, 0, a)
    units = [(b, r, qb) for b in range(NB) for r in range(8) for qb in range(4)]
    NU = len(units)
    proj, back, fresh = iter(()), iter(()), -9
    LN_, LT, LV = 1, 3, 7
    for u in range(NU + LV):
        if u < NU:
            b, r, qb = units[u]
            n = u % 4
            if r == 0 and n == 0 and b + 1 < NB:
                back = returned(b + 1)
            scores1(u, b, r, qb, 0)
        if 0 <= u - LT < NU:
            turn(u - LT, units[u - LT][2], 0)
        if u < NU:
            if r == 2 and n == 2 and b + 1 < NB:
                work = prep1(b + 1)
            next(back, None)
            if n in (0, 3) or b == r == 0:
                next(work, None)
                if b == r == 0:
                    next(work, None)
            if n in (1, 2):
                if r < 7:
                    heads(b, r + 1, n - 1)
                elif b + 1 < NB:
                    heads(b + 1, 0, n - 1)
            scores1(u, b, r, qb, 1)
        if u == fresh + 1:
            next(proj)
        if 0 <= u - LN_ < NU:
            normalise(u - LN_, units[u - LN_][2])
        if 0 <= u - LT < NU:
            turn(u - LT, units[u - LT][2], 1)
        if 0 <= u - LV < NU:
            values((u - LV) // 4, (u - LV) % 4)
            if (u - LV) % 32 == 31:
                proj = chain(proj, project1(units[u - LV][0]), (None for _ in range(5)), route1(units[u - LV][0]))
                fresh = u
        if u != fresh:
            next(proj, None)
    s1_free = [s1_free[0][1], s1_free[1][1]]
    sr = [ar1[:, 768 * i:768 * i + 768] for i in range(2)]
    aa = [ar1[:, 2048 + 768 * i:2816 + 768 * i] for i in range(2)]
    aaT = [ar1[:, 4096 + 768 * i:4864 + 768 * i].rearrange("p (c n) -> p c n", c=6) for i in range(2)]
    g_free = [s1_free[0], s1_free[1]]
    h_free = [tt_free[0], tt_free[1]]
    sr_free, aa_free, aT4_free = [None, None], [None, None], [None, None]
    aa_ready, aT4_ready = {}, {}
    tr_free = [o1_free[0]]
    ar1_free = v1_free + q_free

    def gate(t):
        i = t % 2
        xt = xT4[:, 128 * t:128 * t + 128]
        pe.need(xT4_done[t // 4], g_free[i], s1_free[i])
        M.matmul(pS[i][:, 0:512], xt, gw1[:, 0:512], start=True, stop=True)
        k1 = pe.did(M.matmul(pS[i][:, 512:1024], xt, uw1[:, 0:512], start=True, stop=True))
        act.need(k1, sr_free[i], *ar1_free)
        k1 = act.did(S.activation(sr[i][:, 0:512], pS[i][:, 0:512], ACT.Silu))
        yield
        pe.need(h_free[i])
        M.matmul(bank[i][:, 0:256], xt, gw1[:, 512:768], start=True, stop=True)
        k2 = pe.did(M.matmul(bank[i][:, 256:512], xt, uw1[:, 512:768], start=True, stop=True))
        act.need(k2)
        k2 = act.did(S.activation(sr[i][:, 512:768], bank[i][:, 0:256], ACT.Silu))
        dve.need(k1, aa_free[i])
        g_free[i] = k1 = dve.did(V.tensor_tensor(aa[i][:, 0:512], pS[i][:, 512:1024], sr[i][:, 0:512], ALU.mult))
        dve.need(k2)
        h_free[i] = sr_free[i] = k2 = dve.did(V.tensor_tensor(aa[i][:, 512:768], bank[i][:, 256:512],
                                                              sr[i][:, 512:768], ALU.mult))
        pool.need(k1, k_w1[t // 4])
        av = aa[i][:, 0:512].rearrange("p (e n) -> p e n", e=E)
        k1 = pool.did(G.tensor_tensor(av, av, rw[:, t, :][:, :, None].broadcast_to([128, E, 64]), ALU.mult))
        aa_ready[t] = (k1, k2)
        yield

    def turn4(t):
        i = t % 2
        k1, k2 = aa_ready.pop(t)
        pe.need(k1, k2, tr_free[0])
        for c in range(4):
            ins = M.transpose(bank[2][:, 128 * c:128 * c + 128], aa[i][:, 128 * c:128 * c + 128], identf[:, :])
        k1 = pe.did(ins)
        pe.need(misc_free[0])
        for c in range(2):
            ins = M.transpose(misc[:, 128 * c:128 * c + 128], aa[i][:, 512 + 128 * c:640 + 128 * c], identf[:, :])
        k2 = aa_free[i] = pe.did(ins)
        act.need(k1, aT4_free[i])
        tr_free[0] = k1 = act.did(S.copy(aaT[i][:, 0:4, :], bank[2][:, :].rearrange("p (c n) -> p c n", c=4)))
        act.need(k2)
        k2 = act.did(S.copy(aaT[i][:, 4:6, :], misc[:, 0:256].rearrange("p (c n) -> p c n", c=2)))
        misc_free[0] = k2
        aT4_ready[t] = (k1, k2)

    def down(t):
        i = t % 2
        pe.need(*aT4_ready.pop(t), misc_free[0])
        for c in range(6):
            ins = M.matmul(misc[:, 256:384], aaT[i][:, c, :], dw1[:, c, :], start=(c == 0), stop=(c == 5))
        k = aT4_free[i] = pe.did(ins)
        dve.need(k)
        misc_free[0] = k = dve.did(V.tensor_tensor(x[:, t, :], misc[:, 256:384], x[:, t, :], ALU.add))
        if t % 4 == 3:
            b = t // 4
            sp.need(k)
            done.append(a_out[b].add(nc.sync.dma_start(oview[:, 4 * b:4 * b + 4, :], x[:, 4 * b:4 * b + 4, :])))

    oview = out.rearrange("(t p) d -> p t d", p=128)
    a_out = [Arrivals(nc, f"a_out{b}") for b in range(NB)]
    done = []
    for t in range(NT + 2):
        tile = gate(t) if t < NT else iter(())
        next(tile, None)
        if 0 <= t - 2 < NT:
            down(t - 2)
        next(tile, None)
        next(proj, None)
        if 0 <= t - 1 < NT:
            turn4(t - 1)
        if t == 26:
            for _ in proj:
                pass
    sp.need(*done)


def layout(inputs):
    f = {k: np.asarray(v) for k, v in inputs.items()}
    c = np.ascontiguousarray
    r = {}
    r["x"] = c(f["L0_attn_x"].reshape(4096, 128))
    r["W0"] = c(np.stack([f["L0_attn_W" + n].T for n in "qkvp"], axis=1))
    r["bqk"] = c(np.stack([f["L0_attn_bq"], f["L0_attn_bk"]], axis=1))
    r["bvp"] = c(np.broadcast_to(np.stack([f["L0_attn_bv"], f["L0_attn_bp"]])[None], (128, 2, 128)))
    r["lam"] = c(np.stack([f["L0_attn_lambda_" + n][:, 0, :] for n in ("q1", "k1", "q2", "k2")], axis=1))
    r["rt0"] = c(f["L0_ffn_router_weight"].T)
    r["wx"] = c(np.stack([f["L0_ffn_ff_pre_act_weight"].transpose(0, 2, 1), f["L0_ffn_gate_weight"].transpose(0, 2, 1),
                          f["L0_ffn_ff_post_act_weight"].reshape(8, 128, 4, 128).transpose(0, 3, 2, 1)
                          .reshape(8, 128, 512)], axis=2))
    r["wq1"] = c(f["L1_attn_W_Q"].transpose(1, 0, 2))
    r["wk1"] = c(f["L1_attn_W_K"].transpose(1, 0, 2))
    r["wv1"] = c(f["L1_attn_W_V"].reshape(1024, 128).T)
    r["wo1"] = c(f["L1_attn_W_O"].T.reshape(8, 128, 128).transpose(1, 0, 2))
    for n, m in (("gw1", "gate_w"), ("uw1", "up_w")):
        r[n] = c(np.concatenate([f["L1_ffn_" + m].transpose(1, 0, 2).reshape(128, 512), f["L1_ffn_s_" + m]], axis=1))
    r["dw1"] = c(np.concatenate([f["L1_ffn_down_w"].reshape(512, 128), f["L1_ffn_s_down_w"]])
                 .reshape(6, 128, 128).transpose(1, 0, 2))
    r["stack"] = np.concatenate([np.zeros((24, 4096), np.float32),
                                 np.full((3, 8192), 0x3F80, np.uint16).view(np.float32)])
    r["rt1"] = c(f["L1_ffn_router_w"])
    r["rb1"] = c(np.broadcast_to(f["L1_ffn_router_bias"], (128, 1)))
    p = np.arange(128, dtype=np.float32)[:, None]

    def row(v):
        return np.broadcast_to(np.asarray(v, np.float32)[None], (128, len(v)))

    r["cst"] = c(np.concatenate([row(np.arange(NCH)), 128 * row(np.arange(2 * NCH)) + p, row(CH * np.arange(16)), p,
                                 row(LIST * np.arange(E)), row(np.tile([0] + [1] * 7, 4))], axis=1))
    return r


def kernel(**inputs):
    from concourse import bacc
    from concourse.bass_utils import run_bass_kernel_spmd

    arrays = layout(inputs)
    nc = bacc.Bacc("TRN2", target_bir_lowering=False, num_devices=1)
    T = {n: nc.dram_tensor("in_" + n, a.shape, mybir.dt.from_np(a.dtype), kind="ExternalInput").ap()
         for n, a in arrays.items()}
    out = nc.dram_tensor("out", (4096, 128), F32, kind="ExternalOutput").ap()
    program(nc, T, out)
    r = run_bass_kernel_spmd(nc, [{"in_" + n: a for n, a in arrays.items()}], core_ids=[0])
    return r.results[0]["out"].reshape(8, 512, 128)
```

```python
from itertools import chain

import numpy as np
import concourse.bass as bass
from concourse import mybir
from concourse.alu_op_type import AluOpType as ALU

F32 = mybir.dt.float32
BF16 = mybir.dt.bfloat16
I32 = mybir.dt.int32
U32 = mybir.dt.uint32
ACT = mybir.ActivationFunctionType
AX = mybir.AxisListType

NB = 8
NT = 32
E = 8
CAP = 1280
LIST = (3584, 512)
CH = (256, 128)
NCH = (35, 15)
ROWS = (NCH[0] * CH[0], NCH[1] * CH[1])
PASSES = [(h, n) for h in range(2) for n in range(NCH[h])]
EPS = 1.1920929e-07
LN_EPS = 1e-5
NEG = -1e10


class Eng:

    def __init__(self, nc, eng, name):
        self.e = eng
        self.sem = nc.alloc_semaphore("done_" + name)
        self.n = 0
        self.seen = {}

    def did(self, ins):
        self.n += 1
        ins.then_inc(self.sem, 1)
        return (self.sem, self.n)

    def need(self, *marks):
        for m in marks:
            if m is None:
                continue
            sem, val = m
            key = sem.name if hasattr(sem, "name") else id(sem)
            if self.seen.get(key, 0) < val:
                self.e.wait_ge(sem, val)
                self.seen[key] = val


class Arrivals:

    def __init__(self, nc, name):
        self.sem = nc.alloc_semaphore(name)
        self.n = 0

    def add(self, ins):
        self.n += 16
        ins.then_inc(self.sem, 16)
        return (self.sem, self.n)


def program(nc, T, out):
    pe, dve, act, pool, sp = (Eng(nc, e, n) for e, n in (
        (nc.tensor, "pe"), (nc.vector, "dve"), (nc.scalar, "act"), (nc.gpsimd, "pool"), (nc.sync, "sp")))
    V, S, G, M = nc.vector, nc.scalar, nc.gpsimd, nc.tensor

    def sb(name, shape, dt=F32):
        return nc.alloc_sbuf_tensor(name, shape, dt)

    def dram(name, shape, dt=F32):
        return nc.dram_tensor(name, shape, dt, kind="Internal").ap()

    x = sb("x", [128, NT, 128])
    identf = sb("identf", [128, 128])
    identb = sb("identb", [128, 128], BF16)
    onesf = sb("onesf", [128, 128])
    ustrict = sb("ustrict", [128, 128])
    maskf = sb("maskf", [128, 512])
    mhalf = sb("mhalf", [128, 32])
    w0 = sb("w0", [128, 4, 128])
    bqk = sb("bqk", [128, 2])
    bvp = sb("bvp", [128, 2, 128])
    lam = sb("lam", [8, 4, 8])
    lamw = sb("lamw", [8, 32])
    nlv = sb("nlv", [128, 1])
    warm = sb("warm", [128, 4])
    ar1 = sb("ar1", [128, 16384])
    ar2 = sb("ar2", [128, 8192])
    xn = sb("xn", [128, 4, 128])
    xnT = [sb(f"xnT{i}", [128, 512]) for i in range(2)]
    ln_sets = [[sb(f"ln_{n}{i}", [128, *d]) for n, d in (("st", (4, 6)), ("mv", (4, 2)), ("ve", (4,)), ("rs", (4,)))]
               for i in range(2)]

    bank = [nc.alloc_psum_tensor(f"bank{i}", [128, 512], F32) for i in range(4)]
    pS = [nc.alloc_psum_tensor(f"pS{i}", [128, 1024], F32) for i in range(2)]
    misc = bank[3]
    misc_free = [None]

    xin = T["x"].rearrange("(t p) d -> p t d", p=128)
    ax = [Arrivals(nc, f"ax{b}") for b in range(NB)]
    aw = Arrivals(nc, "aw")
    def whole(t):
        return t[tuple(slice(None) for _ in t.shape)]

    got, late = {}, []

    def load(key, queue, sem, dst, src):
        got[key] = sem.add(queue.dma_start(dst, src))

    load("x0", nc.sync, ax[0], x[:, 0:4, :], xin[:, 0:4, :])
    for dst, src in ((w0, "W0"), (bqk, "bqk"), (bvp, "bvp"), (lam, "lam")):
        load("w0", nc.sync, aw, whole(dst), T[src])
    load("x1", nc.sync, ax[1], x[:, 4:8, :], xin[:, 4:8, :])
    late += [(f"x{b}", nc.sync, ax[b], x[:, 4 * b:4 * b + 4, :], xin[:, 4 * b:4 * b + 4, :]) for b in range(2, NB)]

    c0 = pool.did(G.memset(identf[:, :], 0.0))
    c1 = pool.did(G.memset(identb[:, :], 0.0))
    c2 = pool.did(G.memset(onesf[:, :], 1.0))
    c3 = pool.did(G.memset(mhalf[:, :], -0.5))
    pool.need(c0)
    G_id = pool.did(G.affine_select(out=identf[:, :], in_=identf[:, :], compare_op=ALU.not_equal, fill=1.0,
                                    base=0, pattern=[[-1, 128]], channel_multiplier=1))
    pool.need(c1)
    G_idb = pool.did(G.affine_select(out=identb[:, :], in_=identb[:, :], compare_op=ALU.not_equal, fill=1.0,
                                     base=0, pattern=[[-1, 128]], channel_multiplier=1))

    rt0 = sb("rt0", [128, E])
    cst = sb("cst", [128, 193])
    c_pass, c_row, c_p, c_seg8 = cst[:, 0:35], cst[:, 35:105], cst[:, 105:106], cst[:, 106:138]
    c_steps, c_list = (cst[:, 138:154], cst[:, 154:170]), (cst[:, 170:178], cst[:, 178:186])
    late += [("rt", nc.sync, Arrivals(nc, "a_rt"), rt0[:, :], T["rt0"]),
             ("cst", nc.sync, Arrivals(nc, "a_cst"), cst[:, :], T["cst"])]
    rr = sb("rr", [128, 11, NT, E])
    rd, rp, rsrt, rg, rq, rpx, rsel, rw, rpos, rf0, rf1 = (rr[:, n] for n in range(11))
    re_ = sb("re", [128, 5, E, NT])
    ewm, eg, eq, epos, etmp = (re_[:, n] for n in range(5))
    rsum = sb("rsum", [128, NT + 2, E])
    escan_ = sb("escan", [128, 256])
    escan = escan_[:, :]
    rs8 = sb("rs8", [128, 96])
    tab = sb("tab", [128, 4, NCH[0]])
    r32 = [sb(f"r32_{n}", [128, NT]) for n in range(4)]
    kw_ = [sb(f"kw{n}", [128, NT]) for n in range(2)]
    sidx = [sb(f"sidx{n}", [128, NT], U32) for n in range(2)]
    idx = [sb(f"idx{n}", [128, NT], U32) for n in range(2)]
    widx = [sb(f"widx{h}", [128, NCH[h]], U32) for h in range(2)]
    ridx = [sb(f"ridx{h}", [128, NCH[h] * CH[h] // 128], U32) for h in range(2)]
    segm = sb("segm", [128, 256])
    xs = [sb(f"xs{i}", [128, 4, 128]) for i in range(2)]
    xsT = sb("xsT", [128, 512])
    zrow = sb("zrow", [128, 512])
    wv1, wo1 = sb("wv1", [128, 1024]), sb("wo1", [128, 8, 128])
    gw1, uw1, dw1 = sb("gw1", [128, 768]), sb("uw1", [128, 768]), sb("dw1", [128, 6, 128])
    rt1, rb1 = sb("rt1", [128, E]), sb("rb1", [128, 1])
    nm1, den1, rd1 = (sb(n, [128, 8]) for n in ("nm1", "den1", "rd1"))
    xT4 = sb("xT4", [128, 4096])
    wq1 = xT4[0:64, 0:2048].rearrange("p (h d) -> p h d", h=16)
    wk1 = xT4[0:64, 2048:4096].rearrange("p (h d) -> p h d", h=16)
    a_wl1 = Arrivals(nc, "a_wl1")
    for t_, n in ((wv1, "wv1"), (wo1, "wo1"), (gw1, "gw1"), (uw1, "uw1"), (dw1, "dw1"), (rt1, "rt1"), (rb1, "rb1")):
        late.append(("w1", nc.sync, a_wl1, whole(t_), T[n]))
    a_wqk = Arrivals(nc, "a_wqk")
    for t_, n in ((wq1, "wq1"), (wk1, "wk1")):
        late.append(("wqk", nc.sync, a_wqk, t_, T[n]))
    rows_in = [dram(f"rows_in{h}", [E * LIST[h], 128]) for h in range(2)]
    rows_out = [dram(f"rows_out{h}", [ROWS[h] + 1, 128]) for h in range(2)]
    xn_free = [None]

    def ln_stats(b, ready, i=0):
        stt, mv, ve, rstd = ln_sets[i]
        dve.need(ready)
        for t in range(4):
            k = dve.did(V.bn_stats(stt[:, t, :], x[:, 4 * b + t, :]))
        dve.need(k)
        for t in range(4):
            k = dve.did(V.bn_aggr(mv[:, t, :], stt[:, t, :]))
        dve.need(k)
        pool.need(k, c3)
        k = pool.did(G.tensor_scalar(ve[:, :], mv[:, :, 1], LN_EPS, None, ALU.add))
        pool.need(k)
        return pool.did(G.tensor_tensor(rstd[:, :], ve[:, :], mhalf[:, 0:4], ALU.pow))

    def ln_apply(b, k_rstd, dst, free, i=0):
        mv, rstd = ln_sets[i][1], ln_sets[i][3]
        dve.need(k_rstd, free)
        for t in range(4):
            k = dve.did(V.tensor_scalar(dst[:, t, :], x[:, 4 * b + t, :], mv[:, t, 0:1], rstd[:, t:t + 1],
                                        ALU.subtract, ALU.mult))
        return k

    def transpose_tiles(srcs, ready):
        pe.need(ready, misc_free[0], G_id)
        for t, s in enumerate(srcs):
            ins = M.transpose(misc[:, 128 * t:128 * t + 128], s, identf[:, :])
        return pe.did(ins)

    ab = ar1[:, :].bitcast(BF16).rearrange("p (r s h n) -> p r s h n", r=2, s=2, h=16)
    qst = [ab[:, i, 0] for i in range(2)]
    kst = [ab[:, i, 1] for i in range(2)]
    vst = [ar2[:, 2048 * i:2048 * i + 2048].rearrange("p (k h c) -> p k h c", k=4, h=16) for i in range(2)]
    NPT = 8
    pt = [ar2[:, 4096 + 512 * i:4096 + 512 * i + 512] for i in range(NPT)]
    qkp = [sb(f"qkp{i}", [128, 3, 512], BF16) for i in range(2)]
    res = sb("res", [128, 512])
    mx = [sb(f"mx{i}", [128, 16]) for i in range(2)]
    mr = sb("mr", [128, 4, 4])
    mp = [sb(f"mp{i}", [128, 4, 12], BF16) for i in range(2)]
    mT = [sb(f"mT{i}", [12, 512], BF16) for i in range(2)]
    oT = sb("oT", [128, 512])
    rden = sb("rden", [128, 4, 4])
    att = [sb(f"att{i}", [128, 4, 128]) for i in range(2)]
    aT = sb("aT", [128, 512])
    dq = [dram(f"dq{i}", [16, 24, 512], BF16) for i in range(2)]
    dk = [dram(f"dk{i}", [16, 40, 512], BF16) for i in range(2)]
    dm = [dram(f"dm{i}", [12, 512], BF16) for i in range(2)]
    a_dq, a_dk, a_dm = ([Arrivals(nc, f"a_{n}{i}") for i in range(2)] for n in ("dq", "dk", "dm"))
    a_qs, a_ks, a_ms = ([Arrivals(nc, f"a_{n}{i}") for i in range(2)] for n in ("qs", "ks", "ms"))

    flat_st = ar1[:, :].rearrange("p (r s f) -> p r s f", r=2, s=2)
    z_stack, z_v = [], []
    for i in range(2):
        a_zs = Arrivals(nc, f"a_zs{i}")
        a_zs.add(nc.scalar.dma_start(flat_st[72:96, i, 0], T["stack"][0:24]))
        z_stack.append((a_zs.add(nc.scalar.dma_start(flat_st[72:99, i, 1], T["stack"])),))
    st = {"xnT_free": [None, None], "qkp_free": [None, None], "res_free": None, "v_ready": [None] * NB,
          "stack_ready": [None] * NB, "st_done": [None] * NB, "s_done": [None] * NB, "pv_done": [None] * NB,
          "x_done": [None] * NB}

    def prep(b):
        i = b % 2
        k = ln_stats(b, got[f"x{b}"])
        yield
        k_xn = k = ln_apply(b, k, xn, xn_free[0])
        yield
        k = transpose_tiles([xn[:, t, :] for t in range(4)], k_xn)
        xn_free[0] = k
        pool.need(k_xn, got["w0"])
        st["xb%d" % b] = pool.did(G.tensor_tensor(
            x[:, 4 * b:4 * b + 4, :], x[:, 4 * b:4 * b + 4, :],
            bvp[:, 1, :][:, None, :].broadcast_to([128, 4, 128]), ALU.add))
        act.need(k, st["xnT_free"][i])
        k_T = act.did(S.copy(xnT[i][:, :], misc[:, :]))
        misc_free[0] = k_T
        yield
        own = b == 0
        kq, kqueue = (act, nc.scalar) if own else (sp, nc.sync)
        for n in range(2):
            o, rest = (bank[0], oT) if own and n else (misc, res)
            pe.need(k_T, bST_free[0] if own and n else misc_free[0], got["w0"])
            k = pe.did(M.matmul(o[:, :], w0[:, n, :], xnT[i][:, :], start=True, stop=True))
            act.need(k, st["qkp_free"][n])
            k1 = act.did(S.activation(qkp[n][:, 0, :], o[:, :], ACT.Identity, bias=bqk[:, n:n + 1]))
            dve.need(k1, None if own else st["res_free"])
            k2 = dve.did(V.scalar_tensor_tensor(rest[:, :], o[:, :], bqk[:, n:n + 1], qkp[n][:, 0, :],
                                                ALU.add, ALU.subtract))
            if own and n:
                bST_free[0] = k2
            else:
                misc_free[0] = k2
            dve.need(k2)
            k3 = dve.did(V.tensor_copy(qkp[n][:, 1, :], rest[:, :]))
            dve.need(k3)
            k4 = dve.did(V.tensor_tensor(qkp[n][:, 2, :], rest[:, :], qkp[n][:, 1, :], ALU.subtract))
            if own and n:
                oT_free[0] = k4
            else:
                st["res_free"] = k4
            if n == 0:
                for a in range(3):
                    sp.need(k4 if a else k1)
                    w = a_dq[i].add(nc.sync.dma_start(dq[i][:, 8 * a:8 * a + 8, :], qkp[0][:, a, :]))
                st["qkp_free"][0] = w
                yield
                sp.need(w, *z_stack[i], st["st_done"][b - 2] if b >= 2 else None)
                for g in range(3):
                    w = a_qs[i].add(nc.sync.dma_start(qst[i][24 * g:24 * g + 24, :, :],
                                                      dq[i].rearrange("h c n -> c h n")))
                k_qs = w
            else:
                for a in (0, 3, 1, 4, 2):
                    kq.need(k4 if a % 3 else k1)
                    w = a_dk[i].add(kqueue.dma_start(dk[i][:, 8 * a:8 * a + 8, :], qkp[1][:, a % 3, :]))
                st["qkp_free"][1] = w
                yield
                kq.need(w)
                for g in range(3):
                    w = a_ks[i].add(kqueue.dma_start(kst[i][24 * g:24 * g + 24, :, :],
                                                      dk[i][:, 8 * g:8 * g + 24, :].rearrange("h c n -> c h n")))
                k_ks = w
        st["stack_ready"][b] = (k_qs, k_ks)
        pe.need(misc_free[0])
        for t in range(4):
            ins = M.matmul(misc[:, 128 * t:128 * t + 128], xnT[i][:, 128 * t:128 * t + 128], w0[:, 2, :],
                           start=True, stop=True)
        k = pe.did(ins)
        st["xnT_free"][i] = k
        dve.need(k, z_v[i], st["pv_done"][b - 2] if b >= 2 else None)
        k = dve.did(V.tensor_tensor(vst[i][:, :, :, 0:8],
                                    misc[:, :].rearrange("p (t h d) -> p t h d", t=4, h=16),
                                    bvp[:, 0, :].rearrange("p (h d) -> p h d", d=8)[:, None, :, :]
                                    .broadcast_to([128, 4, 16, 8]), ALU.add))
        misc_free[0] = k
        st["v_ready"][b] = k
        yield

    pS_free = [None, None]
    ns = [0]
    mx_free = [None, None]
    mx_ready = {}

    def scores(Gr, j, halves=(0, 1)):
        b, g = Gr // 4, Gr % 4
        h = 4 * g + j
        for half in halves:
            s = ns[0] % 2
            ns[0] += 1
            pe.need(*st["stack_ready"][b], *z_stack[b % 2], pS_free[s])
            for q in range(2):
                qb = 2 * half + q
                ins = M.matmul(pS[s][:, 512 * q:512 * q + 512], qst[b % 2][0:96, h, 128 * qb:128 * qb + 128],
                               kst[b % 2][0:96, h, :], start=True, stop=True)
            k = pe.did(ins)
            dve.need(k, mx_free[Gr % 2])
            c = 4 * j + 2 * half
            pS_free[s] = dve.did(V.tensor_reduce(mx[Gr % 2][:, c:c + 2],
                                                 pS[s][:, :].rearrange("p (a n) -> p a n", a=2),
                                                 AX.X, ALU.max, negate=True))
        mx_ready[Gr] = pS_free[s]
        if g == 3 and j == 3:
            st["s_done"][b] = k

    mp_free, mT_free, m_ready = [None, None], [None, None], {}

    def shift_parts(Gr):
        i = Gr % 2
        mv_ = mx[i][:, :].rearrange("p (j q) -> p q j", j=4)
        pool.need(mx_ready[Gr], mp_free[i])
        k = pool.did(G.tensor_copy(mp[i][:, :, 0:4], mv_))
        pool.need(k)
        k = pool.did(G.tensor_tensor(mr[:, :, :], mv_, mp[i][:, :, 0:4], ALU.subtract))
        mx_free[i] = k
        pool.need(k)
        k = pool.did(G.tensor_copy(mp[i][:, :, 4:8], mr[:, :, :]))
        pool.need(k)
        return pool.did(G.tensor_tensor(mp[i][:, :, 8:12], mr[:, :, :], mp[i][:, :, 4:8], ALU.subtract))

    def shift_rows(Gr, ready):
        b, g, i = Gr // 4, Gr % 4, Gr % 2
        pe.need(ready, misc_free[0], G_idb)
        mb = misc[:, :].bitcast(BF16)
        for q in range(4):
            ins = M.transpose(mb[0:12, 128 * q:128 * q + 128], mp[i][:, q, :], identb[:, :])
        k = pe.did(ins)
        mp_free[i] = k
        act.need(k, mT_free[i])
        k = act.did(S.copy(mT[i][:, :], mb[0:12, 0:512]))
        misc_free[0] = k
        sp.need(k, m_ready.get(Gr - 2))
        w = a_dm[i].add(nc.sync.dma_start(dm[i], mT[i][:, :]))
        mT_free[i] = w
        sp.need(w, st["st_done"][b - 2] if b >= 2 else None)
        m_ready[Gr] = a_ms[i].add(nc.sync.dma_start(qst[b % 2][96:99, 4 * g:4 * g + 4, :],
                                                    dm[i].rearrange("(a j) n -> a j n", a=3)))

    bST = [bank[0], bank[1]]
    bST_free = [None, None]
    bO, bO_free = bank[2], [None]
    pt_free = [None] * NPT
    pt_ready = {}
    nst = [0]

    def st_exp(Gr, kb, j):
        b, g = Gr // 4, Gr % 4
        h = 4 * g + j
        s = nst[0] % 2
        p = nst[0] % NPT
        nst[0] += 1
        pe.need(m_ready[Gr], bST_free[s])
        k = pe.did(M.matmul(bST[s][:, :], kst[b % 2][0:99, h, 128 * kb:128 * kb + 128], qst[b % 2][0:99, h, :],
                            start=True, stop=True))
        if (g, kb, j) == (3, 3, 3):
            st["st_done"][b] = k
        act.need(k, pt_free[p])
        bST_free[s] = act.did(S.activation(pt[p], bST[s][:, :], ACT.Exp, scale=8 ** -0.5))
        pt_ready[(Gr, kb, j)] = (p, bST_free[s])

    def pv(Gr, kb, j):
        b, g = Gr // 4, Gr % 4
        p, ready = pt_ready.pop((Gr, kb, j))
        pe.need(st["v_ready"][b], bO_free[0], ready)
        k = pt_free[p] = pe.did(M.matmul(bO[32 * j:32 * j + 32, :], vst[b % 2][:, kb, 4 * g + j, :], pt[p],
                                         start=(kb == 0), stop=(kb == 3)))
        if (kb, j) == (3, 3):
            if g == 3:
                st["pv_done"][b] = k
            st["o_done"] = k

    oT_free = [None]
    att_free = [None, None]

    def take_values():
        act.need(st["o_done"], oT_free[0])
        bO_free[0] = act.did(S.copy(oT[:, :], bO[:, :]))

    def finish_group(Gr):
        b, g = Gr // 4, Gr % 4
        k = bO_free[0]
        k = transpose_tiles([oT[:, 128 * t:128 * t + 128] for t in range(4)], k)
        oT_free[0] = k
        mvw = misc[:, :].rearrange("p (t j c) -> p t j c", t=4, j=4)
        dve.need(k)
        k = dve.did(V.reciprocal(rden[:, :, :], mvw[:, :, :, 8]))
        dve.need(k, att_free[b % 2])
        k = dve.did(V.tensor_tensor(att[b % 2][:, :, 32 * g:32 * g + 32].rearrange("p t (j d) -> p t j d", j=4),
                                    mvw[:, :, :, 0:8],
                                    rden[:, :, :, None].broadcast_to([128, 4, 4, 8]), ALU.mult))
        misc_free[0] = k
        return k

    aT_free = [None]

    def project(b, ready):
        i = b % 2
        dve.need(ready, k_nlv)
        k = dve.did(V.scalar_tensor_tensor(att[i][:, :, 0:64], att[i][:, :, 64:128], nlv[:, 0:1],
                                           att[i][:, :, 0:64], ALU.mult, ALU.add))
        yield
        k = transpose_tiles([att[i][:, t, :] for t in range(4)], k)
        att_free[i] = k
        act.need(k, aT_free[0])
        k = act.did(S.copy(aT[:, :], misc[:, :]))
        misc_free[0] = k
        yield
        pe.need(k, misc_free[0])
        for t in range(4):
            ins = M.matmul(misc[:, 128 * t:128 * t + 128], aT[:, 128 * t:128 * t + 128], w0[:, 3, :],
                           start=True, stop=True)
        k = pe.did(ins)
        aT_free[0] = k
        dve.need(k, st["xb%d" % b])
        k = dve.did(V.tensor_tensor(x[:, 4 * b:4 * b + 4, :], misc[:, :].rearrange("p (t d) -> p t d", t=4),
                                    x[:, 4 * b:4 * b + 4, :], ALU.add))
        misc_free[0] = k
        st["x_done"][b] = k
        yield

    a_sc = [Arrivals(nc, f"a_sc{i}") for i in range(3)]
    a_zero = [Arrivals(nc, f"a_zero{b}") for b in range(NB)]
    k_clear = [None] * NB

    def clear(b, half):
        sp.need(k_zero)
        h, at = (1, 0) if b == NB - 1 else (0, 512 * b)
        rows = rows_in[h].rearrange("(e n) d -> e n d", e=E)[4 * half:4 * half + 4, at:at + 512, :]
        k_clear[b] = a_zero[b].add(nc.sync.dma_start(rows.rearrange("e (p r) d -> p e (r d)", p=128),
                                                     zrow[:, None, :].broadcast_to([128, 4, 512])))

    sc_done, xsT_free = [None] * NB, [None]
    k_sel, k_tot = [None] * NB, [None] * NB

    def over(a, b):
        return a[:, 4 * b:4 * b + 4, None].broadcast_to([128, 4, E])

    def logits(b, ready, xT, w):
        B = slice(4 * b, 4 * b + 4)
        pe.need(ready, got["rt"], got["w1"], misc_free[0])
        for t in range(4):
            ins = M.matmul(misc[:, 8 * t:8 * t + 8], xT[:, 128 * t:128 * t + 128], w[:, :], start=True, stop=True)
        k_pe = pe.did(ins)
        lg = misc[:, 0:32].rearrange("p (t e) -> p t e", e=E)
        dve.need(k_pe)
        k = dve.did(V.tensor_reduce(r32[0][:, B], lg, AX.X, ALU.max))
        dve.need(k)
        k = misc_free[0] = dve.did(V.tensor_tensor(rd[:, B, :], lg, over(r32[0], b), ALU.subtract))
        act.need(k)
        return k_pe, act.did(S.activation(rd[:, B, :], rd[:, B, :], ACT.Exp))

    def likely(b, ready):
        B = slice(4 * b, 4 * b + 4)
        yield
        dve.need(ready)
        k = dve.did(V.tensor_reduce(r32[1][:, B], rd[:, B, :], AX.X, ALU.add))
        dve.need(k)
        k = dve.did(V.reciprocal(r32[2][:, B], r32[1][:, B]))
        dve.need(k)
        k = dve.did(V.tensor_tensor(rp[:, B, :], rd[:, B, :], over(r32[2], b), ALU.mult))
        dve.need(k)

    def flat(a, b):
        return a[:, 4 * b:4 * b + 4, :].rearrange("p t e -> p (t e)")

    def chosen(b, pr, K):
        B = slice(4 * b, 4 * b + 4)
        for t in range(4 * b, 4 * b + 4):
            k = dve.did(V.max(rsrt[:, t, :], pr[:, t, :]))
        yield
        dve.need(k, got["cst"])
        last = rsrt[:, B, K - 1:K].broadcast_to([128, 4, E])
        k = dve.did(V.tensor_tensor(rg[:, B, :], pr[:, B, :], last, ALU.is_gt))
        k1 = dve.did(V.tensor_tensor(rq[:, B, :], pr[:, B, :], last, ALU.is_equal))
        dve.need(k)
        k2 = dve.did(V.tensor_reduce(r32[3][:, B], rg[:, B, :], AX.X, ALU.add))
        dve.need(k1)
        k = dve.did(V.tensor_tensor_scan(flat(rpx, b), c_seg8, flat(rq, b), 0.0, ALU.mult, ALU.add))
        pool.need(k, k2)
        k = pool.did(G.tensor_tensor(rpx[:, B, :], rpx[:, B, :], over(r32[3], b), ALU.add))
        pool.need(k)
        k = pool.did(G.tensor_scalar(rpx[:, B, :], rpx[:, B, :], K + 0.5, None, ALU.is_lt))
        pool.need(k)
        k = pool.did(G.tensor_tensor(rq[:, B, :], rpx[:, B, :], rq[:, B, :], ALU.mult))
        pool.need(k)
        return pool.did(G.tensor_tensor(rsel[:, B, :], rg[:, B, :], rq[:, B, :], ALU.add))

    def route(b):
        i, B, h = b % 2, slice(4 * b, 4 * b + 4), int(b == NB - 1)
        wide = [128, 4, E]
        ahead = rsum[:, 4 * b + h:4 * b + h + 5, :]

        k = ln_stats(b, st["x_done"][b], 1)
        yield
        k_xs = k = ln_apply(b, k, xs[i], sc_done[b - 2] if b >= 2 else None, 1)
        yield
        k = transpose_tiles([xs[i][:, t, :] for t in range(4)], k)
        act.need(k, xsT_free[0])
        k = misc_free[0] = act.did(S.copy(xsT[:, :], misc[:, :]))
        yield
        k_lg = logits(b, k, xsT, rt0)
        xsT_free[0] = k_lg[0]
        yield from likely(b, k_lg[1])
        k = yield from chosen(b, rp, 2)
        k_sel[b] = k
        for t in range(4):
            pool.need(k, c_seg)
            k = pool.did(G.tensor_tensor(ahead[:, t + 1, :], ahead[:, t, :], rsel[:, 4 * b + t, :], ALU.add))
        k_sum = k_tot[b] = k
        yield
        yield
        pe.need(k_sum, k_sel[b], misc_free[0], c_us, c2)
        M.matmul(misc[:, 0:32], ustrict[:, :], flat(rsel, b), start=True, stop=False)
        k_pl = pe.did(M.matmul(misc[:, 0:32], onesf[:, :], ahead[:, 0:4, :].rearrange("p t e -> p (t e)"), start=False, stop=True))
        dve.need(k_sel[b])
        k = dve.did(V.tensor_tensor_scan(flat(rpx, b), c_seg8, flat(rsel, b), 0.0, ALU.mult, ALU.add))
        dve.need(k)
        k = dve.did(V.scalar_tensor_tensor(rf0[:, B, :], rpx[:, B, :], 1.0, rsel[:, B, :], ALU.is_equal, ALU.mult))
        k_f = dve.did(V.scalar_tensor_tensor(rf1[:, B, :], rpx[:, B, :], 2.0, rsel[:, B, :], ALU.is_equal, ALU.mult))
        act.need(k_pl)
        k = misc_free[0] = act.did(S.copy(flat(rpos, b), misc[:, 0:32]))
        pool.need(k, k_f)
        k = pool.did(G.tensor_tensor(rd[:, B, :], rpos[:, B, :], c_list[h][:, None, :].broadcast_to(wide), ALU.add))
        pool.need(k)
        k1 = pool.did(G.tensor_tensor(rg[:, B, :], rf0[:, B, :], rd[:, B, :], ALU.mult))
        k2 = pool.did(G.tensor_tensor(rq[:, B, :], rf1[:, B, :], rd[:, B, :], ALU.mult))
        yield
        dve.need(k1)
        k1 = dve.did(V.tensor_reduce(r32[0][:, B], rg[:, B, :], AX.X, ALU.add))
        dve.need(k2)
        k2 = dve.did(V.tensor_reduce(r32[1][:, B], rq[:, B, :], AX.X, ALU.add))
        pool.need(k1)
        k1 = pool.did(G.tensor_scalar(sidx[0][:, B], r32[0][:, B], 0.0, None, ALU.add))
        pool.need(k2)
        k2 = pool.did(G.tensor_scalar(sidx[1][:, B], r32[1][:, B], 0.0, None, ALU.add))
        yield
        pool.need(k1, k2, k_xs, k_clear[b])
        for t in range(4):
            for n in range(2):
                sc_done[b] = a_sc[2 if h else i].add(G.indirect_dma_start(
                    rows_in[h], bass.IndirectOffsetOnAxis(ap=sidx[n][:, 4 * b + t:4 * b + t + 1], axis=0),
                    xs[i][:, t, :], None))
            yield

    table_ready, kept = {}, {}
    half = [0]

    def table(h):
        nch, per = NCH[h], CH[h] // 128
        nall, cend, cbase, tot = (rs8[:, 32 * h + a:32 * h + b] for a, b in ((0, 8), (8, 16), (16, 24), (24, 25)))
        pe.need(misc_free[0], k_tot[NB - 2 + h], c2)
        k = pe.did(M.matmul(misc[:, 0:8], onesf[:, :], rsum[:, 33 if h else 28, :], start=True, stop=True))
        dve.need(k)
        k = misc_free[0] = dve.did(V.tensor_copy(nall, misc[:, 0:8]))
        dve.need(k)
        steps = etmp.rearrange("p e t -> p (e t)")[:, 0:128].rearrange("p (e s) -> p e s", s=16)
        k = dve.did(V.tensor_tensor(steps, nall[:, :, None].broadcast_to([128, E, 16]),
                                    c_steps[h][:, None, :].broadcast_to([128, E, 16]), ALU.is_gt))
        dve.need(k)
        k = dve.did(V.tensor_reduce(cbase, steps, AX.X, ALU.add))
        dve.need(k)
        k = dve.did(V.tensor_tensor_scan(cend, segm[:, 1:9], cbase, 0.0, ALU.mult, ALU.add))
        dve.need(k)
        k = dve.did(V.tensor_tensor(cbase, cend, cbase, ALU.subtract))
        k2 = dve.did(V.tensor_scalar(tot, cend[:, 7:8], -1.0, None, ALU.add))
        dve.need(k, k2)
        t_c, t_e, t_n, t_b = (tab[:, n, 0:nch] for n in range(4))
        grid = [re_[:, 2 * a:2 * a + 2].rearrange("p a e t -> p (a e t)")[:, 0:8 * nch]
                .rearrange("p (c e) -> p c e", e=E) for a in range(2)]
        wide, pair = [128, nch, E], [128, nch, per]
        k = dve.did(V.tensor_scalar(t_c, c_pass[:, 0:nch], tot, None, ALU.min))
        dve.need(k)
        k = dve.did(V.tensor_tensor(grid[0], t_c[:, :, None].broadcast_to(wide),
                                    cend[:, None, :].broadcast_to(wide), ALU.is_ge))
        k2 = dve.did(V.tensor_tensor(grid[1], t_c[:, :, None].broadcast_to(wide),
                                     cbase[:, None, :].broadcast_to(wide), ALU.is_ge))
        dve.need(k)
        k_e = dve.did(V.tensor_reduce(t_e, grid[0], AX.X, ALU.add))
        dve.need(k2)
        k = dve.did(V.tensor_tensor(grid[1], grid[1], grid[0], ALU.subtract))
        dve.need(k)
        k = dve.did(V.tensor_tensor(grid[0], grid[1], nall[:, None, :].broadcast_to(wide), ALU.mult))
        k2 = dve.did(V.tensor_tensor(grid[1], grid[1], cbase[:, None, :].broadcast_to(wide), ALU.mult))
        dve.need(k)
        k = dve.did(V.tensor_reduce(t_n, grid[0], AX.X, ALU.add))
        dve.need(k2)
        k2 = dve.did(V.tensor_reduce(t_b, grid[1], AX.X, ALU.add))
        dve.need(k_e)
        k_w = dve.did(V.tensor_scalar(widx[h][:, :], t_e, 128.0, c_p, ALU.mult, ALU.add))
        dve.need(k, k2)

        def each(a):
            return a[:, :, None].broadcast_to(pair)

        def tiles(a):
            return a.rearrange("p (c j) -> p c j", j=per)

        loc = tiles(escan[:, 0:nch * per])
        k = dve.did(V.tensor_scalar(t_n, t_n, -1.0, None, ALU.add))
        k2 = dve.did(V.scalar_tensor_tensor(loc, each(t_b), -float(CH[h]), tiles(c_row[:, 0:nch * per]),
                                            ALU.mult, ALU.add))
        dve.need(k, k2)
        k2 = dve.did(V.tensor_tensor(loc, loc, each(t_n), ALU.min))
        dve.need(k2)
        k = dve.did(V.scalar_tensor_tensor(tiles(ridx[h][:, :]), each(t_e), float(LIST[h]), loc, ALU.mult, ALU.add))
        table_ready[h] = (k_w, k)
        yield

    NWS = 4
    wx_at = [ar1[:, 5632:7168], ar2[:, 0:1536], ar2[:, 2048:3584], ar2[:, 3584:5120]]
    wx = [t.rearrange("p (m f) -> p m f", m=3) for t in wx_at]
    xe = [ar1[:, 256 * i:256 * i + 256].rearrange("p (t d) -> p t d", d=128) for i in range(NWS)]
    xeT = [ar1[:, 1024 + 256 * i:1280 + 256 * i] for i in range(2)]
    hT = [[ar1[:, 2048 + 1024 * i + 256 * f:2304 + 1024 * i + 256 * f] for f in range(4)] for i in range(2)]
    sg = [ar1[:, 4096 + 256 * i:4352 + 256 * i] for i in range(4)]
    eo = [ar1[:, 5120 + 256 * i:5376 + 256 * i] for i in range(2)]
    a_wx, a_xe = ([Arrivals(nc, f"a_{n}{i}") for i in range(NWS)] for n in ("wx", "xe"))
    a_eo = [Arrivals(nc, f"a_eo{i}") for i in range(2)]
    wx_ready, wx_free, xe_ready, xe_free, xeT_ready, xeT_free = {}, {}, {}, {}, {}, {}
    wx_rows = T["wx"].rearrange("e p m f -> (e p) (m f)")
    row_bank, row_free = bank[2], [None]

    def fetch_rows(p):
        i, (h, n) = p % NWS, PASSES[p]
        pool.need(table_ready[h][1], *([sc_done[NB - 1]] if h else sc_done[NB - 3:NB - 1]),
                  xe_free[p - NWS] if p >= NWS else st["st_done"][NB - 2])
        per = CH[h] // 128
        for j in range(per):
            xe_ready[p] = a_xe[i].add(G.indirect_dma_start(
                xe[i][:, j, :], None, rows_in[h],
                bass.IndirectOffsetOnAxis(ap=ridx[h][:, per * n + j:per * n + j + 1], axis=0)))

    def fetch_weights(p):
        i, (h, n) = p % NWS, PASSES[p]
        pool.need(table_ready[h][0], wx_free[p - NWS] if p >= NWS else st["pv_done"][NB - 1 if i > 1 else NB - 2])
        if p < NWS:
            pool.need(st["st_done"][NB - 2])
        wx_ready[p] = a_wx[i].add(G.indirect_dma_start(
            wx_at[i], None, wx_rows, bass.IndirectOffsetOnAxis(ap=widx[h][:, n:n + 1], axis=0)))

    def turn_rows(p):
        w = CH[PASSES[p][0]]
        pe.need(xe_ready[p], row_free[0])
        for t in range(w // 128):
            ins = M.transpose(row_bank[:, 128 * t:128 * t + 128], xe[p % NWS][:, t, :], identf[:, :])
        k = xe_free[p] = pe.did(ins)
        act.need(k, xeT_free.get(p - 2))
        row_free[0] = xeT_ready[p] = act.did(S.copy(xeT[p % 2][:, 0:w], row_bank[:, 0:w]))

    pg = [pS[i // 2][:, 512 * (i % 2):512 * (i % 2) + 512] for i in range(4)]
    pg_free = [None] * 4
    sg_free, hT_free, hT_ready = [None] * 4, [None, None], {}
    po, po_free = [bank[0], bank[1]], [None, None]
    eo_free = [None, None]

    def hidden(p, f):
        W, w = wx[p % NWS], CH[PASSES[p][0]]
        pe.need(wx_ready[p], xeT_ready[p], pg_free[f])
        r = xeT[p % 2][:, 0:w]
        M.matmul(pg[f][:, 0:w], W[:, 0, 128 * f:128 * f + 128], r, start=True, stop=True)
        k = pe.did(M.matmul(pg[f][:, 256:256 + w], W[:, 1, 128 * f:128 * f + 128], r, start=True, stop=True))
        act.need(k, sg_free[f])
        k2 = act.did(S.activation(sg[f][:, 0:w], pg[f][:, 256:256 + w], ACT.Silu))
        dve.need(k2, hT_free[p % 2])
        sg_free[f] = pg_free[f] = dve.did(V.tensor_tensor(hT[p % 2][f][:, 0:w], pg[f][:, 0:w], sg[f][:, 0:w],
                                                          ALU.mult))
        if f == 3:
            xeT_free[p] = k
            hT_ready[p] = pg_free[f]

    def outward(p):
        i, (h, n) = p % 2, PASSES[p]
        w = CH[h]
        W = wx[p % NWS][:, 2, :].rearrange("p (f d) -> p f d", f=4)
        pe.need(hT_ready[p], po_free[i])
        for t in range(w // 128):
            for f in range(4):
                ins = M.matmul(po[i][:, 128 * t:128 * t + 128], hT[i][f][:, 128 * t:128 * t + 128], W[:, f, :],
                               start=(f == 0), stop=(f == 3))
        k = hT_free[i] = wx_free[p] = st["hid_done"] = pe.did(ins)
        dve.need(k, eo_free[i])
        k2 = po_free[i] = dve.did(V.tensor_copy(eo[i][:, 0:w], po[i][:, 0:w]))
        sp.need(k2)
        eo_free[i] = a_eo[i].add(nc.sync.dma_start(
            rows_out[h][w * n:w * n + w, :].rearrange("(t p) d -> p t d", p=128),
            eo[i][:, 0:w].rearrange("p (t d) -> p t d", d=128)))

    def every(a):
        return a[:, :, None].broadcast_to([128, E, NT])

    def by_expert(a):
        return a.rearrange("p t e -> p e t")

    def by_tile(a):
        return a.rearrange("p e t -> p t e")

    def capacity():
        every_t = [128, NT, E]
        k = dve.did(V.tensor_tensor(rd, rp, rsel, ALU.mult))
        dve.need(k)
        k = dve.did(V.tensor_reduce(r32[0][:, :], rd, AX.X, ALU.add))
        dve.need(k)
        k = dve.did(V.tensor_scalar(r32[1][:, :], r32[0][:, :], EPS, None, ALU.max))
        dve.need(k)
        k = dve.did(V.reciprocal(r32[2][:, :], r32[1][:, :]))
        dve.need(k)
        k_rw = dve.did(V.tensor_tensor(rw, rd, r32[2][:, :, None].broadcast_to(every_t), ALU.mult))
        dve.need(k_rw)
        k = dve.did(V.scalar_tensor_tensor(ewm, by_expert(rw), -1.0, by_expert(rsel), ALU.add, ALU.add))
        yield
        tau, cnt, hit, skip = (rs8[:, 60 + 8 * n:68 + 8 * n] for n in range(4))
        cand, cnt3, hit3 = (rq[:, 3 * n:3 * n + 3, :] for n in range(3))
        k_tau = dve.did(V.memset(tau, 0.0))

        def count(ready):
            dve.need(ready)
            return dve.did(V.tensor_reduce(cnt, eg, AX.X, ALU.add))

        def spread(ready, what):
            pe.need(ready, misc_free[0])
            w = what.shape[-1]
            return pe.did(M.matmul(misc[:, 0:w], onesf[:, :], what, start=True, stop=True))

        flat3, four = [a.rearrange("p k e -> p (k e)") for a in (cand, cnt3, hit3)], [128, 3, E, NT]
        while half[0] == 0:
            yield
        for bit in range(28, -1, -2):
            dve.need(k, k_tau)
            for n in range(3):
                k = dve.did(V.tensor_scalar(cand[:, n, :].bitcast(I32), tau.bitcast(I32), (n + 1) << bit, None,
                                            ALU.bitwise_or))
            dve.need(k)
            k = dve.did(V.tensor_tensor(re_[:, 1:4], ewm[:, None, :, :].broadcast_to(four),
                                        cand[:, :, :, None].broadcast_to(four), ALU.is_ge))
            dve.need(k)
            k = dve.did(V.tensor_reduce(cnt3, re_[:, 1:4], AX.X, ALU.add))
            yield
            k = spread(k, flat3[1])
            yield
            dve.need(k)
            k = misc_free[0] = dve.did(V.scalar_tensor_tensor(flat3[2], misc[:, 0:24], CAP - 0.5, flat3[0],
                                                              ALU.is_ge, ALU.mult))
            dve.need(k)
            k = dve.did(V.tensor_reduce(hit, hit3.rearrange("p k e -> p e k"), AX.X, ALU.max))
            dve.need(k)
            k_tau = dve.did(V.tensor_tensor(tau, tau, hit, ALU.max))
        dve.need(k_tau)
        k = dve.did(V.tensor_tensor(eg, ewm, every(tau), ALU.is_gt))
        kq = dve.did(V.tensor_tensor(eq, ewm, every(tau), ALU.is_equal))
        k = count(k)
        yield
        k = spread(k, cnt)
        yield
        dve.need(k)
        k_more = misc_free[0] = dve.did(V.tensor_copy(hit, misc[:, 0:8]))
        yield
        af = eq.rearrange("p e t -> p (e t)")
        pe.need(kq, misc_free[0])
        M.matmul(misc[:, 0:256], ustrict[:, :], af, start=True, stop=True)
        k = pe.did(M.matmul(misc[:, 256:512], onesf[:, :], af, start=True, stop=True))
        dve.need(k, c_seg)
        k = dve.did(V.tensor_tensor_scan(escan, segm[:, :], misc[:, 256:512], 0.0, ALU.mult, ALU.add))
        dve.need(k)
        k = dve.did(V.tensor_tensor(escan, escan, misc[:, 256:512], ALU.subtract))
        dve.need(k)
        k = misc_free[0] = dve.did(V.tensor_tensor(epos.rearrange("p e t -> p (e t)"), misc[:, 0:256], escan, ALU.add))
        yield
        dve.need(k, k_more)
        k = dve.did(V.tensor_tensor(epos, epos, every(hit), ALU.add))
        dve.need(k)
        k = dve.did(V.scalar_tensor_tensor(eq, epos, CAP - 0.5, eq, ALU.is_lt, ALU.mult))
        dve.need(k)
        k_keep = dve.did(V.tensor_tensor(by_expert(rg), eg, eq, ALU.add))
        for h in range(2):
            k = dve.did(V.tensor_scalar(skip, rs8[:, 32 * h + 16:32 * h + 24], float(CH[h]), -float(ROWS[h]),
                                        ALU.mult, ALU.add))
            dve.need(k)
            part = rpos[:, 28 * h:28 + 4 * h, :]
            k = dve.did(V.tensor_tensor(part, part, skip[:, None, :].broadcast_to([128, 4 if h else 28, E]), ALU.add))
            dve.need(k)
        dve.need(k_keep)
        kw = dve.did(V.tensor_tensor(rw, rw, rg, ALU.mult))
        dve.need(k)
        k = dve.did(V.tensor_tensor(rpos, rpos, rg, ALU.mult))
        yield
        for n in range(2):
            f = (rf0, rf1)[n]
            dve.need(k)
            k1 = dve.did(V.tensor_tensor(rd, f, rpos, ALU.mult))
            dve.need(kw)
            k2 = dve.did(V.tensor_tensor(rq, f, rw, ALU.mult))
            dve.need(k1)
            k1 = dve.did(V.tensor_reduce(r32[0][:, :], rd, AX.X, ALU.add))
            dve.need(k2)
            k2 = dve.did(V.tensor_reduce(kw_[n][:, :], rq, AX.X, ALU.add))
            dve.need(k1, k2)
            for h in range(2):
                part = slice(28 * h, 28 + 4 * h)
                k = dve.did(V.tensor_scalar(idx[n][:, part], r32[0][:, part], float(ROWS[h]), None, ALU.add))
            yield
        kept["idx"] = k
        dve.need(k)
        k1 = dve.did(V.tensor_tensor(r32[0][:, :], kw_[0][:, :], kw_[1][:, :], ALU.add))
        dve.need(k, k1)
        k1 = dve.did(V.tensor_scalar(r32[1][:, :], r32[0][:, :], EPS, None, ALU.max))
        dve.need(k1)
        k1 = dve.did(V.reciprocal(r32[2][:, :], r32[1][:, :]))
        dve.need(k1)
        for n in range(2):
            kept["w"] = dve.did(V.tensor_tensor(kw_[n][:, :], kw_[n][:, :], r32[2][:, :], ALU.mult))
        yield

    def lead():
        for p in range(2):
            fetch_weights(p)
            fetch_rows(p)
            yield

    first = prep(0)
    next(first)
    for i in range(2):
        v0 = pool.did(G.memset(ar2[:, 2048 * i:2048 * i + 2048], 0.0))
        pool.need(v0)
        z_v.append(pool.did(G.memset(vst[i][:, :, :, 8:9], 1.0)))
    for _ in first:
        pass

    dve.need(got["w0"])
    k = dve.did(V.tensor_tensor(lamw[:, 0:16].rearrange("p (a d) -> p a d", a=2), lam[:, 0:4:2, :], lam[:, 1:4:2, :],
                                ALU.mult))
    dve.need(k)
    k = dve.did(V.tensor_reduce(lamw[:, 16:18], lamw[:, 0:16].rearrange("p (a d) -> p a d", a=2), AX.X, ALU.add))
    dve.need(k)
    k = dve.did(V.tensor_scalar(lamw[:, 18:20], lamw[:, 16:18], 5.0, None, ALU.min))
    act.need(k)
    k = act.did(S.activation(lamw[:, 20:22], lamw[:, 18:20], ACT.Exp))
    dve.need(k)
    k = dve.did(V.tensor_tensor(lamw[:, 22:23], lamw[:, 20:21], lamw[:, 21:22], ALU.subtract))
    dve.need(k)
    k = dve.did(V.tensor_scalar(lamw[:, 23:24], lamw[:, 22:23], 0.8, -1.0 / 8, ALU.add, ALU.mult))
    pe.need(k, c2)
    k = pe.did(M.matmul(misc[:, 0:1], onesf[0:8, :], lamw[:, 23:24], start=True, stop=True))
    dve.need(k)
    k_nlv = dve.did(V.tensor_copy(nlv[:, :], misc[:, 0:1]))
    misc_free[0] = k_nlv

    k = pool.did(G.memset(maskf[:, :], 0.0))
    pool.need(k)
    c_mask = pool.did(G.affine_select(out=maskf[:, 384:512], in_=maskf[:, 384:512], compare_op=ALU.is_ge, fill=NEG,
                                      base=0, pattern=[[-1, 128]], channel_multiplier=1))
    pool.need(c2)
    c_us = pool.did(G.affine_select(out=ustrict[:, :], in_=onesf[:, :], compare_op=ALU.is_gt, fill=0.0,
                                    base=0, pattern=[[1, 128]], channel_multiplier=-1))
    k_warm = pool.did(G.memset(warm[:, :], 0.0))
    act.need(k_warm)
    k_zero = pool.did(G.memset(zrow[:, :], 0.0))
    act.need(k_zero)
    a_zr = Arrivals(nc, "a_zr")
    for h in range(2):
        k_zrow = a_zr.add(nc.scalar.dma_start(rows_out[h][ROWS[h]:ROWS[h] + 1, :], zrow[0:1, 0:128]))
    k = dve.did(V.memset(segm[:, :], 1.0))
    dve.need(k)
    c_seg = dve.did(V.memset(segm[:, 0:256:NT], 0.0))
    for t in (0, 29):
        c_seg = dve.did(V.memset(rsum[:, t, :], 0.0))

    sp.need(*st["stack_ready"][0])
    for ld in late:
        load(*ld)
    NG = 4 * NB
    for j in range(4):
        scores(0, j)
    shift_rows(0, shift_parts(0))
    scores(1, 0)
    scores(1, 1)
    PREP_AT = (12, 14, 15, 0, 3, 5)
    work, proj, rout = iter(()), iter(()), iter(())
    parts_ready = None
    for Gr in range(NG):
        b, g = Gr // 4, Gr % 4
        for kb in range(4):
            if Gr == 0 and kb == 0:
                work = prep(1)
            if 4 * g + kb == PREP_AT[0] and b + 2 < NB:
                work = prep(b + 2)
            before = (Gr, kb - 1) if kb else (Gr - 1, 3)
            for step in "0A1WP2B3":
                if step in "0123":
                    st_exp(Gr, kb, int(step))
                elif step == "P" and before[0] >= 0:
                    for j in range(4):
                        pv(*before, j)
                elif step in "AB" and Gr + 2 < NG:
                    scores(Gr + 2, kb, (0 if step == "A" else 1,))
                elif step == "W" and (Gr < 2 or 4 * g + kb in PREP_AT):
                    next(work, None)
            if kb == 0 and Gr > 0:
                take_values()
                if parts_ready is not None:
                    shift_rows(Gr + 1, parts_ready)
                    parts_ready = None
            if kb == 1 and Gr > 0:
                k = finish_group(Gr - 1)
                if g == 0:
                    proj = project(b - 1, k)
                    next(proj)
            if kb == 1 and g < 2:
                clear(b, g)
            if Gr == 0:
                if kb < 2:
                    scores(1, kb + 2)
                elif kb == 2:
                    shift_rows(1, shift_parts(1))
            if kb >= 2:
                next(proj, None)
            if g == 1 and kb == 0 and b > 0:
                rout = chain(rout, route(b - 1), *((table(0), lead()) if b == NB - 1 else ()))
            for _ in range(2 if b == NB - 1 and g >= 2 else 1):
                next(rout, None)
            if kb == 3 and Gr + 2 < NG:
                parts_ready = shift_parts(Gr + 2)
        if g == 1:
            for _ in work:
                pass
    for j in range(4):
        pv(NG - 1, 3, j)
    take_values()
    for _ in rout:
        pass
    row_free[0], po_free[:] = bO_free[0], bST_free
    pg_free[:] = [pS_free[0], pS_free[0], pS_free[1], pS_free[1]]

    mh = [res, oT, att[0][:, :, :].rearrange("p t d -> p (t d)"), att[1][:, :, :].rearrange("p t d -> p (t d)")]

    def matrices():
        mh_free = [st["res_free"], oT_free[0], att_free[0], att_free[1]]
        for a in range(4):
            pe.need(got["wqk"], misc_free[0])
            for q in range(4):
                h = 4 * a + q
                ins = M.matmul(misc[:, 128 * q:128 * q + 128], wq1[:, h, :], wk1[:, h, :], start=True, stop=True)
            k = kept["wqk"] = pe.did(ins)
            act.need(k, mh_free[a])
            kept["mh"] = misc_free[0] = act.did(S.mul(mh[a][:, :], misc[:, :], 0.125))
            yield

    def last_batch():
        k = finish_group(NG - 1)
        yield
        yield from project(NB - 1, k)

    NGR = 4
    gat = [[ar2[:, 6656 + 256 * i + 128 * n:6784 + 256 * i + 128 * n] for n in range(2)] for i in range(NGR)]
    a_ga = [Arrivals(nc, f"a_ga{i}") for i in range(NGR)]
    gat_free = [st["pv_done"][NB - 1]] * NGR

    def fetch(b, t):
        i = (4 * b + t) % NGR
        pool.need(gat_free[i], k_zrow, kept["idx"], *(eo_free if b == NB - 1 else kept["rows"]))
        for n in range(2):
            w = a_ga[i].add(G.indirect_dma_start(
                gat[i][n], None, rows_out[int(b == NB - 1)], bass.IndirectOffsetOnAxis(ap=idx[n][:, 4 * b + t:4 * b + t + 1], axis=0)))
            yield w

    def combine(b, t, w):
        i, c = (4 * b + t) % NGR, 4 * b + t
        dve.need(w, kept["w"])
        k = dve.did(V.scalar_tensor_tensor(x[:, c, :], gat[i][0], kw_[0][:, c:c + 1], x[:, c, :], ALU.mult, ALU.add))
        dve.need(k)
        gat_free[i] = st["x_done"][b] = dve.did(V.scalar_tensor_tensor(
            x[:, c, :], gat[i][1], kw_[1][:, c:c + 1], x[:, c, :], ALU.mult, ALU.add))

    def returned(b):
        ws = []
        for t in range(4):
            for w in fetch(b, t):
                yield
            ws.append(w)
        for t in range(4):
            combine(b, t, ws[t])
            yield

    zT = ar2[:, 0:4096].rearrange("p (r n) -> p r n", r=8)
    v1 = [ar1[:, 4096 * i:4096 * i + 4096].rearrange("p (k f) -> p k f", k=4) for i in range(2)]
    yT = [[ar1[:, 8192 + 1024 * i + 512 * a:8704 + 1024 * i + 512 * a] for a in range(2)] for i in range(2)]
    NP = 8
    pr_ = [ar1[:, 10240 + 512 * i:10752 + 512 * i] for i in range(7)] + [ar2[:, 7680:8192]]
    pT = [ar1[:, 13824:16384], ar2[:, 4096:6656]]
    pT4 = [t.rearrange("p (k n) -> p k n", k=4) for t in pT]

    old1 = []

    xT1 = xnT
    xT1_free, v1_free = [st["xnT_free"][0], st["xnT_free"][1]], [None, None]
    xT1_ready, v1_ready = {}, {}
    st["x_done1"] = [None] * NB

    def turn_batch(b, dst, free):
        k = ln_stats(b, st["x_done"][b])
        yield
        k = ln_apply(b, k, xn, xn_free[0])
        yield
        k = transpose_tiles([xn[:, t, :] for t in range(4)], k)
        xn_free[0] = k
        act.need(k, free)
        misc_free[0] = k = act.did(S.copy(dst, misc[:, :]))
        return k

    def prep1(b):
        i = b % 2
        xT1_ready[b] = k = yield from turn_batch(b, xT1[i][:, :], xT1_free[i])
        yield
        for t in range(4):
            for n in range(2):
                o_, f_ = (bank[2], o1_free) if b == 0 and n else (misc, misc_free)
                pe.need(k, f_[0], got["w1"])
                k1 = pe.did(M.matmul(o_[:, :], xT1[i][:, 128 * t:128 * t + 128], wv1[:, 512 * n:512 * n + 512],
                                     start=True, stop=True))
                e_ = act if n else dve
                e_.need(k1, v1_free[i], *old1)
                o = v1[i][:, t, 512 * n:512 * n + 512]
                f_[0] = e_.did(S.copy(o, o_[:, :]) if n else V.tensor_copy(o, o_[:, :]))
                v1_ready.setdefault(b, []).append(f_[0])
                yield

    y_ready, y_free = {}, [None, None]

    def heads(b, r, a):
        i = (8 * b + r) % 2
        pe.need(xT1_ready[b], misc_free[0], kept["mh"])
        k = pe.did(M.matmul(misc[:, :], mh[r // 2][:, 128 * (2 * (r % 2) + a):128 * (2 * (r % 2) + a) + 128], xT1[b % 2][:, :], start=True, stop=True))
        dve.need(k, y_free[i])
        misc_free[0] = y_ready[(b, r, a)] = dve.did(V.tensor_copy(yT[i][a], misc[:, :]))

    e_ready, p_ready, p_free, q_ready, q_free = {}, {}, [None] * NP, {}, [None, None]
    s1_free, tt_free, o1_free = [[None] * 2, [None] * 2], [None] * 2, [None]
    nm_free, rd_free = [None] * 8, [None] * 8

    def scores1(u, b, r, qb, a):
        s, w = u % 2, 128 * (qb + 1)
        i = (8 * b + r) % 2
        pe.need(y_ready[(b, r, a)], s1_free[s][a], *([st["hid_done"]] if u < 2 else []))
        o = pS[s][:, 512 * a:512 * a + w]
        k = pe.did(M.matmul(o, yT[i][a][:, 128 * qb:128 * qb + 128], xT1[b % 2][:, 0:w], start=True, stop=True))
        if qb == 3 and a == 1:
            y_free[i] = k
            if r == 7:
                xT1_free[b % 2] = k
        c = 2 * (u % 4) + a
        pi = (2 * u + a) % NP
        p = pr_[pi][:, 0:w]
        dve.need(k, nm_free[c], p_free[pi], c_mask)
        k = s1_free[s][a] = dve.did(V.tensor_tensor_reduce(p, o, maskf[:, 512 - w:512], -1.0, 3e38, ALU.add, ALU.min,
                                                           accum_out=nm1[:, c:c + 1]))
        act.need(k, rd_free[c])
        nm_free[c] = e_ready[(u, a)] = act.did(S.activation(p, p, ACT.Exp, bias=nm1[:, c:c + 1], scale=-1.0,
                                                            accum_out=den1[:, c:c + 1]))

    def normalise(u, qb):
        w, c = 128 * (qb + 1), 2 * (u % 4)
        dve.need(e_ready.pop((u, 0)), e_ready.pop((u, 1)), *[p_ready.get((u - 4, a)) for a in range(2)])
        k = dve.did(V.reciprocal(rd1[:, c:c + 2], den1[:, c:c + 2]))
        rd_free[c] = rd_free[c + 1] = k
        pool.need(k)
        for a in range(2):
            p = pr_[(2 * u + a) % NP][:, 0:w]
            p_ready[(u, a)] = pool.did(G.tensor_scalar(p, p, rd1[:, c + a:c + a + 1], 1.0, ALU.mult, ALU.mult))

    tbank = [bank[0], bank[1]]

    def turn(u, qb, a):
        pi, i = (2 * u + a) % NP, (u // 4) % 2
        w = 128 * (qb + 1)
        pe.need(p_ready[(u, a)], tt_free[a])
        for t in range(qb + 1):
            at = 128 * (qb - t if a else t)
            ins = M.transpose(tbank[a][:, at:at + 128], pr_[pi][:, 128 * t:128 * t + 128], identf[:, :])
        k = p_free[pi] = pe.did(ins)
        e_ = dve if a else act
        e_.need(k, q_free[i])
        src = tbank[a][:, 0:w].rearrange("p (t n) -> p t n", n=128)
        if a:
            k = dve.did(V.tensor_copy(pT4[i][:, 3 - qb:4, w:w + 128], src))
        else:
            o = pT[i][:, 128 * qb:128 * qb + 512 * (qb + 1)].rearrange("p (t n) -> p t n", n=512)
            k = act.did(S.copy(o[:, :, 0:128], src))
        tt_free[a] = q_ready[(u // 4, a)] = k

    z_free = [None]

    def values(pair, kb):
        b, r, i = pair // 8, pair % 8, pair % 2
        pe.need(q_ready[(pair, 0)], q_ready[(pair, 1)], *v1_ready[b])
        if kb == 0:
            pe.need(o1_free[0])
        for a in range(2):
            h = 2 * r + a
            w = pT4[i][:, 3 - kb, 128 * (kb + 1):640] if a else pT4[i][:, kb, 0:128 * (4 - kb)]
            ins = M.matmul(bank[2][64 * a:64 * a + 64, 128 * kb:512], v1[b % 2][:, kb, 64 * h:64 * h + 64], w,
                           start=(kb == 0), stop=(kb == 3))
        k = pe.did(ins)
        if kb == 3:
            q_free[i] = k
            act.need(k, z_free[0], kept["wqk"])
            o1_free[0] = act.did(S.copy(zT[:, r, :], bank[2][:, :]))
            if r == 7:
                v1_free[b % 2] = k

    def project1(b):
        ready = o1_free[0]
        for t in range(4):
            pe.need(ready, misc_free[0], got["w1"])
            for r in range(8):
                ins = M.matmul(misc[:, 0:128], zT[:, r, 128 * t:128 * t + 128], wo1[:, r, :],
                               start=(r == 0), stop=(r == 7))
            k = z_free[0] = pe.did(ins)
            dve.need(k)
            xt = x[:, 4 * b + t, :]
            misc_free[0] = st["x_done1"][b] = dve.did(V.tensor_tensor(xt, misc[:, 0:128], xt, ALU.add))
            yield

    xT4_done, k_w1 = [None] * NB, [None] * NB

    def route1(b):
        B = slice(4 * b, 4 * b + 4)
        dst = xT4[:, 512 * b:512 * b + 512]
        k = ln_stats(b, st["x_done1"][b], 1)
        yield
        k = ln_apply(b, k, xs[0], xs_free[0], 1)
        yield
        k = xs_free[0] = transpose_tiles([xs[0][:, t, :] for t in range(4)], k)
        act.need(k)
        k = xT4_done[b] = misc_free[0] = act.did(S.copy(dst, misc[:, :]))
        yield
        yield from likely(b, logits(b, k, dst, rt1)[1])
        dve.need(got["w1"])
        k = dve.did(V.tensor_scalar(rd[:, B, :], rp[:, B, :], rb1[:, 0:1], None, ALU.add))
        dve.need(k)
        k = yield from chosen(b, rd, 4)
        yield
        dve.need(k)
        k = dve.did(V.tensor_tensor(rq[:, B, :], rp[:, B, :], rsel[:, B, :], ALU.mult))
        dve.need(k)
        k = dve.did(V.tensor_reduce(r32[0][:, B], rq[:, B, :], AX.X, ALU.add))
        dve.need(k)
        k = dve.did(V.tensor_scalar(r32[1][:, B], r32[0][:, B], 1e-20, None, ALU.add))
        dve.need(k)
        k = dve.did(V.reciprocal(r32[2][:, B], r32[1][:, B]))
        dve.need(k)
        k_w1[b] = dve.did(V.tensor_tensor(rw[:, B, :], rq[:, B, :], over(r32[2], b), ALU.mult))
        yield

    xs_free = [sc_done[NB - 2]]
    def begin():
        yield from returned(0)
        for _ in range(3):
            next(work)
            yield
        for a in range(2):
            heads(0, 0, a)
            yield

    work = prep1(0)
    side = chain(last_batch(), route(NB - 1), table(1), matrices(), capacity())
    fetch_rows(2)
    fetch_weights(2)
    turn_rows(0)
    for p in range(len(PASSES)):
        if p == NCH[0] + 2:
            for _ in side:
                pass
            side = begin()
        hidden(p, 0)
        hidden(p, 1)
        half[0] = 0
        next(side, None)
        if p + 1 < len(PASSES):
            turn_rows(p + 1)
        hidden(p, 2)
        hidden(p, 3)
        half[0] = 1
        if not NCH[0] + 2 <= p < NCH[0] + 9:
            next(side, None)
        if p:
            outward(p - 1)
        if p == NCH[0]:
            kept["rows"] = list(eo_free)
        if p + 3 < len(PASSES):
            fetch_rows(p + 3)
            fetch_weights(p + 3)
    outward(len(PASSES) - 1)
    for _ in side:
        pass
    act.did(S.activation(warm[:, 2:3], warm[:, 0:1], ACT.Exp))
    s1_free[:] = [[pg_free[0], pg_free[1]], [pg_free[2], pg_free[3]]]
    tt_free[:], o1_free[0] = po_free, row_free[0]
    old1 += [hT_free[0], hT_free[1], *eo_free]

    units = [(b, r, qb) for b in range(NB) for r in range(8) for qb in range(4)]
    NU = len(units)
    proj, back, fresh = iter(()), iter(()), -9
    LN_, LT, LV = 1, 3, 7
    for u in range(NU + LV):
        if u < NU:
            b, r, qb = units[u]
            n = u % 4
            if u == 0 or (u % 32 == 28 and b + 2 < NB):
                back = returned(1 if u == 0 else b + 2)
            scores1(u, b, r, qb, 0)
        if 0 <= u - LT < NU:
            turn(u - LT, units[u - LT][2], 0)
        if u < NU:
            if r == 2 and n == 2 and b + 1 < NB:
                work = prep1(b + 1)
            next(back, None)
            if n in (0, 3) or b == r == 0:
                next(work, None)
                if b == r == 0:
                    next(work, None)
            if n in (1, 2):
                if r < 7:
                    heads(b, r + 1, n - 1)
                elif b + 1 < NB:
                    heads(b + 1, 0, n - 1)
            scores1(u, b, r, qb, 1)
        if u == fresh + 1:
            next(proj)
        if 0 <= u - LN_ < NU:
            normalise(u - LN_, units[u - LN_][2])
        if 0 <= u - LT < NU:
            turn(u - LT, units[u - LT][2], 1)
        if 0 <= u - LV < NU:
            values((u - LV) // 4, (u - LV) % 4)
            if (u - LV) % 32 == 31:
                proj = chain(proj, project1(units[u - LV][0]), (None for _ in range(5)), route1(units[u - LV][0]))
                fresh = u
        if u != fresh:
            next(proj, None)
    s1_free = [s1_free[0][1], s1_free[1][1]]
    sr = [ar1[:, 768 * i:768 * i + 768] for i in range(2)]
    aa = [ar1[:, 2048 + 768 * i:2816 + 768 * i] for i in range(2)]
    aaT = [ar1[:, 4096 + 768 * i:4864 + 768 * i].rearrange("p (c n) -> p c n", c=6) for i in range(2)]
    g_free = [s1_free[0], s1_free[1]]
    h_free = [tt_free[0], tt_free[1]]
    sr_free, aa_free, aT4_free = [None, None], [None, None], [None, None]
    aa_ready, aT4_ready = {}, {}
    tr_free = [o1_free[0]]
    ar1_free = v1_free + q_free

    def gate(t):
        i = t % 2
        xt = xT4[:, 128 * t:128 * t + 128]
        pe.need(xT4_done[t // 4], g_free[i], s1_free[i])
        M.matmul(pS[i][:, 0:512], xt, gw1[:, 0:512], start=True, stop=True)
        k1 = pe.did(M.matmul(pS[i][:, 512:1024], xt, uw1[:, 0:512], start=True, stop=True))
        act.need(k1, sr_free[i], *ar1_free)
        k1 = act.did(S.activation(sr[i][:, 0:512], pS[i][:, 0:512], ACT.Silu))
        yield
        pe.need(h_free[i])
        M.matmul(bank[i][:, 0:256], xt, gw1[:, 512:768], start=True, stop=True)
        k2 = pe.did(M.matmul(bank[i][:, 256:512], xt, uw1[:, 512:768], start=True, stop=True))
        act.need(k2)
        k2 = act.did(S.activation(sr[i][:, 512:768], bank[i][:, 0:256], ACT.Silu))
        dve.need(k1, aa_free[i])
        g_free[i] = k1 = dve.did(V.tensor_tensor(aa[i][:, 0:512], pS[i][:, 512:1024], sr[i][:, 0:512], ALU.mult))
        dve.need(k2)
        h_free[i] = sr_free[i] = k2 = dve.did(V.tensor_tensor(aa[i][:, 512:768], bank[i][:, 256:512],
                                                              sr[i][:, 512:768], ALU.mult))
        pool.need(k1, k_w1[t // 4])
        av = aa[i][:, 0:512].rearrange("p (e n) -> p e n", e=E)
        k1 = pool.did(G.tensor_tensor(av, av, rw[:, t, :][:, :, None].broadcast_to([128, E, 64]), ALU.mult))
        aa_ready[t] = (k1, k2)
        yield

    def turn4(t):
        i = t % 2
        k1, k2 = aa_ready.pop(t)
        pe.need(k1, k2, tr_free[0])
        for c in range(4):
            ins = M.transpose(bank[2][:, 128 * c:128 * c + 128], aa[i][:, 128 * c:128 * c + 128], identf[:, :])
        k1 = pe.did(ins)
        pe.need(misc_free[0])
        for c in range(2):
            ins = M.transpose(misc[:, 128 * c:128 * c + 128], aa[i][:, 512 + 128 * c:640 + 128 * c], identf[:, :])
        k2 = aa_free[i] = pe.did(ins)
        act.need(k1, aT4_free[i])
        tr_free[0] = k1 = act.did(S.copy(aaT[i][:, 0:4, :], bank[2][:, :].rearrange("p (c n) -> p c n", c=4)))
        act.need(k2)
        k2 = act.did(S.copy(aaT[i][:, 4:6, :], misc[:, 0:256].rearrange("p (c n) -> p c n", c=2)))
        misc_free[0] = k2
        aT4_ready[t] = (k1, k2)

    def down(t):
        i = t % 2
        pe.need(*aT4_ready.pop(t), misc_free[0])
        for c in range(6):
            ins = M.matmul(misc[:, 256:384], aaT[i][:, c, :], dw1[:, c, :], start=(c == 0), stop=(c == 5))
        k = aT4_free[i] = pe.did(ins)
        dve.need(k)
        misc_free[0] = k = dve.did(V.tensor_tensor(x[:, t, :], misc[:, 256:384], x[:, t, :], ALU.add))
        if t % 4 == 3:
            b = t // 4
            sp.need(k)
            done.append(a_out[b].add(nc.sync.dma_start(oview[:, 4 * b:4 * b + 4, :], x[:, 4 * b:4 * b + 4, :])))

    oview = out.rearrange("(t p) d -> p t d", p=128)
    a_out = [Arrivals(nc, f"a_out{b}") for b in range(NB)]
    done = []
    for t in range(NT + 2):
        tile = gate(t) if t < NT else iter(())
        next(tile, None)
        if 0 <= t - 2 < NT:
            down(t - 2)
        next(tile, None)
        next(proj, None)
        if 0 <= t - 1 < NT:
            turn4(t - 1)
        if t == 26:
            for _ in proj:
                pass
    sp.need(*done)


def layout(inputs):
    f = {k: np.asarray(v) for k, v in inputs.items()}
    c = np.ascontiguousarray
    r = {}
    r["x"] = c(f["L0_attn_x"].reshape(4096, 128))
    r["W0"] = c(np.stack([f["L0_attn_W" + n].T for n in "qkvp"], axis=1))
    r["bqk"] = c(np.stack([f["L0_attn_bq"], f["L0_attn_bk"]], axis=1))
    r["bvp"] = c(np.broadcast_to(np.stack([f["L0_attn_bv"], f["L0_attn_bp"]])[None], (128, 2, 128)))
    r["lam"] = c(np.stack([f["L0_attn_lambda_" + n][:, 0, :] for n in ("q1", "k1", "q2", "k2")], axis=1))
    r["rt0"] = c(f["L0_ffn_router_weight"].T)
    r["wx"] = c(np.stack([f["L0_ffn_ff_pre_act_weight"].transpose(0, 2, 1), f["L0_ffn_gate_weight"].transpose(0, 2, 1),
                          f["L0_ffn_ff_post_act_weight"].reshape(8, 128, 4, 128).transpose(0, 3, 2, 1)
                          .reshape(8, 128, 512)], axis=2))
    r["wq1"] = c(f["L1_attn_W_Q"].transpose(1, 0, 2))
    r["wk1"] = c(f["L1_attn_W_K"].transpose(1, 0, 2))
    r["wv1"] = c(f["L1_attn_W_V"].reshape(1024, 128).T)
    r["wo1"] = c(f["L1_attn_W_O"].T.reshape(8, 128, 128).transpose(1, 0, 2))
    for n, m in (("gw1", "gate_w"), ("uw1", "up_w")):
        r[n] = c(np.concatenate([f["L1_ffn_" + m].transpose(1, 0, 2).reshape(128, 512), f["L1_ffn_s_" + m]], axis=1))
    r["dw1"] = c(np.concatenate([f["L1_ffn_down_w"].reshape(512, 128), f["L1_ffn_s_down_w"]])
                 .reshape(6, 128, 128).transpose(1, 0, 2))
    r["stack"] = np.concatenate([np.zeros((24, 4096), np.float32),
                                 np.full((3, 8192), 0x3F80, np.uint16).view(np.float32)])
    r["rt1"] = c(f["L1_ffn_router_w"])
    r["rb1"] = c(np.broadcast_to(f["L1_ffn_router_bias"], (128, 1)))
    p = np.arange(128, dtype=np.float32)[:, None]

    def row(v):
        return np.broadcast_to(np.asarray(v, np.float32)[None], (128, len(v)))

    r["cst"] = c(np.concatenate(
        [row(np.arange(35)), 128 * row(np.arange(70)) + p, p, row(np.tile([0] + [1] * 7, 4))]
        + [row(CH[h] * np.arange(16)) for h in range(2)] + [row(LIST[h] * np.arange(E)) for h in range(2)]
        + [row(np.zeros(7))], axis=1))
    return r


def kernel(**inputs):
    from concourse import bacc
    from concourse.bass_utils import run_bass_kernel_spmd

    arrays = layout(inputs)
    nc = bacc.Bacc("TRN2", target_bir_lowering=False, num_devices=1)
    T = {n: nc.dram_tensor("in_" + n, a.shape, mybir.dt.from_np(a.dtype), kind="ExternalInput").ap()
         for n, a in arrays.items()}
    out = nc.dram_tensor("out", (4096, 128), F32, kind="ExternalOutput").ap()
    program(nc, T, out)
    r = run_bass_kernel_spmd(nc, [{"in_" + n: a for n, a in arrays.items()}], core_ids=[0])
    return r.results[0]["out"].reshape(8, 512, 128)
```
